# Optimizing a Trainium2 kernel written in Bass

```python
import numpy as np
import jax
import jax.numpy as jnp

def _softmax(x, axis=-1):
    return jax.nn.softmax(x, axis=axis)

def _gelu(x):
    return jax.nn.gelu(x, approximate=True)

def _silu(x):
    return jax.nn.silu(x)

def _sigmoid(x):
    return jax.nn.sigmoid(x)

def _layernorm(x, axis=-1, eps=1e-05):
    m = jnp.mean(x, axis=axis, keepdims=True)
    v = jnp.var(x, axis=axis, keepdims=True)
    return (x - m) / jnp.sqrt(v + eps)

def _scatter_add(tgt, idx, src, axis=0):
    return tgt.at[idx].add(src)

def _segment_sum(src, seg, n):
    return jax.ops.segment_sum(src, seg, n)
kernel_name = 'mk_xattn_seq_d4_seqx_r8_864a49'

def setup_inputs(seed: int=0):
    np.random.seed(seed)
    _w = jnp.asarray

    def _rec_inputs():
        import jax
        import jax.numpy as jnp
        _rk = jax.random.key(seed)
        x = -0.000125 + 0.9999 * jax.random.normal(jax.random.fold_in(_rk, 1), (64, 64, 256), jnp.float32)
        _lenS = 64 - jax.random.randint(jax.random.fold_in(_rk, 7), (64,), 0, max(1, 64 // 4) + 1, jnp.int32)
        _lenS2 = 64 - jax.random.randint(jax.random.fold_in(_rk, 8), (64,), 0, max(1, 64 // 4) + 1, jnp.int32)
        _ctx_1024P = jax.random.normal(jax.random.fold_in(_rk, 11), (64, 16, 128), jnp.float32)
        _ctx_1024c = jax.random.dirichlet(jax.random.fold_in(_rk, 511), 0.3 * jnp.ones((16,), jnp.float32), (64, 64))
        _ctx_1024t = jnp.einsum('bsk,bkd->bsd', _ctx_1024c, _ctx_1024P)
        _ctx_1024t = _ctx_1024t * jax.lax.rsqrt(jnp.mean(jnp.square(_ctx_1024t)) + 1e-12) * 0.953939
        ctx_1024 = 4.13588e-05 + 0.999923 * (_ctx_1024t + 0.3 * jax.random.normal(jax.random.fold_in(_rk, 611), (64, 64, 128), jnp.float32))
        pos_1xS = jnp.broadcast_to(jnp.arange(64, dtype=jnp.int32), (1, 64))
        _validS = jnp.arange(64)[None, :] < _lenS[:, None]
        _validS2 = jnp.arange(64)[None, :] < _lenS2[:, None]
        _causal = jnp.tril(jnp.ones((64, 64), dtype=bool))
        mask_BxS_ik0 = jnp.where(jnp.broadcast_to(_validS[:, :], (64, 64)), 0, 1).astype(jnp.int32)
        mask_BxS2_bk0 = jnp.logical_not(jnp.broadcast_to(_validS2[:, :], (64, 64)))
        return (x, ctx_1024, pos_1xS, mask_BxS_ik0, mask_BxS2_bk0)
    x, ctx_1024, pos_1xS, mask_BxS_ik0, mask_BxS2_bk0 = _rec_inputs()

    def _L0_xattn_setup():
        import jax, jax.numpy as jnp
        import numpy as np
        EPS = 1e-06

        def _rmsnorm(x, w):
            var = jnp.mean(jnp.square(x), axis=-1, keepdims=True)
            return x * jax.lax.rsqrt(var + EPS) * w
        key = jax.random.key(seed)
        ks = jax.random.split(key, 6)
        B, N, M = (4, 512, 256)
        d_model, memory_dim = (256, 128)
        hidden_states = jax.random.normal(ks[0], (B, N, d_model), dtype=jnp.float32)
        memory = jax.random.normal(ks[1], (B, M, memory_dim), dtype=jnp.float32)
        W_mem = jax.random.normal(ks[2], (d_model, memory_dim), dtype=jnp.float32) / np.sqrt(memory_dim)
        W_gate = jax.random.normal(ks[3], (d_model, 2 * d_model), dtype=jnp.float32) / np.sqrt(2 * d_model)
        b_gate = jax.random.normal(ks[4], (d_model,), dtype=jnp.float32) * 0.01
        norm_w = jnp.ones((d_model,), dtype=jnp.float32)
        return {'hidden_states': hidden_states, 'memory': memory, 'W_mem': W_mem, 'W_gate': W_gate, 'b_gate': b_gate, 'norm_w': norm_w}
    _L0_xattn_all = _L0_xattn_setup()
    _L0_xattn_in = {k: v for k, v in _L0_xattn_all.items() if k in ('W_mem', 'W_gate', 'b_gate', 'norm_w')}
    del _L0_xattn_all

    def _L1_xattn_setup():
        import jax, jax.numpy as jnp
        import numpy as np
        H = 256
        NH = 16
        HD = H // NH
        CH = 128
        CC = 128
        CHD = CC // NH
        I = 688
        B = 2
        L = 256
        LE = 128
        EPS = 1e-06

        def rms_norm(x, w):
            xf = x.astype(jnp.float32)
            var = jnp.mean(xf * xf, axis=-1, keepdims=True)
            return (w * (xf * jax.lax.rsqrt(var + EPS))).astype(x.dtype)

        def expert_mask(tt):
            vm = jnp.zeros(tt.shape, dtype=bool)
            vm = vm.at[:, :-1].set((tt[:, :-1] == 1) & (tt[:, 1:] == 1))
            return vm

        def rotate_half(x):
            d = x.shape[-1] // 2
            return jnp.concatenate([-x[..., d:], x[..., :d]], axis=-1)

        def apply_rotary(q, k, position_ids, seq_len):
            inv = 1.0 / 10000.0 ** (jnp.arange(0, HD, 2, dtype=jnp.float32) / HD)
            t = jnp.arange(seq_len, dtype=jnp.float32)
            freqs = jnp.outer(t, inv)
            emb = jnp.concatenate([freqs, freqs], axis=-1)
            cos = jnp.cos(emb)[position_ids][:, None].astype(q.dtype)
            sin = jnp.sin(emb)[position_ids][:, None].astype(q.dtype)
            return (q * cos + rotate_half(q) * sin, k * cos + rotate_half(k) * sin)

        def sdpa(q, k, v, causal):
            scale = 1.0 / np.sqrt(q.shape[-1])
            scores = jnp.einsum('bhqd,bhkd->bhqk', q * scale, k)
            if causal:
                mask = jnp.tril(jnp.ones((q.shape[-2], k.shape[-2]), dtype=bool))
                scores = jnp.where(mask, scores, jnp.finfo(jnp.float32).min)
            p = jax.nn.softmax(scores.astype(jnp.float32), axis=-1).astype(q.dtype)
            return jnp.einsum('bhqk,bhkd->bhqd', p, v)

        def heads(x, nh, hd):
            b, l, _ = x.shape
            return x.reshape(b, l, nh, hd).transpose(0, 2, 1, 3)
        key = jax.random.key(seed)
        ks = jax.random.split(key, 20)
        s = 0.02
        f32 = jnp.float32
        return {'hidden_states': jax.random.normal(ks[0], (B, L, H), f32), 'encoder_outputs': jax.random.normal(ks[1], (B, LE, CH), f32), 'token_type_ids': jax.random.randint(ks[2], (B, L), 0, 2, jnp.int32), 'position_ids': jnp.arange(L, dtype=jnp.int32)[None, :], 'ln_in_w': jnp.ones((H,), f32), 'ln_post_attn_w': jnp.ones((H,), f32), 'ln_post_cross_w': jnp.ones((H,), f32), 'v_qkv': jax.random.normal(ks[3], (H, 3 * H), f32) * s, 'l_qkv': jax.random.normal(ks[4], (H, 3 * H), f32) * s, 'v_dense': jax.random.normal(ks[5], (H, H), f32) * s, 'l_dense': jax.random.normal(ks[6], (H, H), f32) * s, 'cq_w': jax.random.normal(ks[7], (H, CC), f32) * s, 'ckv_w': jax.random.normal(ks[8], (CH, 2 * CC), f32) * s, 'cdense_w': jax.random.normal(ks[9], (CC, H), f32) * s, 'v_gate': jax.random.normal(ks[10], (H, I), f32) * s, 'v_up': jax.random.normal(ks[11], (H, I), f32) * s, 'v_down': jax.random.normal(ks[12], (I, H), f32) * s, 'l_gate': jax.random.normal(ks[13], (H, I), f32) * s, 'l_up': jax.random.normal(ks[14], (H, I), f32) * s, 'l_down': jax.random.normal(ks[15], (I, H), f32) * s}
    _L1_xattn_all = _L1_xattn_setup()
    _L1_xattn_in = {k: v for k, v in _L1_xattn_all.items() if k in ('ln_in_w', 'ln_post_attn_w', 'ln_post_cross_w', 'v_qkv', 'l_qkv', 'v_dense', 'l_dense', 'cq_w', 'ckv_w', 'cdense_w', 'v_gate', 'v_up', 'v_down', 'l_gate', 'l_up', 'l_down')}
    del _L1_xattn_all

    def _L2_xattn_setup():
        import jax, jax.numpy as jnp
        import numpy as np
        DIM = 256
        DIM_MEDIA = 128
        HEADS = 16
        DIM_HEAD = 64
        INNER = HEADS * DIM_HEAD
        FF_INNER = 4 * DIM
        B, N_TOK, N_LAT = (4, 256, 64)
        EPS = 1e-05

        def layernorm(x, g, b):
            mu = jnp.mean(x, axis=-1, keepdims=True)
            var = jnp.var(x, axis=-1, keepdims=True)
            return (x - mu) * jax.lax.rsqrt(var + EPS) * g + b
        key = jax.random.key(seed)
        ks = jax.random.split(key, 12)
        x = jax.random.normal(ks[0], (B, N_TOK, DIM), dtype=jnp.float32)
        media = jax.random.normal(ks[1], (B, N_LAT, DIM_MEDIA), dtype=jnp.float32)
        media_mask = jax.random.randint(ks[2], (B, N_LAT), 0, 2).astype(bool)
        media_mask = media_mask.at[:, 0].set(True)
        s = lambda d: 1.0 / np.sqrt(d)
        Wq = jax.random.normal(ks[3], (DIM, INNER), dtype=jnp.float32) * s(DIM)
        Wkv = jax.random.normal(ks[4], (DIM_MEDIA, 2 * INNER), dtype=jnp.float32) * s(DIM_MEDIA)
        Wo = jax.random.normal(ks[5], (INNER, DIM), dtype=jnp.float32) * s(INNER)
        W1 = jax.random.normal(ks[6], (DIM, FF_INNER), dtype=jnp.float32) * s(DIM)
        W2 = jax.random.normal(ks[7], (FF_INNER, DIM), dtype=jnp.float32) * s(FF_INNER)
        return {'x': x, 'media': media, 'media_mask': media_mask, 'ln_q_g': jnp.ones((DIM,), jnp.float32), 'ln_q_b': jnp.zeros((DIM,), jnp.float32), 'Wq': Wq, 'Wkv': Wkv, 'Wo': Wo, 'attn_gate': jax.random.normal(ks[8], (1,), jnp.float32) * 0.5, 'ln_ff_g': jnp.ones((DIM,), jnp.float32), 'ln_ff_b': jnp.zeros((DIM,), jnp.float32), 'W1': W1, 'W2': W2, 'ff_gate': jax.random.normal(ks[9], (1,), jnp.float32) * 0.5}
    _L2_xattn_all = _L2_xattn_setup()
    _L2_xattn_in = {k: v for k, v in _L2_xattn_all.items() if k in ('ln_q_g', 'ln_q_b', 'Wq', 'Wkv', 'Wo', 'attn_gate', 'ln_ff_g', 'ln_ff_b', 'W1', 'W2', 'ff_gate')}
    del _L2_xattn_all

    def _L3_xattn_setup():
        import jax, jax.numpy as jnp
        import numpy as np
        H = 256
        NH = 16
        HD = H // NH
        CH = 128
        CC = 128
        CHD = CC // NH
        I = 688
        B = 2
        L = 256
        LE = 128
        EPS = 1e-06

        def rms_norm(x, w):
            xf = x.astype(jnp.float32)
            var = jnp.mean(xf * xf, axis=-1, keepdims=True)
            return (w * (xf * jax.lax.rsqrt(var + EPS))).astype(x.dtype)

        def expert_mask(tt):
            vm = jnp.zeros(tt.shape, dtype=bool)
            vm = vm.at[:, :-1].set((tt[:, :-1] == 1) & (tt[:, 1:] == 1))
            return vm

        def rotate_half(x):
            d = x.shape[-1] // 2
            return jnp.concatenate([-x[..., d:], x[..., :d]], axis=-1)

        def apply_rotary(q, k, position_ids, seq_len):
            inv = 1.0 / 10000.0 ** (jnp.arange(0, HD, 2, dtype=jnp.float32) / HD)
            t = jnp.arange(seq_len, dtype=jnp.float32)
            freqs = jnp.outer(t, inv)
            emb = jnp.concatenate([freqs, freqs], axis=-1)
            cos = jnp.cos(emb)[position_ids][:, None].astype(q.dtype)
            sin = jnp.sin(emb)[position_ids][:, None].astype(q.dtype)
            return (q * cos + rotate_half(q) * sin, k * cos + rotate_half(k) * sin)

        def sdpa(q, k, v, causal):
            scale = 1.0 / np.sqrt(q.shape[-1])
            scores = jnp.einsum('bhqd,bhkd->bhqk', q * scale, k)
            if causal:
                mask = jnp.tril(jnp.ones((q.shape[-2], k.shape[-2]), dtype=bool))
                scores = jnp.where(mask, scores, jnp.finfo(jnp.float32).min)
            p = jax.nn.softmax(scores.astype(jnp.float32), axis=-1).astype(q.dtype)
            return jnp.einsum('bhqk,bhkd->bhqd', p, v)

        def heads(x, nh, hd):
            b, l, _ = x.shape
            return x.reshape(b, l, nh, hd).transpose(0, 2, 1, 3)
        key = jax.random.key(seed)
        ks = jax.random.split(key, 20)
        s = 0.02
        f32 = jnp.float32
        return {'hidden_states': jax.random.normal(ks[0], (B, L, H), f32), 'encoder_outputs': jax.random.normal(ks[1], (B, LE, CH), f32), 'token_type_ids': jax.random.randint(ks[2], (B, L), 0, 2, jnp.int32), 'position_ids': jnp.arange(L, dtype=jnp.int32)[None, :], 'ln_in_w': jnp.ones((H,), f32), 'ln_post_attn_w': jnp.ones((H,), f32), 'ln_post_cross_w': jnp.ones((H,), f32), 'v_qkv': jax.random.normal(ks[3], (H, 3 * H), f32) * s, 'l_qkv': jax.random.normal(ks[4], (H, 3 * H), f32) * s, 'v_dense': jax.random.normal(ks[5], (H, H), f32) * s, 'l_dense': jax.random.normal(ks[6], (H, H), f32) * s, 'cq_w': jax.random.normal(ks[7], (H, CC), f32) * s, 'ckv_w': jax.random.normal(ks[8], (CH, 2 * CC), f32) * s, 'cdense_w': jax.random.normal(ks[9], (CC, H), f32) * s, 'v_gate': jax.random.normal(ks[10], (H, I), f32) * s, 'v_up': jax.random.normal(ks[11], (H, I), f32) * s, 'v_down': jax.random.normal(ks[12], (I, H), f32) * s, 'l_gate': jax.random.normal(ks[13], (H, I), f32) * s, 'l_up': jax.random.normal(ks[14], (H, I), f32) * s, 'l_down': jax.random.normal(ks[15], (I, H), f32) * s}
    _L3_xattn_all = _L3_xattn_setup()
    _L3_xattn_in = {k: v for k, v in _L3_xattn_all.items() if k in ('ln_in_w', 'ln_post_attn_w', 'ln_post_cross_w', 'v_qkv', 'l_qkv', 'v_dense', 'l_dense', 'cq_w', 'ckv_w', 'cdense_w', 'v_gate', 'v_up', 'v_down', 'l_gate', 'l_up', 'l_down')}
    del _L3_xattn_all
    return {'x': x, 'ctx_1024': ctx_1024, 'pos_1xS': pos_1xS, 'mask_BxS_ik0': mask_BxS_ik0, 'mask_BxS2_bk0': mask_BxS2_bk0, 'L0_xattn_W_mem': _L0_xattn_in['W_mem'], 'L0_xattn_W_gate': _L0_xattn_in['W_gate'], 'L0_xattn_b_gate': _L0_xattn_in['b_gate'], 'L0_xattn_norm_w': _L0_xattn_in['norm_w'], 'L1_xattn_ln_in_w': _L1_xattn_in['ln_in_w'], 'L1_xattn_ln_post_attn_w': _L1_xattn_in['ln_post_attn_w'], 'L1_xattn_ln_post_cross_w': _L1_xattn_in['ln_post_cross_w'], 'L1_xattn_v_qkv': _L1_xattn_in['v_qkv'], 'L1_xattn_l_qkv': _L1_xattn_in['l_qkv'], 'L1_xattn_v_dense': _L1_xattn_in['v_dense'], 'L1_xattn_l_dense': _L1_xattn_in['l_dense'], 'L1_xattn_cq_w': _L1_xattn_in['cq_w'], 'L1_xattn_ckv_w': _L1_xattn_in['ckv_w'], 'L1_xattn_cdense_w': _L1_xattn_in['cdense_w'], 'L1_xattn_v_gate': _L1_xattn_in['v_gate'], 'L1_xattn_v_up': _L1_xattn_in['v_up'], 'L1_xattn_v_down': _L1_xattn_in['v_down'], 'L1_xattn_l_gate': _L1_xattn_in['l_gate'], 'L1_xattn_l_up': _L1_xattn_in['l_up'], 'L1_xattn_l_down': _L1_xattn_in['l_down'], 'L2_xattn_ln_q_g': _L2_xattn_in['ln_q_g'], 'L2_xattn_ln_q_b': _L2_xattn_in['ln_q_b'], 'L2_xattn_Wq': _L2_xattn_in['Wq'], 'L2_xattn_Wkv': _L2_xattn_in['Wkv'], 'L2_xattn_Wo': _L2_xattn_in['Wo'], 'L2_xattn_attn_gate': _L2_xattn_in['attn_gate'], 'L2_xattn_ln_ff_g': _L2_xattn_in['ln_ff_g'], 'L2_xattn_ln_ff_b': _L2_xattn_in['ln_ff_b'], 'L2_xattn_W1': _L2_xattn_in['W1'], 'L2_xattn_W2': _L2_xattn_in['W2'], 'L2_xattn_ff_gate': _L2_xattn_in['ff_gate'], 'L3_xattn_ln_in_w': _L3_xattn_in['ln_in_w'], 'L3_xattn_ln_post_attn_w': _L3_xattn_in['ln_post_attn_w'], 'L3_xattn_ln_post_cross_w': _L3_xattn_in['ln_post_cross_w'], 'L3_xattn_v_qkv': _L3_xattn_in['v_qkv'], 'L3_xattn_l_qkv': _L3_xattn_in['l_qkv'], 'L3_xattn_v_dense': _L3_xattn_in['v_dense'], 'L3_xattn_l_dense': _L3_xattn_in['l_dense'], 'L3_xattn_cq_w': _L3_xattn_in['cq_w'], 'L3_xattn_ckv_w': _L3_xattn_in['ckv_w'], 'L3_xattn_cdense_w': _L3_xattn_in['cdense_w'], 'L3_xattn_v_gate': _L3_xattn_in['v_gate'], 'L3_xattn_v_up': _L3_xattn_in['v_up'], 'L3_xattn_v_down': _L3_xattn_in['v_down'], 'L3_xattn_l_gate': _L3_xattn_in['l_gate'], 'L3_xattn_l_up': _L3_xattn_in['l_up'], 'L3_xattn_l_down': _L3_xattn_in['l_down']}

def reference(x, ctx_1024, pos_1xS, mask_BxS_ik0, mask_BxS2_bk0, L0_xattn_W_mem, L0_xattn_W_gate, L0_xattn_b_gate, L0_xattn_norm_w, L1_xattn_ln_in_w, L1_xattn_ln_post_attn_w, L1_xattn_ln_post_cross_w, L1_xattn_v_qkv, L1_xattn_l_qkv, L1_xattn_v_dense, L1_xattn_l_dense, L1_xattn_cq_w, L1_xattn_ckv_w, L1_xattn_cdense_w, L1_xattn_v_gate, L1_xattn_v_up, L1_xattn_v_down, L1_xattn_l_gate, L1_xattn_l_up, L1_xattn_l_down, L2_xattn_ln_q_g, L2_xattn_ln_q_b, L2_xattn_Wq, L2_xattn_Wkv, L2_xattn_Wo, L2_xattn_attn_gate, L2_xattn_ln_ff_g, L2_xattn_ln_ff_b, L2_xattn_W1, L2_xattn_W2, L2_xattn_ff_gate, L3_xattn_ln_in_w, L3_xattn_ln_post_attn_w, L3_xattn_ln_post_cross_w, L3_xattn_v_qkv, L3_xattn_l_qkv, L3_xattn_v_dense, L3_xattn_l_dense, L3_xattn_cq_w, L3_xattn_ckv_w, L3_xattn_cdense_w, L3_xattn_v_gate, L3_xattn_v_up, L3_xattn_v_down, L3_xattn_l_gate, L3_xattn_l_up, L3_xattn_l_down):
    import jax
    import jax.numpy as jnp

    def _L0_xattn_ref(hidden_states, memory, W_mem, W_gate, b_gate, norm_w):
        import jax, jax.numpy as jnp
        import numpy as np
        EPS = 1e-06

        def _rmsnorm(x, w):
            var = jnp.mean(jnp.square(x), axis=-1, keepdims=True)
            return x * jax.lax.rsqrt(var + EPS) * w
        D = hidden_states.shape[-1]
        memory_proj = jnp.einsum('bme,de->bmd', memory, W_mem)
        scores = jnp.einsum('bnd,bmd->bnm', hidden_states, memory_proj) / jnp.sqrt(jnp.float32(D))
        attn = jax.nn.softmax(scores, axis=-1)
        memory_context = jnp.einsum('bnm,bmd->bnd', attn, memory_proj)
        gate_input = jnp.concatenate([hidden_states, memory_context], axis=-1)
        gate = jax.nn.sigmoid(jnp.einsum('bnf,df->bnd', gate_input, W_gate) + b_gate)
        fused = hidden_states + gate * memory_context
        return _rmsnorm(fused, norm_w)

    def _L1_xattn_ref(hidden_states, encoder_outputs, token_type_ids, position_ids, ln_in_w, ln_post_attn_w, ln_post_cross_w, v_qkv, l_qkv, v_dense, l_dense, cq_w, ckv_w, cdense_w, v_gate, v_up, v_down, l_gate, l_up, l_down):
        import jax, jax.numpy as jnp
        import numpy as np
        H = 256
        NH = 16
        HD = H // NH
        CH = 128
        CC = 128
        CHD = CC // NH
        I = 688
        B = 2
        L = 256
        LE = 128
        EPS = 1e-06

        def rms_norm(x, w):
            xf = x.astype(jnp.float32)
            var = jnp.mean(xf * xf, axis=-1, keepdims=True)
            return (w * (xf * jax.lax.rsqrt(var + EPS))).astype(x.dtype)

        def expert_mask(tt):
            vm = jnp.zeros(tt.shape, dtype=bool)
            vm = vm.at[:, :-1].set((tt[:, :-1] == 1) & (tt[:, 1:] == 1))
            return vm

        def rotate_half(x):
            d = x.shape[-1] // 2
            return jnp.concatenate([-x[..., d:], x[..., :d]], axis=-1)

        def apply_rotary(q, k, position_ids, seq_len):
            inv = 1.0 / 10000.0 ** (jnp.arange(0, HD, 2, dtype=jnp.float32) / HD)
            t = jnp.arange(seq_len, dtype=jnp.float32)
            freqs = jnp.outer(t, inv)
            emb = jnp.concatenate([freqs, freqs], axis=-1)
            cos = jnp.cos(emb)[position_ids][:, None].astype(q.dtype)
            sin = jnp.sin(emb)[position_ids][:, None].astype(q.dtype)
            return (q * cos + rotate_half(q) * sin, k * cos + rotate_half(k) * sin)

        def sdpa(q, k, v, causal):
            scale = 1.0 / np.sqrt(q.shape[-1])
            scores = jnp.einsum('bhqd,bhkd->bhqk', q * scale, k)
            if causal:
                mask = jnp.tril(jnp.ones((q.shape[-2], k.shape[-2]), dtype=bool))
                scores = jnp.where(mask, scores, jnp.finfo(jnp.float32).min)
            p = jax.nn.softmax(scores.astype(jnp.float32), axis=-1).astype(q.dtype)
            return jnp.einsum('bhqk,bhkd->bhqd', p, v)

        def heads(x, nh, hd):
            b, l, _ = x.shape
            return x.reshape(b, l, nh, hd).transpose(0, 2, 1, 3)
        b, l, _ = hidden_states.shape
        vm = expert_mask(token_type_ids)[..., None]
        residual = hidden_states
        x = rms_norm(hidden_states, ln_in_w)
        mixed = jnp.where(vm, x @ v_qkv, x @ l_qkv)
        q, k, v = jnp.split(mixed, 3, axis=-1)
        q, k, v = (heads(q, NH, HD), heads(k, NH, HD), heads(v, NH, HD))
        q, k = apply_rotary(q, k, position_ids, l)
        ctx = sdpa(q, k, v, causal=True)
        ctx = ctx.transpose(0, 2, 1, 3).reshape(b, l, H)
        attn_out = jnp.where(vm, ctx @ v_dense, ctx @ l_dense)
        hidden_states = residual + attn_out
        ci = rms_norm(hidden_states, ln_post_cross_w)
        cq = heads(ci @ cq_w, NH, CHD)
        ckv = encoder_outputs @ ckv_w
        ck, cv = jnp.split(ckv, 2, axis=-1)
        ck, cv = (heads(ck, NH, CHD), heads(cv, NH, CHD))
        cctx = sdpa(cq, ck, cv, causal=False)
        cctx = cctx.transpose(0, 2, 1, 3).reshape(b, l, CC)
        hidden_states = hidden_states + cctx @ cdense_w
        mi = rms_norm(hidden_states, ln_post_attn_w)
        v_out = jax.nn.silu(mi @ v_gate) * (mi @ v_up) @ v_down
        l_out = jax.nn.silu(mi @ l_gate) * (mi @ l_up) @ l_down
        hidden_states = hidden_states + jnp.where(vm, v_out, l_out)
        return hidden_states

    def _L2_xattn_ref(x, media, media_mask, ln_q_g, ln_q_b, Wq, Wkv, Wo, attn_gate, ln_ff_g, ln_ff_b, W1, W2, ff_gate):
        import jax, jax.numpy as jnp
        import numpy as np
        DIM = 256
        DIM_MEDIA = 128
        HEADS = 16
        DIM_HEAD = 64
        INNER = HEADS * DIM_HEAD
        FF_INNER = 4 * DIM
        B, N_TOK, N_LAT = (4, 256, 64)
        EPS = 1e-05

        def layernorm(x, g, b):
            mu = jnp.mean(x, axis=-1, keepdims=True)
            var = jnp.var(x, axis=-1, keepdims=True)
            return (x - mu) * jax.lax.rsqrt(var + EPS) * g + b
        scale = DIM_HEAD ** (-0.5)
        qn = layernorm(x, ln_q_g, ln_q_b)
        q = qn @ Wq * scale
        kv = media @ Wkv
        k, v = jnp.split(kv, 2, axis=-1)
        split_heads = lambda t: t.reshape(t.shape[0], t.shape[1], HEADS, DIM_HEAD).transpose(0, 2, 1, 3)
        q, k, v = (split_heads(q), split_heads(k), split_heads(v))
        sim = jnp.einsum('bhid,bhjd->bhij', q, k)
        neg_inf = jnp.finfo(sim.dtype).min
        sim = jnp.where(media_mask[:, None, None, :], sim, neg_inf)
        attn = jax.nn.softmax(sim, axis=-1)
        out = jnp.einsum('bhij,bhjd->bhid', attn, v)
        out = out.transpose(0, 2, 1, 3).reshape(x.shape[0], x.shape[1], INNER)
        attn_out = out @ Wo
        x = x + jnp.tanh(attn_gate) * attn_out
        h = layernorm(x, ln_ff_g, ln_ff_b)
        h = jax.nn.gelu(h @ W1, approximate=False) @ W2
        x = x + jnp.tanh(ff_gate) * h
        return x

    def _L3_xattn_ref(hidden_states, encoder_outputs, token_type_ids, position_ids, ln_in_w, ln_post_attn_w, ln_post_cross_w, v_qkv, l_qkv, v_dense, l_dense, cq_w, ckv_w, cdense_w, v_gate, v_up, v_down, l_gate, l_up, l_down):
        import jax, jax.numpy as jnp
        import numpy as np
        H = 256
        NH = 16
        HD = H // NH
        CH = 128
        CC = 128
        CHD = CC // NH
        I = 688
        B = 2
        L = 256
        LE = 128
        EPS = 1e-06

        def rms_norm(x, w):
            xf = x.astype(jnp.float32)
            var = jnp.mean(xf * xf, axis=-1, keepdims=True)
            return (w * (xf * jax.lax.rsqrt(var + EPS))).astype(x.dtype)

        def expert_mask(tt):
            vm = jnp.zeros(tt.shape, dtype=bool)
            vm = vm.at[:, :-1].set((tt[:, :-1] == 1) & (tt[:, 1:] == 1))
            return vm

        def rotate_half(x):
            d = x.shape[-1] // 2
            return jnp.concatenate([-x[..., d:], x[..., :d]], axis=-1)

        def apply_rotary(q, k, position_ids, seq_len):
            inv = 1.0 / 10000.0 ** (jnp.arange(0, HD, 2, dtype=jnp.float32) / HD)
            t = jnp.arange(seq_len, dtype=jnp.float32)
            freqs = jnp.outer(t, inv)
            emb = jnp.concatenate([freqs, freqs], axis=-1)
            cos = jnp.cos(emb)[position_ids][:, None].astype(q.dtype)
            sin = jnp.sin(emb)[position_ids][:, None].astype(q.dtype)
            return (q * cos + rotate_half(q) * sin, k * cos + rotate_half(k) * sin)

        def sdpa(q, k, v, causal):
            scale = 1.0 / np.sqrt(q.shape[-1])
            scores = jnp.einsum('bhqd,bhkd->bhqk', q * scale, k)
            if causal:
                mask = jnp.tril(jnp.ones((q.shape[-2], k.shape[-2]), dtype=bool))
                scores = jnp.where(mask, scores, jnp.finfo(jnp.float32).min)
            p = jax.nn.softmax(scores.astype(jnp.float32), axis=-1).astype(q.dtype)
            return jnp.einsum('bhqk,bhkd->bhqd', p, v)

        def heads(x, nh, hd):
            b, l, _ = x.shape
            return x.reshape(b, l, nh, hd).transpose(0, 2, 1, 3)
        b, l, _ = hidden_states.shape
        vm = expert_mask(token_type_ids)[..., None]
        residual = hidden_states
        x = rms_norm(hidden_states, ln_in_w)
        mixed = jnp.where(vm, x @ v_qkv, x @ l_qkv)
        q, k, v = jnp.split(mixed, 3, axis=-1)
        q, k, v = (heads(q, NH, HD), heads(k, NH, HD), heads(v, NH, HD))
        q, k = apply_rotary(q, k, position_ids, l)
        ctx = sdpa(q, k, v, causal=True)
        ctx = ctx.transpose(0, 2, 1, 3).reshape(b, l, H)
        attn_out = jnp.where(vm, ctx @ v_dense, ctx @ l_dense)
        hidden_states = residual + attn_out
        ci = rms_norm(hidden_states, ln_post_cross_w)
        cq = heads(ci @ cq_w, NH, CHD)
        ckv = encoder_outputs @ ckv_w
        ck, cv = jnp.split(ckv, 2, axis=-1)
        ck, cv = (heads(ck, NH, CHD), heads(cv, NH, CHD))
        cctx = sdpa(cq, ck, cv, causal=False)
        cctx = cctx.transpose(0, 2, 1, 3).reshape(b, l, CC)
        hidden_states = hidden_states + cctx @ cdense_w
        mi = rms_norm(hidden_states, ln_post_attn_w)
        v_out = jax.nn.silu(mi @ v_gate) * (mi @ v_up) @ v_down
        l_out = jax.nn.silu(mi @ l_gate) * (mi @ l_up) @ l_down
        hidden_states = hidden_states + jnp.where(vm, v_out, l_out)
        return hidden_states
    x = _L0_xattn_ref(x, ctx_1024, L0_xattn_W_mem, L0_xattn_W_gate, L0_xattn_b_gate, L0_xattn_norm_w)
    x = _L1_xattn_ref(x, ctx_1024, mask_BxS_ik0, pos_1xS, L1_xattn_ln_in_w, L1_xattn_ln_post_attn_w, L1_xattn_ln_post_cross_w, L1_xattn_v_qkv, L1_xattn_l_qkv, L1_xattn_v_dense, L1_xattn_l_dense, L1_xattn_cq_w, L1_xattn_ckv_w, L1_xattn_cdense_w, L1_xattn_v_gate, L1_xattn_v_up, L1_xattn_v_down, L1_xattn_l_gate, L1_xattn_l_up, L1_xattn_l_down)
    x = _L2_xattn_ref(x, ctx_1024, mask_BxS2_bk0, L2_xattn_ln_q_g, L2_xattn_ln_q_b, L2_xattn_Wq, L2_xattn_Wkv, L2_xattn_Wo, L2_xattn_attn_gate, L2_xattn_ln_ff_g, L2_xattn_ln_ff_b, L2_xattn_W1, L2_xattn_W2, L2_xattn_ff_gate)
    x = _L3_xattn_ref(x, ctx_1024, mask_BxS_ik0, pos_1xS, L3_xattn_ln_in_w, L3_xattn_ln_post_attn_w, L3_xattn_ln_post_cross_w, L3_xattn_v_qkv, L3_xattn_l_qkv, L3_xattn_v_dense, L3_xattn_l_dense, L3_xattn_cq_w, L3_xattn_ckv_w, L3_xattn_cdense_w, L3_xattn_v_gate, L3_xattn_v_up, L3_xattn_v_down, L3_xattn_l_gate, L3_xattn_l_up, L3_xattn_l_down)
    return x

_drawn_inputs = setup_inputs


def setup_inputs(seed=0):
    import zlib

    import numpy as np

    out = dict(_drawn_inputs(seed))
    spreads = {'L0_xattn_norm_w': (1.0, 0.2),
     'L1_xattn_ln_in_w': (1.0, 0.6),
     'L1_xattn_ln_post_attn_w': (1.0, 0.6),
     'L1_xattn_ln_post_cross_w': (1.0, 0.6),
     'L2_xattn_ln_q_g': (1.0, 0.6),
     'L2_xattn_ln_q_b': (0.0, 2.0),
     'L2_xattn_ln_ff_g': (1.0, 0.6),
     'L2_xattn_ln_ff_b': (0.0, 2.0),
     'L3_xattn_ln_in_w': (1.0, 0.6),
     'L3_xattn_ln_post_attn_w': (1.0, 0.6),
     'L3_xattn_ln_post_cross_w': (1.0, 0.6)}
    factors = {'L0_xattn_b_gate': 8.0,
     'L1_xattn_v_qkv': 8.0,
     'L1_xattn_v_dense': 6.979,
     'L1_xattn_cq_w': 64.0,
     'L1_xattn_v_gate': 6.46,
     'L1_xattn_v_up': 6.381,
     'L1_xattn_v_down': 6.375,
     'L2_xattn_W1': 15.253,
     'L3_xattn_v_qkv': 8.0,
     'L3_xattn_v_dense': 5.775,
     'L3_xattn_cq_w': 64.0,
     'L3_xattn_v_gate': 6.55,
     'L3_xattn_v_up': 6.449,
     'L3_xattn_v_down': 6.482,
     'L1_xattn_l_dense': 7.069,
     'L1_xattn_ckv_w': 6.392,
     'L1_xattn_cdense_w': 6.399,
     'L1_xattn_l_gate': 8.0,
     'L1_xattn_l_up': 8.0,
     'L1_xattn_l_down': 8.0,
     'L2_xattn_Wq': 28.229,
     'L2_xattn_W2': 4.566,
     'L3_xattn_l_qkv': 3.56,
     'L3_xattn_l_dense': 8.0,
     'L3_xattn_ckv_w': 8.0,
     'L3_xattn_cdense_w': 8.0,
     'L3_xattn_l_gate': 8.0,
     'L3_xattn_l_up': 8.0,
     'L3_xattn_l_down': 8.0,
     'L2_xattn_Wkv': 5.552,
     'L2_xattn_Wo': 5.491}
    for name, (base, spread) in spreads.items():
        noise = np.random.default_rng([zlib.crc32(name.encode()), seed]).standard_normal(out[name].shape)
        drawn = base * np.exp(spread * noise) if base else spread * noise
        out[name] = jnp.asarray(drawn.astype(out[name].dtype))
    for name, factor in factors.items():
        out[name] = (out[name] * factor).astype(out[name].dtype)
    return out
```

```python
import numpy as np
import concourse.bass as bass
from concourse import mybir
from contextlib import ExitStack

F32 = mybir.dt.float32
BF16 = mybir.dt.bfloat16
I32 = mybir.dt.int32
U8 = mybir.dt.uint8
ALU = mybir.AluOpType
ACT = mybir.ActivationFunctionType
AX = mybir.AxisListType

P = 128
B, S, D = 64, 64, 256
DC = 128
PAIRS = B // 2
CH = D // P
NH = 16
HD = D // NH
CHD = DC // NH
HD2 = 64
INNER = NH * HD2
J = NH // 2
I = 688
IC = -(-I // P)
FF = 4 * D
G = 4
GROUPS = PAIRS // G
GT = G * P
MASKED = -1.0e38
FIRST, LAST = 3, 26

C_IDENT, C_H16, C_H8, C_CAUSAL, C_BLOCK, C_ROPE, C_IOTA = 0, 128, 136, 152, 216, 344, 376
C_ALL = 377


def constants():
    c = np.zeros((P, C_ALL), np.float32)
    r = np.arange(P)
    c[:, C_IDENT:C_IDENT + P] = np.eye(P)
    c[:, C_H16:C_H16 + 8] = (r[:, None] // HD) == np.arange(8)
    c[:, C_H8:C_H8 + 16] = (r[:, None] // CHD) == np.arange(16)
    c[:, C_CAUSAL:C_CAUSAL + S] = np.where(np.arange(S) > (r % S)[:, None], np.float32(MASKED), 0)
    c[:, C_BLOCK:C_BLOCK + P] = np.where(r[:, None] // S != r[None] // S, np.float32(MASKED), 0)
    inv = np.float32(1) / np.float32(10000) ** (np.arange(0, HD, 2, dtype=np.float32) / np.float32(HD))
    f = np.outer(np.arange(S, dtype=np.float32), inv).astype(np.float32)
    c[:S, C_ROPE:C_ROPE + HD] = np.concatenate([np.cos(f), np.cos(f)], 1)
    c[:S, C_ROPE + HD:C_ROPE + 2 * HD] = np.concatenate([-np.sin(f), np.sin(f)], 1)
    c[:, C_IOTA] = r
    return c


class Count:

    def __init__(self, handle, per=1):
        self.handle, self.per, self.base = handle, per, 0

    def at(self, units, extra=0):
        return units * self.per + (self.base + extra)

    def due(self, units, extra=0):
        return not isinstance(units, int) or units * self.per + extra > 0

    def close(self, units):
        self.base += self.per * units


def build(nc, t):
    with ExitStack() as ctx:
        def sb(name, shape, dt=F32, where=None):
            return (where or ctx).enter_context(nc.sbuf_tensor(name, shape, dt))

        def ps(name, cols=512):
            return ctx.enter_context(nc.psum_tensor(name, [P, cols], F32))

        def count(name, per=1):
            return Count(ctx.enter_context(nc.semaphore(name)), per)

        x_res = sb("x_res", [P, PAIRS * D])
        const = sb("const", [P, C_ALL])
        ident_b = sb("ident_b", [P, P], BF16)
        causal_b = sb("causal_b", [P, S], BF16)
        block_b = sb("block_b", [P, P], BF16)
        keymask = sb("keymask", [P, PAIRS, S], BF16)
        rope = sb("rope", [P, 2 * HD])
        vm = sb("vm", [P, PAIRS, 2])
        half_neg = sb("half_neg", [P, G])
        eps6 = sb("eps6", [P, G])
        eps5 = sb("eps5", [P, G])
        stat = sb("stat", [P, 2, G])
        rstd = sb("rstd", [P, 2, G])
        ident = const[:, C_IDENT:C_IDENT + P]

        ps_t = ps("ps_t")
        ps_a = ps("ps_a")
        ps_b = ps("ps_b")
        ps_s = ps("ps_s", 1024)
        ps_p = ps("ps_p")
        ps_o = ps("ps_o")
        ps_d = ps("ps_d")

        loaded = count("loaded", 16)
        ctx_in = [count(f"ctx_in{u}", 16) for u in range(2)]
        stored = count("stored", 16)
        cold = count("cold")
        stat_ok = count("stat_ok")
        aggr_ok = count("aggr_ok")
        eps_ok = count("eps_ok")
        rstd_ok = count("rstd_ok")
        mixw_ok = count("mixw_ok")
        xn_ok = count("xn_ok")
        xt_pe = count("xt_pe")
        xt_ok = count("xt_ok")
        qk_pe = count("qk_pe")
        rope1 = count("rope1")
        rope_ok = count("rope_ok")
        qkt_pe = count("qkt_pe")
        qkt_ok = count("qkt_ok")
        kx_ok = count("kx_ok")
        v_pe = count("v_pe")
        v_ok = count("v_ok")
        s_pe = count("s_pe")
        max_ok = count("max_ok")
        sub_ok = count("sub_ok")
        exp_ok = count("exp_ok")
        sum_ok = count("sum_ok")
        inv_ok = count("inv_ok")
        prob_ok = count("prob_ok")
        pt_pe = count("pt_pe", 2)
        pt_ok = count("pt_ok", 2)
        pv_pe = count("pv_pe", 2)
        o_ok = count("o_ok", 2)
        d_pe = count("d_pe")
        sel_ok = count("sel_ok")
        q2_pe, q2_ok, k2_pe, k2_ok, v2_pe = (
            count(name, 2) for name in ("q2_pe", "q2_ok", "k2_pe", "k2_ok", "v2_pe"))
        v_half = count("v_half")
        g_pe = count("g_pe")
        a_ok = count("a_ok")
        h_ok = count("h_ok")
        mix_ok = count("mix_ok")
        res_ok = count("res_ok")
        def arrival(p, u, dmas):
            return (p + (2 - u)) * (8 * dmas) + ctx_in[u].base

        def close(units, *used):
            for c in used:
                c.close(units)

        def x_tile(p):
            return x_res[:, bass.ds(p * D, D)]

        def steps(eng, step):
            for p in range(FIRST):
                step(p, p % 2)
            with eng.Fori(0, (LAST - FIRST + 1) // 2) as i:
                for u in range(2):
                    step(2 * i + (FIRST + u), (FIRST + u) % 2)
            for p in range(LAST + 1, PAIRS + 1):
                step(p, p % 2)

        def has(p):
            return not isinstance(p, int) or 0 <= p < PAIRS

        with ExitStack() as own:
            m_raw = sb("m_raw", [B, S], I32, own)
            m_one = sb("m_one", [B, S], F32, own)
            vm_bs = sb("vm_bs", [B, 2, S], F32, own)
            km_raw = sb("km_raw", [P, PAIRS, S], U8, own)
            pos_raw = sb("pos_raw", [S, S], I32, own)
            pos = sb("pos", [S, 2, S], F32, own)
            onehot = sb("onehot", [S, 2, S], F32, own)
            with nc.Block() as block:
                @block.sync
                def _(sp):
                    sp.dma_start(const[:], t["consts"]).then_inc(loaded.handle, 16)
                    sp.dma_start(m_raw[:], t["mask_BxS_ik0"]).then_inc(loaded.handle, 16)
                    sp.dma_start(pos_raw[:], t["pos_1xS"].broadcast_to([S, S])).then_inc(loaded.handle, 16)
                    km = t["mask_BxS2_bk0"].rearrange("(n two) k -> two n k", two=2)
                    for u in range(2):
                        sp.dma_start(km_raw[S * u:S * u + S], km[u:u + 1].broadcast_to([S, PAIRS, S])) \
                            .then_inc(loaded.handle, 16)
                    xin = t["x"].rearrange("(n two) s d -> (two s) n d", two=2)
                    x3 = x_res[:].rearrange("p (n d) -> p n d", d=D)
                    for g in range(GROUPS):
                        sp.dma_start(x3[:, g * G:g * G + G], xin[:, g * G:g * G + G]).then_inc(loaded.handle, 16)

                @block.gpsimd
                def _(pool):
                    nc.gpsimd.memset(eps6[:], 1e-6)
                    nc.gpsimd.memset(eps5[:], 1e-5)
                    nc.gpsimd.memset(half_neg[:], -0.5).then_inc(cold.handle, 1)

                @block.vector
                def _(dve):
                    dve.wait_ge(loaded.handle, 16 * (5 + GROUPS))
                    nc.vector.tensor_copy(ident_b[:], ident)
                    nc.vector.tensor_copy(causal_b[:], const[:, C_CAUSAL:C_CAUSAL + S])
                    nc.vector.tensor_copy(block_b[:], const[:, C_BLOCK:C_BLOCK + P])
                    nc.vector.tensor_scalar(keymask[:], km_raw[:], 1.0, -MASKED, ALU.subtract, ALU.mult)
                    nc.vector.tensor_scalar(m_one[:], m_raw[:], 1.0, None, ALU.is_equal).then_inc(aggr_ok.handle, 1)
                    nc.vector.memset(vm_bs[:], 0.0).then_inc(sub_ok.handle, 1)
                    dve.wait_ge(aggr_ok.handle, 1)
                    dve.wait_ge(sub_ok.handle, 1)
                    for r in range(2):
                        nc.vector.tensor_tensor(vm_bs[:, r, 0:S - 1], m_one[:, 0:S - 1], m_one[:, 1:S], ALU.mult) \
                            .then_inc(sel_ok.handle, 1)
                    nc.vector.tensor_copy(pos[:, 0], pos_raw[:]).then_inc(rope1.handle, 1)
                    dve.wait_ge(rope1.handle, 1)
                    nc.vector.tensor_scalar(pos[:, 1], pos[:, 0], 0.0, float(S), ALU.is_lt, ALU.mult) \
                        .then_inc(rope1.handle, 1)
                    dve.wait_ge(rope1.handle, 2)
                    nc.vector.tensor_tensor(pos[:, 0], pos[:, 0], pos[:, 1], ALU.add).then_inc(rope1.handle, 1)
                    dve.wait_ge(rope1.handle, 3)
                    nc.vector.tensor_scalar(pos[:, 1], pos[:, 0], 0.0, float(S - 1), ALU.max, ALU.min) \
                        .then_inc(rope1.handle, 1)
                    dve.wait_ge(rope1.handle, 4)
                    for r in range(2):
                        nc.vector.tensor_scalar(onehot[:, r], pos[:, 1], const[0:S, C_IOTA:C_IOTA + 1], None,
                                                ALU.is_equal).then_inc(sel_ok.handle, 1)
                    nc.vector.memset(stat[:], 1.0).then_inc(cold.handle, 1)
                    dve.wait_ge(xt_pe.handle, 1)
                    nc.vector.tensor_copy(rope[:], ps_a[:, 0:2 * HD]).then_inc(cold.handle, 1)
                    for u in range(2):
                        nc.vector.tensor_copy(
                            vm[S * u:S * u + S, :, 0],
                            ps_t[S * u:S * u + S, 0:B].rearrange("p (n two) -> p n two", two=2)[:, :, u]) \
                            .then_inc(mix_ok.handle, 1)
                    dve.wait_ge(mix_ok.handle, 2)
                    nc.vector.tensor_scalar(vm[:, :, 1], vm[:, :, 0], -1.0, 1.0, ALU.mult, ALU.add) \
                        .then_inc(cold.handle, 1)

                @block.tensor
                def _(pe):
                    pe.wait_ge(loaded.handle, 16 * (5 + GROUPS))
                    pe.wait_ge(sel_ok.handle, 4)
                    nc.tensor.matmul(ps_a[:, 0:2 * HD], onehot[:].rearrange("p r s -> p (r s)"),
                                     const[0:S, C_ROPE:C_ROPE + 2 * HD], start=True, stop=True)
                    nc.tensor.transpose(ps_t[:, 0:B], vm_bs[:].rearrange("p r s -> p (r s)"), ident[0:B, 0:B]) \
                        .then_inc(xt_pe.handle, 1)
            loaded.base += 16 * (5 + GROUPS)
            cold.base += 4
            aggr_ok.base += 1
            sub_ok.base += 1
            sel_ok.base += 4
            rope1.base += 4
            mix_ok.base += 2
            xt_pe.base += 1

        def put_rstd(pool, p, u, eps):
            pool.wait_ge(stat_ok.handle, stat_ok.at(p + 1))
            nc.gpsimd.tensor_tensor(stat[:, u, 1:2], stat[:, u, 0:1], eps[:, 0:1], ALU.add).then_inc(eps_ok.handle, 1)
            pool.wait_ge(eps_ok.handle, eps_ok.at(p + 1))
            if xn_ok.due(p - 1):
                pool.wait_ge(xn_ok.handle, xn_ok.at(p - 1))
            nc.gpsimd.tensor_tensor(rstd[:, u, 0:1], stat[:, u, 1:2], half_neg[:, 0:1], ALU.pow) \
                .then_inc(rstd_ok.handle, 1)

        def softmax_front(dve, mx, probs, p, u):
            s3 = ps_s[:].rearrange("p (h k) -> p h k", k=S)
            dve.wait_ge(s_pe.handle, s_pe.at(p + 1))
            nc.vector.tensor_reduce(mx[:, u], s3, op=ALU.max, axis=AX.X).then_inc(max_ok.handle, 1)
            dve.wait_ge(max_ok.handle, max_ok.at(p + 1))
            if pt_pe.due(p - 1):
                dve.wait_ge(pt_pe.handle, pt_pe.at(p - 1))
            nc.vector.tensor_tensor(probs[:, u].rearrange("p (h k) -> p h k", k=S), s3,
                                    mx[:, u].unsqueeze(2).broadcast_to([P, NH, S]), ALU.subtract) \
                .then_inc(sub_ok.handle, 1)

        def softmax_exp(act, probs, p, u, scale):
            act.wait_ge(sub_ok.handle, sub_ok.at(p + 1))
            nc.scalar.activation(probs[:, u], probs[:, u], ACT.Exp, scale=scale).then_inc(exp_ok.handle, 1)

        def softmax_sum(dve, sm, probs, p, u):
            dve.wait_ge(exp_ok.handle, exp_ok.at(p + 1))
            if prob_ok.due(p - 1):
                dve.wait_ge(prob_ok.handle, prob_ok.at(p - 1))
            nc.vector.tensor_reduce(sm[:, u, 0], probs[:, u].rearrange("p (h k) -> p h k", k=S),
                                    op=ALU.add, axis=AX.X).then_inc(sum_ok.handle, 1)
            dve.wait_ge(sum_ok.handle, sum_ok.at(p + 1))
            nc.vector.reciprocal(sm[:, u, 1], sm[:, u, 0]).then_inc(inv_ok.handle, 1)

        def softmax_norm(pool, sm, probs, p, u):
            pool.wait_ge(inv_ok.handle, inv_ok.at(p + 1))
            pr = probs[:, u].rearrange("p (h k) -> p h k", k=S)
            nc.gpsimd.tensor_tensor(pr, pr, sm[:, u, 1].unsqueeze(2).broadcast_to([P, NH, S]), ALU.mult) \
                .then_inc(prob_ok.handle, 1)

        def prob_transposes(pe, probs, p, u):
            pe.wait_ge(prob_ok.handle, prob_ok.at(p + 1))
            for r, bank in enumerate((ps_p, ps_d)):
                if r == 0:
                    if pt_ok.due(p):
                        pe.wait_ge(pt_ok.handle, pt_ok.at(p))
                    if o_ok.due(p):
                        pe.wait_ge(o_ok.handle, o_ok.at(p))
                else:
                    if res_ok.due(p):
                        pe.wait_ge(res_ok.handle, res_ok.at(p))
                for j in range(4):
                    ins = nc.tensor.transpose(bank[:, j * P:j * P + P],
                                              probs[:, u, (4 * r + j) * P:(4 * r + j + 1) * P], ident)
                ins.then_inc(pt_pe.handle, 1)

        def prob_copies(act, pt, p):
            for r, bank in enumerate((ps_p, ps_d)):
                act.wait_ge(pt_pe.handle, pt_pe.at(p, r + 1))
                if r == 0:
                    if pv_pe.due(p):
                        act.wait_ge(pv_pe.handle, pv_pe.at(p))
                nc.scalar.activation(pt[:, 4 * r:4 * r + 4].rearrange("p j q -> p (j q)"), bank[:], ACT.Copy) \
                    .then_inc(pt_ok.handle, 1)

        def layer0():
            with ExitStack() as own:
                w_mem = sb("w_mem", [P, D], F32, own)
                w_gate = sb("w_gate", [P, 2 * CH, D], F32, own)
                bias = sb("l0_bias", [P, D], F32, own)
                w_norm = sb("l0_norm", [P, D], F32, own)
                rows = sb("l0_rows", [P, 2, D + DC], F32, own)
                xt = sb("l0_xt", [P, 2, 3 * P], F32, own)
                mpt = sb("l0_mpt", [P, 2 * P], F32, own)
                mp = sb("l0_mp", [P, 2, D], F32, own)
                gx = sb("l0_gx", [P, PAIRS * D], F32, own)
                mx = sb("l0_mx", [P, 2, 2], F32, own)
                sm = sb("l0_sm", [P, 2, 2], F32, own)
                pr = sb("l0_pr", [P, 2, 2, P], F32, own)
                pt = sb("l0_pt", [P, P], F32, own)
                mc = sb("l0_mc", [P, 2, D], F32, own)
                mct = sb("l0_mct", [P, 2 * P], F32, own)
                z = sb("l0_z", [P, 3, D], F32, own)
                junk = sb("l0_junk", [P, D], F32, own)
                SCALE = D ** -0.5

                with nc.Block() as block:
                    @block.sync
                    def _(sp):
                        sp.dma_start(w_mem[:], t["W_mem_T"]).then_inc(loaded.handle, 16)
                        sp.dma_start(w_gate[:], t["W_gate_T"].rearrange("(c p) n -> p c n", p=P)) \
                            .then_inc(loaded.handle, 16)
                        sp.dma_start(bias[:], t["L0_xattn_b_gate"].rearrange("(a n) -> a n", a=1).broadcast_to([P, D])) \
                            .then_inc(loaded.handle, 16)
                        sp.dma_start(w_norm[:], t["L0_xattn_norm_w"].rearrange("(a n) -> a n", a=1)
                                     .broadcast_to([P, D])).then_inc(loaded.handle, 16)

                        def step(p, u):
                            if has(p + 2):
                                if xt_pe.due(p + 1):
                                    sp.wait_ge(xt_pe.handle, xt_pe.at(p + 1))
                                sp.dma_start(rows[:, u, 0:D], x_flat[bass.ds((p + 2) * P, P), :]) \
                                    .then_inc(ctx_in[u].handle, 16)
                                sp.dma_start(rows[:, u, D:D + DC], ctx_rows(p + 2)).then_inc(ctx_in[u].handle, 16)
                        for p in (-2, -1):
                            step(p, p % 2)
                        steps(sp, step)

                    @block.tensor
                    def _(pe):
                        pe.wait_ge(loaded.handle, loaded.at(0, 64))

                        def xt_(p, u):
                            pe.wait_ge(ctx_in[u].handle, arrival(p, u, 2))
                            if xt_ok.due(p):
                                pe.wait_ge(xt_ok.handle, xt_ok.at(p))
                            for c in range(3):
                                ins = nc.tensor.transpose(ps_t[:, c * P:c * P + P], rows[:, u, c * P:c * P + P], ident)
                            ins.then_inc(xt_pe.handle, 1)

                        def memory_t(p, u):
                            pe.wait_ge(xt_ok.handle, xt_ok.at(p + 1))
                            if qkt_ok.due(p):
                                pe.wait_ge(qkt_ok.handle, qkt_ok.at(p))
                            for c in range(CH):
                                ins = nc.tensor.matmul(ps_a[:, c * P:c * P + P], w_mem[:, c * P:c * P + P],
                                                       xt[:, u, 2 * P:3 * P], start=True, stop=True)
                            ins.then_inc(qk_pe.handle, 1)

                        def memory(p, u):
                            if v_ok.due(p):
                                pe.wait_ge(v_ok.handle, v_ok.at(p))
                            nc.tensor.matmul(ps_b[:, 0:D], xt[:, u, 2 * P:3 * P], w_mem[:], start=True, stop=True)
                            for c in range(CH):
                                ins = nc.tensor.matmul(ps_b[:, D:2 * D], xt[:, u, c * P:c * P + P], w_gate[:, c],
                                                       start=(c == 0), stop=(c == CH - 1))
                            ins.then_inc(v_pe.handle, 1)

                        def scores(p, u):
                            pe.wait_ge(qkt_ok.handle, qkt_ok.at(p + 1))
                            if exp_ok.due(p):
                                pe.wait_ge(exp_ok.handle, exp_ok.at(p))
                            nc.tensor.matmul(ps_s[:, 0:P], ident_b[:], block_b[:], start=True, stop=False)
                            for c in range(CH):
                                ins = nc.tensor.matmul(ps_s[:, 0:P], xt[:, u, c * P:c * P + P], mpt[:, c * P:c * P + P],
                                                       start=False, stop=(c == CH - 1))
                            ins.then_inc(s_pe.handle, 1)

                        def probs_t(p, u):
                            pe.wait_ge(prob_ok.handle, prob_ok.at(p + 1))
                            if pt_ok.due(p):
                                pe.wait_ge(pt_ok.handle, pt_ok.at(p))
                            nc.tensor.transpose(ps_p[:, 0:P], pr[:, u, 1], ident).then_inc(pt_pe.handle, 2)

                        def context(p, u):
                            pe.wait_ge(pt_ok.handle, pt_ok.at(p + 1))
                            pe.wait_ge(v_ok.handle, v_ok.at(p + 1))
                            if o_ok.due(p):
                                pe.wait_ge(o_ok.handle, o_ok.at(p))
                            nc.tensor.matmul(ps_o[:, 0:D], pt[:], mp[:, u], start=True, stop=True) \
                                .then_inc(pv_pe.handle, 1)

                        def context_t(p, u):
                            pe.wait_ge(o_ok.handle, o_ok.at(p, 1))
                            for c in range(CH):
                                ins = nc.tensor.transpose(ps_o[:, D + c * P:D + c * P + P], mc[:, u, c * P:c * P + P], ident)
                            ins.then_inc(pv_pe.handle, 1)

                        def gate(p, u):
                            pe.wait_ge(o_ok.handle, o_ok.at(p + 1))
                            if sel_ok.due(p):
                                pe.wait_ge(sel_ok.handle, sel_ok.at(p))
                            for c in range(CH):
                                ins = nc.tensor.matmul(ps_d[:, 0:D], mct[:, c * P:c * P + P], w_gate[:, CH + c],
                                                       start=(c == 0), stop=(c == CH - 1))
                            ins.then_inc(d_pe.handle, 1)

                        def step(p, u):
                            v = 1 - u
                            if has(p):
                                scores(p, u)
                            if has(p - 1):
                                probs_t(p - 1, v)
                            if has(p + 1):
                                memory_t(p + 1, v)
                            if has(p - 1):
                                context(p - 1, v)
                            if has(p + 1):
                                memory(p + 1, v)
                            if has(p - 1):
                                context_t(p - 1, v)
                            if has(p + 2):
                                xt_(p + 2, u)
                            if has(p - 1):
                                gate(p - 1, v)
                        xt_(0, 0)
                        memory_t(0, 0)
                        memory(0, 0)
                        xt_(1, 1)
                        steps(pe, step)

                    @block.scalar
                    def _(act):
                        def xt_copy(p, u):
                            act.wait_ge(xt_pe.handle, xt_pe.at(p + 1))
                            if has(p - 1):
                                if s_pe.due(p - 1):
                                    act.wait_ge(s_pe.handle, s_pe.at(p - 1))
                                if v_pe.due(p - 1):
                                    act.wait_ge(v_pe.handle, v_pe.at(p - 1))
                            nc.scalar.activation(xt[:, u], ps_t[:, 0:3 * P], ACT.Copy).then_inc(xt_ok.handle, 1)

                        def mpt_copy(p):
                            act.wait_ge(qk_pe.handle, qk_pe.at(p + 1))
                            if s_pe.due(p):
                                act.wait_ge(s_pe.handle, s_pe.at(p))
                            nc.scalar.activation(mpt[:], ps_a[:, 0:2 * P], ACT.Copy).then_inc(qkt_ok.handle, 1)

                        def step(p, u):
                            v = 1 - u
                            if has(p - 2):
                                act.wait_ge(sel_ok.handle, sel_ok.at(p - 1))
                                nc.scalar.activation(z[:, 1], z[:, 0], ACT.Tanh, scale=0.5).then_inc(rope1.handle, 1)
                            if has(p - 1):
                                act.wait_ge(pt_pe.handle, pt_pe.at(p))
                                if pv_pe.due(p - 1):
                                    act.wait_ge(pv_pe.handle, pv_pe.at(p - 1))
                                nc.scalar.activation(pt[:], ps_p[:, 0:P], ACT.Copy).then_inc(pt_ok.handle, 2)
                            if has(p):
                                act.wait_ge(sub_ok.handle, sub_ok.at(p + 1))
                                if prob_ok.due(p - 1):
                                    act.wait_ge(prob_ok.handle, prob_ok.at(p - 1))
                                nc.scalar.activation(pr[:, u, 0], ps_s[:, 0:P], ACT.Exp, bias=mx[:, u, 1:2],
                                                     scale=SCALE, accum_out=sm[:, u, 0:1]).then_inc(exp_ok.handle, 1)
                            if has(p - 2):
                                act.wait_ge(mix_ok.handle, mix_ok.at(p - 1))
                                if eps_ok.due(p - 3):
                                    act.wait_ge(eps_ok.handle, eps_ok.at(p - 3))
                                if stat_ok.due(p - 2):
                                    act.wait_ge(stat_ok.handle, stat_ok.at(p - 2))
                                nc.scalar.activation(junk[:], x_tile(p - 2), ACT.Square, scale=D ** -0.5,
                                                     accum_out=stat[:, u, 0:1]).then_inc(stat_ok.handle, 1)
                            if has(p + 1):
                                mpt_copy(p + 1)
                            if has(p - 1):
                                act.wait_ge(pv_pe.handle, pv_pe.at(p - 1, 1))
                                if mix_ok.due(p - 2):
                                    act.wait_ge(mix_ok.handle, mix_ok.at(p - 2))
                                nc.scalar.activation(mc[:, v], ps_o[:, 0:D], ACT.Copy).then_inc(o_ok.handle, 1)
                            if has(p - 1):
                                act.wait_ge(pv_pe.handle, pv_pe.at(p))
                                if d_pe.due(p - 1):
                                    act.wait_ge(d_pe.handle, d_pe.at(p - 1))
                                nc.scalar.activation(mct[:], ps_o[:, D:D + 2 * P], ACT.Copy).then_inc(o_ok.handle, 1)
                            if has(p + 2):
                                xt_copy(p + 2, u)
                        xt_copy(0, 0)
                        mpt_copy(0)
                        xt_copy(1, 1)
                        steps(act, step)
                        step(PAIRS + 1, 1)

                    @block.vector
                    def _(dve):
                        dve.wait_ge(loaded.handle, loaded.at(0, 64))

                        def v_copy(p, u):
                            dve.wait_ge(v_pe.handle, v_pe.at(p + 1))
                            if pv_pe.due(p - 2, 1):
                                dve.wait_ge(pv_pe.handle, pv_pe.at(p - 2, 1))
                            nc.vector.tensor_tensor(gx[:, bass.ds(p * D, D)], ps_b[:, D:2 * D], bias[:], ALU.add) \
                                .then_inc(kx_ok.handle, 1)
                            nc.vector.tensor_copy(mp[:, u], ps_b[:, 0:D]).then_inc(v_ok.handle, 1)

                        def step(p, u):
                            v = 1 - u
                            if has(p - 2):
                                dve.wait_ge(d_pe.handle, d_pe.at(p - 1))
                                if rope1.due(p - 2):
                                    dve.wait_ge(rope1.handle, rope1.at(p - 2))
                                dve.wait_ge(kx_ok.handle, kx_ok.at(p - 1))
                                nc.vector.tensor_tensor(z[:, 0], ps_d[:, 0:D], gx[:, bass.ds((p - 2) * D, D)], ALU.add) \
                                    .then_inc(sel_ok.handle, 1)
                            if has(p):
                                dve.wait_ge(s_pe.handle, s_pe.at(p + 1))
                                nc.vector.tensor_reduce(mx[:, u, 0:1], ps_s[:, 0:P], op=ALU.max, axis=AX.X) \
                                    .then_inc(max_ok.handle, 1)
                                dve.wait_ge(max_ok.handle, max_ok.at(p + 1))
                                nc.vector.tensor_scalar(mx[:, u, 1:2], mx[:, u, 0:1], -SCALE, None, ALU.mult) \
                                    .then_inc(sub_ok.handle, 1)
                            if has(p - 2):
                                dve.wait_ge(rope1.handle, rope1.at(p - 1))
                                nc.vector.scalar_tensor_tensor(z[:, 2], z[:, 1], 1.0, mc[:, u], ALU.add, ALU.mult) \
                                    .then_inc(aggr_ok.handle, 1)
                                dve.wait_ge(aggr_ok.handle, aggr_ok.at(p - 1))
                                nc.vector.scalar_tensor_tensor(x_tile(p - 2), z[:, 2], 0.5, x_tile(p - 2),
                                                               ALU.mult, ALU.add).then_inc(mix_ok.handle, 1)
                            if has(p):
                                dve.wait_ge(exp_ok.handle, exp_ok.at(p + 1))
                                nc.vector.reciprocal(sm[:, u, 1:2], sm[:, u, 0:1]).then_inc(inv_ok.handle, 1)
                                dve.wait_ge(inv_ok.handle, inv_ok.at(p + 1))
                                if pt_pe.due(p - 1):
                                    dve.wait_ge(pt_pe.handle, pt_pe.at(p - 1))
                                nc.vector.tensor_scalar(pr[:, u, 1], pr[:, u, 0], sm[:, u, 1:2], None, ALU.mult) \
                                    .then_inc(prob_ok.handle, 1)
                            if has(p + 1):
                                v_copy(p + 1, v)
                            if has(p - 2):
                                dve.wait_ge(rstd_ok.handle, rstd_ok.at(p - 1))
                                dve.wait_ge(stat_ok.handle, stat_ok.at(p - 1))
                                nc.vector.scalar_tensor_tensor(x_tile(p - 2), x_tile(p - 2), rstd[:, u, 0:1],
                                                               w_norm[:], ALU.mult, ALU.mult).then_inc(res_ok.handle, 1)
                        v_copy(0, 0)
                        steps(dve, step)
                        step(PAIRS + 1, 1)

                    @block.gpsimd
                    def _(pool):
                        def step(p, u):
                            if has(p - 2):
                                pool.wait_ge(stat_ok.handle, stat_ok.at(p - 1))
                                nc.gpsimd.tensor_tensor(stat[:, u, 1:2], stat[:, u, 0:1], eps6[:, 0:1], ALU.add) \
                                    .then_inc(eps_ok.handle, 1)
                                pool.wait_ge(eps_ok.handle, eps_ok.at(p - 1))
                                if res_ok.due(p - 3):
                                    pool.wait_ge(res_ok.handle, res_ok.at(p - 3))
                                nc.gpsimd.tensor_tensor(rstd[:, u, 0:1], stat[:, u, 1:2], half_neg[:, 0:1], ALU.pow) \
                                    .then_inc(rstd_ok.handle, 1)
                        steps(pool, step)
                        step(PAIRS + 1, 1)
                loaded.base += 64
                for c in ctx_in:
                    c.base += 16 * PAIRS
                close(PAIRS, stat_ok, aggr_ok, eps_ok, rstd_ok, xt_pe, xt_ok, qk_pe, rope1, qkt_ok, kx_ok,
                      v_pe, v_ok, s_pe, max_ok, sub_ok, exp_ok, inv_ok, prob_ok, pt_pe, pt_ok, pv_pe, o_ok, d_pe,
                      sel_ok, mix_ok, res_ok)

        x_flat = t["x"].rearrange("b s d -> (b s) d")
        ctx_flat = t["ctx_1024"].rearrange("b s d -> (b s) d")

        def ctx_rows(p):
            return ctx_flat[bass.ds(p * P, P), :]

        def self_attention(n):
            L = f"L{n}_xattn_"
            with ExitStack() as own:
                def ob(name, shape, dt=F32):
                    return sb(f"s{n}_{name}", shape, dt, own)

                w_qkv = ob("w_qkv", [P, 2 * CH, 3 * D])
                w_out = ob("w_out", [P, CH, 2, D])
                w_ln = ob("w_ln", [P, CH])
                junk = ob("junk", [P, D])
                mixw = ob("mixw", [P, 2])
                xn = ob("xn", [P, 2, D])
                xt = ob("xt", [P, 2, CH, 2, P])
                roped = ob("roped", [P, 2, 2 * D])
                qkt = ob("qkt", [P, 4, P])
                kx = ob("kx", [P, CH, 2, 8, S])
                vb = ob("vb", [P, 2, 2, J, 2, HD])
                mx = ob("mx", [P, 2, NH])
                sm = ob("sm", [P, 2, 2, NH])
                probs = ob("probs", [P, 2, NH * S])
                pt = ob("pt", [P, J, P])
                ot = ob("ot", [P, CH, P])
                sel = ob("sel", [P, 2])
                part = ob("part", [P, D])

                with nc.Block() as block:
                    @block.sync
                    def _(sp):
                        for e, x in enumerate("vl"):
                            sp.dma_start(w_qkv[:, e * CH:e * CH + CH],
                                         t[L + x + "_qkv"].rearrange("(c p) n -> p c n", p=P)).then_inc(loaded.handle, 16)
                            sp.dma_start(w_out[:, :, e], t[L + x + "_dense"].rearrange("(c p) n -> p c n", p=P)) \
                                .then_inc(loaded.handle, 16)
                        sp.dma_start(w_ln[:], t[L + "ln_in_w"]).then_inc(loaded.handle, 16)

                    @block.tensor
                    def _(pe):
                        pe.wait_ge(loaded.handle, loaded.at(0, 80))
                        pe.wait_ge(cold.handle, cold.at(0, 1))

                        def xt_(p, u):
                            pe.wait_ge(xn_ok.handle, xn_ok.at(p + 1))
                            if qkt_ok.due(p):
                                pe.wait_ge(qkt_ok.handle, qkt_ok.at(p))
                            for c in range(CH):
                                for e in range(2):
                                    ins = nc.tensor.transpose(ps_t[:, (2 * c + e) * P:(2 * c + e + 1) * P],
                                                              xn[:, e, c * P:c * P + P], ident)
                            ins.then_inc(xt_pe.handle, 1)

                        def proj_qk(p, u):
                            pe.wait_ge(xt_ok.handle, xt_ok.at(p + 1))
                            if rope1.due(p):
                                pe.wait_ge(rope1.handle, rope1.at(p))
                            for k in range(2 * CH):
                                e, c = divmod(k, CH)
                                ins = nc.tensor.matmul(ps_a[:], xt[:, u, c, e], w_qkv[:, k, 0:2 * D],
                                                       start=(k == 0), stop=(k == 2 * CH - 1))
                            ins.then_inc(qk_pe.handle, 1)

                        def proj_v(p, u):
                            if v_ok.due(p):
                                pe.wait_ge(v_ok.handle, v_ok.at(p))
                            for b in range(2):
                                for h in range(2):
                                    for k in range(2 * CH):
                                        e, c = divmod(k, CH)
                                        w = w_qkv[:, k, 2 * D:3 * D].rearrange("p (j h d) -> p j h d", h=2, d=HD)
                                        ins = nc.tensor.matmul(ps_b[S * h:S * h + S, b * P:b * P + P],
                                                               xt[:, u, c, e, b * S:b * S + S], w[:, :, h],
                                                               start=(k == 0), stop=(k == 2 * CH - 1))
                            ins.then_inc(v_pe.handle, 1)

                        def qk_t(p):
                            pe.wait_ge(rope_ok.handle, rope_ok.at(p + 1))
                            pe.wait_ge(xt_ok.handle, xt_ok.at(p + 1))
                            for c in range(4):
                                ins = nc.tensor.transpose(ps_t[:, c * P:c * P + P], roped[:, 0, c * P:c * P + P], ident)
                            ins.then_inc(qkt_pe.handle, 1)

                        def scores(p):
                            if sub_ok.due(p):
                                pe.wait_ge(sub_ok.handle, sub_ok.at(p))
                            pe.wait_ge(kx_ok.handle, kx_ok.at(p + 1))
                            for h in range(CH):
                                out = ps_s[:, 512 * h:512 * h + 512]
                                nc.tensor.matmul(out, ident_b[:], causal_b[:].unsqueeze(1).broadcast_to([P, 8, S]),
                                                 start=True, stop=False, skip_group_check=True)
                                for b in range(2):
                                    ins = nc.tensor.matmul(out[b * S:b * S + S], qkt[:, h, b * S:b * S + S],
                                                           kx[:, h, b].rearrange("p h k -> p (h k)"),
                                                           start=False, stop=True, skip_group_check=True)
                            ins.then_inc(s_pe.handle, 1)

                        def pv(p, u):
                            pe.wait_ge(pt_ok.handle, pt_ok.at(p + 1))
                            pe.wait_ge(v_ok.handle, v_ok.at(p + 1))
                            if o_ok.due(p):
                                pe.wait_ge(o_ok.handle, o_ok.at(p))
                            for b in range(2):
                                for j in range(J):
                                    r, h = j % 4, j // 4
                                    ins = nc.tensor.matmul(
                                        ps_o[32 * r:32 * r + 32, h * P + b * S:h * P + b * S + S],
                                        vb[:, u, b, j].rearrange("p h d -> p (h d)"), pt[:, j, b * S:b * S + S],
                                        start=True, stop=True, skip_group_check=True)
                            ins.then_inc(pv_pe.handle, 2)

                        def dense(p):
                            pe.wait_ge(o_ok.handle, o_ok.at(p + 1))
                            for c in range(CH):
                                ins = nc.tensor.matmul(ps_d[:], ot[:, c], w_out[:, c].rearrange("p e n -> p (e n)"),
                                                       start=(c == 0), stop=(c == CH - 1))
                            ins.then_inc(d_pe.handle, 1)

                        def step(p, u):
                            v = 1 - u
                            if has(p + 1):
                                proj_qk(p + 1, v)
                            if has(p):
                                scores(p)
                            if has(p + 1):
                                qk_t(p + 1)
                            if has(p - 1):
                                prob_transposes(pe, probs, p - 1, v)
                            if has(p + 2):
                                xt_(p + 2, u)
                            if has(p - 1):
                                pv(p - 1, v)
                            if has(p + 1):
                                proj_v(p + 1, v)
                            if has(p - 1):
                                dense(p - 1)
                        xt_(0, 0)
                        proj_qk(0, 0)
                        qk_t(0)
                        xt_(1, 1)
                        proj_v(0, 0)
                        steps(pe, step)

                    @block.scalar
                    def _(act):
                        act.wait_ge(loaded.handle, loaded.at(0, 80))

                        def stat_(p, u):
                            if eps_ok.due(p - 1):
                                act.wait_ge(eps_ok.handle, eps_ok.at(p - 1))
                            if stat_ok.due(p):
                                act.wait_ge(stat_ok.handle, stat_ok.at(p))
                            nc.scalar.activation(junk[:], x_tile(p), ACT.Square, scale=D ** -0.5,
                                                 accum_out=stat[:, u, 0:1]).then_inc(stat_ok.handle, 1)
                            
                        def xt_copy(p, u):
                            act.wait_ge(xt_pe.handle, xt_pe.at(p + 1))
                            if v_pe.due(p - 1):
                                act.wait_ge(v_pe.handle, v_pe.at(p - 1))
                            for c in range(CH):
                                ins = nc.scalar.activation(xt[:, u, c].rearrange("p e n -> p (e n)"),
                                                           ps_t[:, 2 * c * P:2 * (c + 1) * P], ACT.Copy,
                                                           scale=w_ln[:, c:c + 1])
                            ins.then_inc(xt_ok.handle, 1)

                        def qkt_copy(p):
                            act.wait_ge(qkt_pe.handle, qkt_pe.at(p + 1))
                            if s_pe.due(p):
                                act.wait_ge(s_pe.handle, s_pe.at(p))
                            nc.scalar.activation(qkt[:].rearrange("p c n -> p (c n)"), ps_t[:], ACT.Copy) \
                                .then_inc(qkt_ok.handle, 1)

                        def step(p, u):
                            v = 1 - u
                            if has(p + 1):
                                qkt_copy(p + 1)
                            if has(p - 1):
                                prob_copies(act, pt, p - 1)
                            if has(p):
                                softmax_exp(act, probs, p, u, HD ** -0.5)
                            if has(p + 2):
                                xt_copy(p + 2, u)
                            if has(p - 1):
                                act.wait_ge(pv_pe.handle, pv_pe.at(p))
                                if d_pe.due(p - 1):
                                    act.wait_ge(d_pe.handle, d_pe.at(p - 1))
                                nc.scalar.activation(ot[:].rearrange("p c n -> p (c n)"), ps_o[:, 0:2 * P], ACT.Copy) \
                                    .then_inc(o_ok.handle, 2)
                            if has(p + 4):
                                stat_(p + 4, u)
                        for p in range(4):
                            stat_(p, p % 2)
                            if p == 1:
                                xt_copy(0, 0)
                        qkt_copy(0)
                        xt_copy(1, 1)
                        steps(act, step)

                    @block.gpsimd
                    def _(pool):
                        nc.gpsimd.memset(vb[:].rearrange("p a b j h d -> p (a b j h d)"), 0.0).then_inc(cold.handle, 1)

                        def spread(p):
                            pool.wait_ge(qkt_ok.handle, qkt_ok.at(p + 1))
                            if s_pe.due(p):
                                pool.wait_ge(s_pe.handle, s_pe.at(p))
                            for h in range(CH):
                                for b in range(2):
                                    ins = nc.gpsimd.tensor_tensor(
                                        kx[:, h, b], qkt[:, 2 + h, b * S:b * S + S].unsqueeze(1).broadcast_to([P, 8, S]),
                                        const[:, C_H16:C_H16 + 8].unsqueeze(2).broadcast_to([P, 8, S]), ALU.mult)
                            ins.then_inc(kx_ok.handle, 1)

                        def step(p, u):
                            if has(p + 1):
                                spread(p + 1)
                            if has(p):
                                softmax_norm(pool, sm, probs, p, u)
                            if has(p + 4):
                                put_rstd(pool, p + 4, u, eps6)
                        for p in range(4):
                            put_rstd(pool, p, p % 2, eps6)
                        spread(0)
                        steps(pool, step)

                    @block.vector
                    def _(dve):
                        dve.wait_ge(cold.handle, cold.at(0, 1))

                        def norm(p, u):
                            dve.wait_ge(rstd_ok.handle, rstd_ok.at(p + 1))
                            if xt_pe.due(p):
                                dve.wait_ge(xt_pe.handle, xt_pe.at(p))
                            nc.vector.tensor_scalar(mixw[:], vm[:, bass.ds(p, 1), :].rearrange("p a e -> p (a e)"),
                                                    rstd[:, u, 0:1], None, ALU.mult).then_inc(mixw_ok.handle, 1)
                            dve.wait_ge(mixw_ok.handle, mixw_ok.at(p + 1))
                            for e in range(2):
                                ins = nc.vector.tensor_scalar(xn[:, e], x_tile(p), mixw[:, e:e + 1], None, ALU.mult)
                            ins.then_inc(xn_ok.handle, 1)

                        def rope_(p):
                            dve.wait_ge(qk_pe.handle, qk_pe.at(p + 1))
                            if qkt_pe.due(p):
                                dve.wait_ge(qkt_pe.handle, qkt_pe.at(p))
                            a = ps_a[:].rearrange("p (h d) -> p h d", d=HD)
                            o = [roped[:, r].rearrange("p (h d) -> p h d", d=HD) for r in range(2)]
                            H2 = HD // 2

                            def table(c0, w):
                                return rope[:, c0:c0 + w].unsqueeze(1).broadcast_to([P, 2 * NH, w])
                            nc.vector.tensor_tensor(o[0], a, table(0, HD), ALU.mult)
                            nc.vector.tensor_tensor(o[1][:, :, 0:H2], a[:, :, H2:HD], table(HD, H2), ALU.mult)
                            nc.vector.tensor_tensor(o[1][:, :, H2:HD], a[:, :, 0:H2], table(HD + H2, H2), ALU.mult) \
                                .then_inc(rope1.handle, 1)
                            dve.wait_ge(rope1.handle, rope1.at(p + 1))
                            nc.vector.tensor_tensor(roped[:, 0], roped[:, 0], roped[:, 1], ALU.add) \
                                .then_inc(rope_ok.handle, 1)

                        def v_blocks(p, u):
                            dve.wait_ge(v_pe.handle, v_pe.at(p + 1))
                            if pv_pe.due(p - 1):
                                dve.wait_ge(pv_pe.handle, pv_pe.at(p - 1))
                            for h in range(2):
                                rows = slice(S * h, S * h + S)
                                ins = nc.vector.tensor_copy(
                                    vb[rows, u, :, :, h].rearrange("p b j d -> p (b j) d"),
                                    ps_b[rows, 0:D].rearrange("p (bj d) -> p bj d", d=HD))
                            ins.then_inc(v_ok.handle, 1)

                        def residual(p):
                            dve.wait_ge(d_pe.handle, d_pe.at(p + 1))
                            nc.vector.tensor_copy(sel[:], vm[:, bass.ds(p, 1), :].rearrange("p a e -> p (a e)")) \
                                .then_inc(sel_ok.handle, 1)
                            dve.wait_ge(sel_ok.handle, sel_ok.at(p + 1))
                            nc.vector.scalar_tensor_tensor(part[:], ps_d[:, 0:D], sel[:, 0:1], x_tile(p),
                                                           ALU.mult, ALU.add).then_inc(mix_ok.handle, 1)
                            dve.wait_ge(mix_ok.handle, mix_ok.at(p + 1))
                            nc.vector.scalar_tensor_tensor(x_tile(p), ps_d[:, D:2 * D], sel[:, 1:2], part[:],
                                                           ALU.mult, ALU.add).then_inc(res_ok.handle, 1)

                        def step(p, u):
                            v = 1 - u
                            if has(p + 1):
                                rope_(p + 1)
                            if has(p):
                                softmax_front(dve, mx, probs, p, u)
                                softmax_sum(dve, sm, probs, p, u)
                            if has(p + 3):
                                norm(p + 3, v)
                            if has(p + 1):
                                v_blocks(p + 1, v)
                            if has(p - 1):
                                residual(p - 1)
                        norm(0, 0)
                        rope_(0)
                        norm(1, 1)
                        norm(2, 0)
                        v_blocks(0, 0)
                        steps(dve, step)
                loaded.base += 80
                cold.base += 1
                close(PAIRS, stat_ok, eps_ok, rstd_ok, mixw_ok, xn_ok, xt_pe, xt_ok, qk_pe, rope1, rope_ok, qkt_pe,
                      qkt_ok, kx_ok, v_pe, v_ok, s_pe, max_ok, sub_ok, exp_ok, sum_ok, inv_ok, prob_ok, pt_pe, pt_ok,
                      pv_pe, o_ok, d_pe, sel_ok, mix_ok, res_ok)

        def cross_attention(n):
            L = f"L{n}_xattn_"
            with ExitStack() as own:
                def ob(name, shape, dt=F32):
                    return sb(f"c{n}_{name}", shape, dt, own)

                w_q = ob("w_q", [P, CH, DC])
                w_kv = ob("w_kv", [P, 2 * DC])
                w_out = ob("w_out", [P, D])
                w_ln = ob("w_ln", [P, CH])
                ctx_t = ob("ctx_t", [P, 2, DC])
                junk = ob("junk", [P, D])
                xn = ob("xn", [P, D])
                xt = ob("xt", [P, 2, 3, P])
                qkt = ob("qkt", [P, 2, 2, P])
                kx = ob("kx", [P, 2, 2, NH, S])
                vb = ob("vb", [P, 2, 2, J, 2 * HD])
                mx = ob("mx", [P, 2, NH])
                sm = ob("sm", [P, 2, 2, NH])
                probs = ob("probs", [P, 2, NH * S])
                pt = ob("pt", [P, J, P])
                ot = ob("ot", [P, P])

                with nc.Block() as block:
                    @block.sync
                    def _(sp):
                        sp.dma_start(w_q[:], t[L + "cq_w"].rearrange("(c p) n -> p c n", p=P)).then_inc(loaded.handle, 16)
                        sp.dma_start(w_kv[:], t[L + "ckv_w"]).then_inc(loaded.handle, 16)
                        sp.dma_start(w_out[:], t[L + "cdense_w"]).then_inc(loaded.handle, 16)
                        sp.dma_start(w_ln[:], t[L + "ln_post_cross_w"]).then_inc(loaded.handle, 16)

                        def step(p, u):
                            if has(p + 2):
                                if xt_pe.due(p + 1):
                                    sp.wait_ge(xt_pe.handle, xt_pe.at(p + 1))
                                sp.dma_start(ctx_t[:, u], ctx_rows(p + 2)).then_inc(ctx_in[u].handle, 16)
                        for p in (-2, -1):
                            step(p, p % 2)
                        steps(sp, step)

                    @block.tensor
                    def _(pe):
                        pe.wait_ge(loaded.handle, loaded.at(0, 64))
                        pe.wait_ge(cold.handle, cold.at(0, 1))

                        def xt_(p, u):
                            pe.wait_ge(xn_ok.handle, xn_ok.at(p + 1))
                            pe.wait_ge(ctx_in[u].handle, arrival(p, u, 1))
                            if xt_ok.due(p):
                                pe.wait_ge(xt_ok.handle, xt_ok.at(p))
                            for c in range(CH):
                                nc.tensor.transpose(ps_t[:, c * P:c * P + P], xn[:, c * P:c * P + P], ident)
                            nc.tensor.transpose(ps_t[:, CH * P:CH * P + P], ctx_t[:, u], ident).then_inc(xt_pe.handle, 1)

                        def proj_qk(p, u):
                            pe.wait_ge(xt_ok.handle, xt_ok.at(p + 1))
                            if qkt_ok.due(p):
                                pe.wait_ge(qkt_ok.handle, qkt_ok.at(p))
                            for c in range(CH):
                                nc.tensor.matmul(ps_a[:, 0:P], w_q[:, c], xt[:, u, c], start=(c == 0), stop=(c == CH - 1))
                            nc.tensor.matmul(ps_a[:, P:2 * P], w_kv[:, 0:DC], xt[:, u, CH], start=True, stop=True) \
                                .then_inc(qk_pe.handle, 1)

                        def proj_v(p, u):
                            if v_ok.due(p):
                                pe.wait_ge(v_ok.handle, v_ok.at(p))
                            w = w_kv[:, DC:2 * DC].rearrange("p (j h d) -> p j h d", h=2, d=CHD)
                            for b in range(2):
                                for h in range(2):
                                    ins = nc.tensor.matmul(ps_b[S * h:S * h + S, b * S:b * S + S],
                                                           xt[:, u, CH, b * S:b * S + S], w[:, :, h],
                                                           start=True, stop=True)
                            ins.then_inc(v_pe.handle, 1)

                        def scores(p, u):
                            if sub_ok.due(p):
                                pe.wait_ge(sub_ok.handle, sub_ok.at(p))
                            pe.wait_ge(kx_ok.handle, kx_ok.at(p + 1))
                            for h in range(2):
                                for b in range(2):
                                    ins = nc.tensor.matmul(ps_s[b * S:b * S + S, 512 * h:512 * h + 512],
                                                           qkt[:, u, 0, b * S:b * S + S],
                                                           kx[:, u, b, 8 * h:8 * h + 8].rearrange("p h k -> p (h k)"),
                                                           start=True, stop=True)
                            ins.then_inc(s_pe.handle, 1)

                        def pv(p, u):
                            pe.wait_ge(pt_ok.handle, pt_ok.at(p + 1))
                            pe.wait_ge(v_ok.handle, v_ok.at(p + 1))
                            if o_ok.due(p):
                                pe.wait_ge(o_ok.handle, o_ok.at(p))
                            for b in range(2):
                                for j in range(J):
                                    r = j // 2
                                    ins = nc.tensor.matmul(
                                        ps_o[32 * r:32 * r + 32, b * S:b * S + S], vb[:, u, b, j],
                                        pt[:, j, b * S:b * S + S], start=(j % 2 == 0), stop=(j % 2 == 1))
                            ins.then_inc(pv_pe.handle, 2)

                        def dense(p):
                            pe.wait_ge(o_ok.handle, o_ok.at(p + 1))
                            nc.tensor.matmul(ps_d[:, 0:D], ot[:], w_out[:], start=True, stop=True).then_inc(d_pe.handle, 1)

                        def step(p, u):
                            v = 1 - u
                            if has(p + 1):
                                proj_qk(p + 1, v)
                            if has(p):
                                scores(p, u)
                            if has(p - 1):
                                prob_transposes(pe, probs, p - 1, v)
                            if has(p + 2):
                                xt_(p + 2, u)
                            if has(p - 1):
                                pv(p - 1, v)
                            if has(p + 1):
                                proj_v(p + 1, v)
                            if has(p - 1):
                                dense(p - 1)
                        xt_(0, 0)
                        proj_qk(0, 0)
                        xt_(1, 1)
                        proj_v(0, 0)
                        steps(pe, step)

                    @block.scalar
                    def _(act):
                        act.wait_ge(loaded.handle, loaded.at(0, 64))

                        def stat_(p, u):
                            if eps_ok.due(p - 1):
                                act.wait_ge(eps_ok.handle, eps_ok.at(p - 1))
                            if stat_ok.due(p):
                                act.wait_ge(stat_ok.handle, stat_ok.at(p))
                            nc.scalar.activation(junk[:], x_tile(p), ACT.Square, scale=D ** -0.5,
                                                 accum_out=stat[:, u, 0:1]).then_inc(stat_ok.handle, 1)

                        def xt_copy(p, u):
                            act.wait_ge(xt_pe.handle, xt_pe.at(p + 1))
                            if v_pe.due(p - 1):
                                act.wait_ge(v_pe.handle, v_pe.at(p - 1))
                            for c in range(CH):
                                nc.scalar.activation(xt[:, u, c], ps_t[:, c * P:c * P + P], ACT.Copy, scale=w_ln[:, c:c + 1])
                            nc.scalar.activation(xt[:, u, CH], ps_t[:, CH * P:CH * P + P], ACT.Copy) \
                                .then_inc(xt_ok.handle, 1)

                        def qkt_copy(p, u):
                            act.wait_ge(qk_pe.handle, qk_pe.at(p + 1))
                            if s_pe.due(p - 1):
                                act.wait_ge(s_pe.handle, s_pe.at(p - 1))
                            nc.scalar.activation(qkt[:, u].rearrange("p c n -> p (c n)"), ps_a[:, 0:2 * P], ACT.Copy) \
                                .then_inc(qkt_ok.handle, 1)

                        def step(p, u):
                            v = 1 - u
                            if has(p + 1):
                                qkt_copy(p + 1, v)
                            if has(p - 1):
                                prob_copies(act, pt, p - 1)
                            if has(p):
                                softmax_exp(act, probs, p, u, CHD ** -0.5)
                            if has(p - 1):
                                act.wait_ge(pv_pe.handle, pv_pe.at(p))
                                if d_pe.due(p - 1):
                                    act.wait_ge(d_pe.handle, d_pe.at(p - 1))
                                nc.scalar.activation(ot[:], ps_o[:, 0:P], ACT.Copy).then_inc(o_ok.handle, 2)
                            if has(p + 2):
                                xt_copy(p + 2, u)
                            if has(p + 4):
                                stat_(p + 4, u)
                        for p in range(4):
                            stat_(p, p % 2)
                            if p == 1:
                                xt_copy(0, 0)
                            if p == 2:
                                qkt_copy(0, 0)
                                xt_copy(1, 1)
                        steps(act, step)

                    @block.gpsimd
                    def _(pool):
                        nc.gpsimd.memset(vb[:].rearrange("p a b j c -> p (a b j c)"), 0.0).then_inc(cold.handle, 1)

                        def spread(p, u):
                            pool.wait_ge(qkt_ok.handle, qkt_ok.at(p + 1))
                            if s_pe.due(p - 1):
                                pool.wait_ge(s_pe.handle, s_pe.at(p - 1))
                            for b in range(2):
                                ins = nc.gpsimd.tensor_tensor(
                                    kx[:, u, b], qkt[:, u, 1, b * S:b * S + S].unsqueeze(1).broadcast_to([P, NH, S]),
                                    const[:, C_H8:C_H8 + NH].unsqueeze(2).broadcast_to([P, NH, S]), ALU.mult)
                            ins.then_inc(kx_ok.handle, 1)

                        def step(p, u):
                            if has(p + 1):
                                spread(p + 1, 1 - u)
                            if has(p + 4):
                                put_rstd(pool, p + 4, u, eps6)
                            if has(p):
                                softmax_norm(pool, sm, probs, p, u)
                        for p in range(4):
                            put_rstd(pool, p, p % 2, eps6)
                        spread(0, 0)
                        steps(pool, step)

                    @block.vector
                    def _(dve):
                        dve.wait_ge(cold.handle, cold.at(0, 1))

                        def norm(p, u):
                            dve.wait_ge(rstd_ok.handle, rstd_ok.at(p + 1))
                            if xt_pe.due(p):
                                dve.wait_ge(xt_pe.handle, xt_pe.at(p))
                            nc.vector.tensor_scalar(xn[:], x_tile(p), rstd[:, u, 0:1], None, ALU.mult) \
                                .then_inc(xn_ok.handle, 1)

                        def v_blocks(p, u):
                            dve.wait_ge(v_pe.handle, v_pe.at(p + 1))
                            if pv_pe.due(p - 1):
                                dve.wait_ge(pv_pe.handle, pv_pe.at(p - 1))
                            for h in range(2):
                                rows = slice(S * h, S * h + S)
                                v4 = ps_b[rows, 0:2 * S].rearrange("p (r two d) -> p r two d", two=2, d=CHD)
                                to = vb[rows, u].rearrange("p b (r two) c -> p (b r) two c", two=2)
                                for j in range(2):
                                    at = 2 * CHD * j + CHD * h
                                    ins = nc.vector.tensor_copy(to[:, :, j, at:at + CHD], v4[:, :, j])
                            ins.then_inc(v_ok.handle, 1)

                        def residual(p):
                            dve.wait_ge(d_pe.handle, d_pe.at(p + 1))
                            nc.vector.tensor_tensor(x_tile(p), ps_d[:, 0:D], x_tile(p), ALU.add).then_inc(res_ok.handle, 1)

                        def step(p, u):
                            v = 1 - u
                            if has(p):
                                softmax_front(dve, mx, probs, p, u)
                                softmax_sum(dve, sm, probs, p, u)
                            if has(p + 3):
                                norm(p + 3, v)
                            if has(p + 1):
                                v_blocks(p + 1, v)
                            if has(p - 1):
                                residual(p - 1)
                        norm(0, 0)
                        norm(1, 1)
                        norm(2, 0)
                        v_blocks(0, 0)
                        steps(dve, step)
                loaded.base += 64
                cold.base += 1
                for c in ctx_in:
                    c.base += 8 * PAIRS
                close(PAIRS, stat_ok, eps_ok, rstd_ok, xn_ok, xt_pe, xt_ok, qk_pe, qkt_ok, kx_ok, v_pe, v_ok,
                      s_pe, max_ok, sub_ok, exp_ok, sum_ok, inv_ok, prob_ok, pt_pe, pt_ok, pv_pe, o_ok, d_pe, res_ok)

        def latent_attention():
            L = "L2_xattn_"
            with ExitStack() as own:
                def ob(name, shape, dt=F32):
                    return sb(f"a2_{name}", shape, dt, own)

                w_q = ob("w_q", [P, CH, INNER])
                w_kv = ob("w_kv", [P, 2 * INNER])
                w_out = ob("w_out", [P, J, D])
                ln = ob("ln", [P, 2, CH])
                gate = ob("gate", [P, 2])
                ctx_t = ob("ctx_t", [P, 2, DC])
                bn = ob("bn", [P, 2, 6])
                mv = ob("mv", [P, 2, 2])
                xn = ob("xn", [P, D])
                xt = ob("xt", [P, 2, 3, P])
                qt = ob("qt", [P, J, P])
                kx = ob("kx", [P, J, 2, 2, S])
                vb = ob("vb", [P, 2, 2, J, 2, HD2])
                mx = ob("mx", [P, 2, NH])
                sm = ob("sm", [P, 2, 2, NH])
                probs = ob("probs", [P, 2, NH * S])
                pt = ob("pt", [P, J, P])
                ot = ob("ot", [P, J, P])

                with nc.Block() as block:
                    @block.sync
                    def _(sp):
                        sp.dma_start(w_q[:], t[L + "Wq"].rearrange("(c p) n -> p c n", p=P)).then_inc(loaded.handle, 16)
                        sp.dma_start(w_kv[:], t[L + "Wkv"]).then_inc(loaded.handle, 16)
                        sp.dma_start(w_out[:], t[L + "Wo"].rearrange("(c p) n -> p c n", p=P)).then_inc(loaded.handle, 16)
                        sp.dma_start(ln[:, 0], t[L + "ln_q_g"]).then_inc(loaded.handle, 16)
                        sp.dma_start(ln[:, 1], t[L + "ln_q_b"]).then_inc(loaded.handle, 16)
                        sp.dma_start(gate[:, 0:1], t[L + "attn_gate"].rearrange("(a n) -> a n", a=1).broadcast_to([P, 1])) \
                            .then_inc(loaded.handle, 16)

                        def step(p, u):
                            if has(p + 2):
                                if xt_pe.due(p + 1):
                                    sp.wait_ge(xt_pe.handle, xt_pe.at(p + 1))
                                sp.dma_start(ctx_t[:, u], ctx_rows(p + 2)).then_inc(ctx_in[u].handle, 16)
                        for p in (-2, -1):
                            step(p, p % 2)
                        steps(sp, step)

                    @block.tensor
                    def _(pe):
                        pe.wait_ge(loaded.handle, loaded.at(0, 96))
                        pe.wait_ge(cold.handle, cold.at(0, 2))

                        def xt_(p, u):
                            pe.wait_ge(xn_ok.handle, xn_ok.at(p + 1))
                            pe.wait_ge(ctx_in[u].handle, arrival(p, u, 1))
                            if xt_ok.due(p):
                                pe.wait_ge(xt_ok.handle, xt_ok.at(p))
                            for c in range(CH):
                                nc.tensor.transpose(ps_t[:, c * P:c * P + P], xn[:, c * P:c * P + P], ident)
                            nc.tensor.transpose(ps_t[:, CH * P:CH * P + P], ctx_t[:, u], ident).then_inc(xt_pe.handle, 1)

                        def proj_q(p, u):
                            pe.wait_ge(xt_ok.handle, xt_ok.at(p + 1))
                            if v_ok.due(p):
                                pe.wait_ge(v_ok.handle, v_ok.at(p))
                            for r, bank in enumerate((ps_a, ps_b)):
                                for j in range(4):
                                    at = (4 * r + j) * P
                                    for c in range(CH):
                                        ins = nc.tensor.matmul(bank[:, j * P:j * P + P], w_q[:, c, at:at + P], xt[:, u, c],
                                                               start=(c == 0), stop=(c == CH - 1))
                                ins.then_inc(q2_pe.handle, 1)

                        def proj_k(p, u):
                            for r, bank in enumerate((ps_a, ps_b)):
                                pe.wait_ge(q2_ok.handle, q2_ok.at(p, r + 1))
                                for j in range(4):
                                    at = (4 * r + j) * P
                                    ins = nc.tensor.matmul(bank[:, j * P:j * P + P], w_kv[:, at:at + P], xt[:, u, CH],
                                                           start=True, stop=True)
                                ins.then_inc(k2_pe.handle, 1)

                        def proj_v(p, u):
                            w = w_kv[:, INNER:2 * INNER].rearrange("p (j h d) -> p j h d", h=2, d=HD2)
                            for b, bank in enumerate((ps_a, ps_b)):
                                pe.wait_ge(k2_ok.handle, k2_ok.at(p, b + 1))
                                for h in range(2):
                                    ins = nc.tensor.matmul(bank[S * h:S * h + S], xt[:, u, CH, b * S:b * S + S], w[:, :, h],
                                                           start=True, stop=True)
                                ins.then_inc(v2_pe.handle, 1)

                        def scores(p):
                            if sub_ok.due(p):
                                pe.wait_ge(sub_ok.handle, sub_ok.at(p))
                            pe.wait_ge(k2_ok.handle, k2_ok.at(p + 1))
                            for h in range(2):
                                bank = ps_s[:, 512 * h:512 * h + 512]
                                nc.tensor.matmul(bank, ident_b[:],
                                                 keymask[:, bass.ds(p, 1), :].broadcast_to([P, 8, S]),
                                                 start=True, stop=False, skip_group_check=True)
                                for b in range(2):
                                    for j in range(4):
                                        ins = nc.tensor.matmul(
                                            ps_s[b * S:b * S + S, 512 * h + P * j:512 * h + P * j + P],
                                            qt[:, 4 * h + j, b * S:b * S + S],
                                            kx[:, 4 * h + j, b].rearrange("p h k -> p (h k)"),
                                            start=False, stop=True, skip_group_check=True)
                            ins.then_inc(s_pe.handle, 1)

                        def pv(p, u):
                            pe.wait_ge(pt_ok.handle, pt_ok.at(p + 1))
                            pe.wait_ge(v_ok.handle, v_ok.at(p + 1))
                            if o_ok.due(p):
                                pe.wait_ge(o_ok.handle, o_ok.at(p))
                            for r, bank in enumerate((ps_o, ps_p)):
                                for b in range(2):
                                    for j in range(4):
                                        ins = nc.tensor.matmul(
                                            bank[:, j * P + b * S:j * P + b * S + S],
                                            vb[:, u, b, 4 * r + j].rearrange("p h d -> p (h d)"),
                                            pt[:, 4 * r + j, b * S:b * S + S], start=True, stop=True)
                                ins.then_inc(pv_pe.handle, 1)

                        def dense(p):
                            pe.wait_ge(o_ok.handle, o_ok.at(p + 1))
                            for c in range(J):
                                ins = nc.tensor.matmul(ps_d[:, 0:D], ot[:, c], w_out[:, c], start=(c == 0), stop=(c == J - 1))
                            ins.then_inc(d_pe.handle, 1)

                        def step(p, u):
                            v = 1 - u
                            if has(p):
                                scores(p)
                            if has(p + 1):
                                proj_q(p + 1, v)
                            if has(p - 1):
                                prob_transposes(pe, probs, p - 1, v)
                            if has(p + 1):
                                proj_k(p + 1, v)
                            if has(p - 1):
                                pv(p - 1, v)
                            if has(p + 1):
                                proj_v(p + 1, v)
                            if has(p + 2):
                                xt_(p + 2, u)
                            if has(p - 1):
                                dense(p - 1)
                        xt_(0, 0)
                        proj_q(0, 0)
                        proj_k(0, 0)
                        proj_v(0, 0)
                        xt_(1, 1)
                        steps(pe, step)

                    @block.scalar
                    def _(act):
                        act.wait_ge(loaded.handle, loaded.at(0, 96))
                        nc.scalar.activation(gate[:, 1:2], gate[:, 0:1], ACT.Tanh).then_inc(sel_ok.handle, 1)

                        def xt_copy(p, u):
                            act.wait_ge(xt_pe.handle, xt_pe.at(p + 1))
                            if v2_pe.due(p - 1):
                                act.wait_ge(v2_pe.handle, v2_pe.at(p - 1))
                            for c in range(CH):
                                nc.scalar.activation(xt[:, u, c], ps_t[:, c * P:c * P + P], ACT.Identity,
                                                     scale=ln[:, 0, c:c + 1], bias=ln[:, 1, c:c + 1])
                            nc.scalar.activation(xt[:, u, CH], ps_t[:, CH * P:CH * P + P], ACT.Copy) \
                                .then_inc(xt_ok.handle, 1)

                        def q_copy(p):
                            for r, bank in enumerate((ps_a, ps_b)):
                                act.wait_ge(q2_pe.handle, q2_pe.at(p, r + 1))
                                if r == 0:
                                    if s_pe.due(p):
                                        act.wait_ge(s_pe.handle, s_pe.at(p))
                                nc.scalar.activation(qt[:, 4 * r:4 * r + 4].rearrange("p j n -> p (j n)"), bank[:],
                                                     ACT.Copy).then_inc(q2_ok.handle, 1)

                        def v_blocks(p, u, b):
                            bank = (ps_a, ps_b)[b]
                            act.wait_ge(v2_pe.handle, v2_pe.at(p, b + 1))
                            if pv_pe.due(p - 1):
                                act.wait_ge(pv_pe.handle, pv_pe.at(p - 1))
                            for h in range(2):
                                rows = slice(S * h, S * h + S)
                                ins = nc.scalar.activation(vb[rows, u, b, :, h],
                                                           bank[rows].rearrange("p (j d) -> p j d", d=HD2), ACT.Copy)
                            return ins

                        def step(p, u):
                            v = 1 - u
                            if has(p + 1):
                                q_copy(p + 1)
                            if has(p - 1):
                                prob_copies(act, pt, p - 1)
                            if has(p):
                                softmax_exp(act, probs, p, u, HD2 ** -0.5)
                            if has(p - 1):
                                for r, bank in enumerate((ps_o, ps_p)):
                                    act.wait_ge(pv_pe.handle, pv_pe.at(p - 1, r + 1))
                                    if r == 0:
                                        if d_pe.due(p - 1):
                                            act.wait_ge(d_pe.handle, d_pe.at(p - 1))
                                    nc.scalar.activation(ot[:, 4 * r:4 * r + 4].rearrange("p j n -> p (j n)"), bank[:],
                                                         ACT.Copy).then_inc(o_ok.handle, 1)
                            if has(p + 1):
                                v_blocks(p + 1, v, 0).then_inc(v_half.handle, 1)
                            if has(p + 2):
                                xt_copy(p + 2, u)
                        xt_copy(0, 0)
                        q_copy(0)
                        v_blocks(0, 0, 0).then_inc(v_half.handle, 1)
                        xt_copy(1, 1)
                        steps(act, step)

                    @block.gpsimd
                    def _(pool):
                        nc.gpsimd.memset(vb[:].rearrange("p a b j h d -> p (a b j h d)"), 0.0).then_inc(cold.handle, 1)

                        def step(p, u):
                            if has(p):
                                softmax_norm(pool, sm, probs, p, u)
                            if has(p + 4):
                                put_rstd_var(pool, p + 4, u)

                        def put_rstd_var(pool, p, u):
                            pool.wait_ge(stat_ok.handle, stat_ok.at(p + 1))
                            nc.gpsimd.tensor_tensor(stat[:, u, 1:2], mv[:, u, 1:2], eps5[:, 0:1], ALU.add) \
                                .then_inc(eps_ok.handle, 1)
                            pool.wait_ge(eps_ok.handle, eps_ok.at(p + 1))
                            if xn_ok.due(p - 1):
                                pool.wait_ge(xn_ok.handle, xn_ok.at(p - 1))
                            nc.gpsimd.tensor_tensor(rstd[:, u, 0:1], stat[:, u, 1:2], half_neg[:, 0:1], ALU.pow) \
                                .then_inc(rstd_ok.handle, 1)
                        for p in range(4):
                            put_rstd_var(pool, p, p % 2)
                        steps(pool, step)

                    @block.vector
                    def _(dve):
                        nc.vector.memset(kx[:].rearrange("p j b h k -> p (j b h k)"), 0.0).then_inc(cold.handle, 1)
                        dve.wait_ge(cold.handle, cold.at(0, 2))
                        dve.wait_ge(sel_ok.handle, sel_ok.at(1))

                        def stat_(p, u):
                            if xn_ok.due(p - 1):
                                dve.wait_ge(xn_ok.handle, xn_ok.at(p - 1))
                            nc.vector.bn_stats(bn[:, u], x_tile(p)).then_inc(aggr_ok.handle, 1)
                            dve.wait_ge(aggr_ok.handle, aggr_ok.at(p + 1))
                            nc.vector.tensor_copy(gate[:, 0:1], gate[:, 1:2])
                            nc.vector.bn_aggr(mv[:, u], bn[:, u]).then_inc(stat_ok.handle, 1)

                        def norm(p, u):
                            dve.wait_ge(rstd_ok.handle, rstd_ok.at(p + 1))
                            if xt_pe.due(p):
                                dve.wait_ge(xt_pe.handle, xt_pe.at(p))
                            nc.vector.tensor_scalar(xn[:], x_tile(p), mv[:, u, 0:1], rstd[:, u, 0:1],
                                                    ALU.subtract, ALU.mult).then_inc(xn_ok.handle, 1)

                        def k_blocks(p):
                            for r, bank in enumerate((ps_a, ps_b)):
                                dve.wait_ge(k2_pe.handle, k2_pe.at(p, r + 1))
                                if r == 0:
                                    if s_pe.due(p):
                                        dve.wait_ge(s_pe.handle, s_pe.at(p))
                                for h in range(2):
                                    rows = slice(S * h, S * h + S)
                                    ins = nc.vector.tensor_copy(
                                        kx[rows, 4 * r:4 * r + 4, :, h].rearrange("p j b k -> p (j b) k"),
                                        bank[rows].rearrange("p (jb k) -> p jb k", k=S))
                                ins.then_inc(k2_ok.handle, 1)

                        def v_blocks(p, u):
                            dve.wait_ge(v2_pe.handle, v2_pe.at(p + 1))
                            if pv_pe.due(p - 1):
                                dve.wait_ge(pv_pe.handle, pv_pe.at(p - 1))
                            dve.wait_ge(v_half.handle, v_half.at(p + 1))
                            for h in range(2):
                                rows = slice(S * h, S * h + S)
                                ins = nc.vector.tensor_copy(vb[rows, u, 1, :, h],
                                                            ps_b[rows].rearrange("p (j d) -> p j d", d=HD2))
                            ins.then_inc(v_ok.handle, 1)

                        def residual(p):
                            dve.wait_ge(d_pe.handle, d_pe.at(p + 1))
                            nc.vector.scalar_tensor_tensor(x_tile(p), ps_d[:, 0:D], gate[:, 1:2], x_tile(p),
                                                           ALU.mult, ALU.add).then_inc(res_ok.handle, 1)

                        def step(p, u):
                            v = 1 - u
                            if has(p):
                                softmax_front(dve, mx, probs, p, u)
                                softmax_sum(dve, sm, probs, p, u)
                            if has(p + 1):
                                k_blocks(p + 1)
                            if has(p + 4):
                                stat_(p + 4, u)
                            if has(p + 1):
                                v_blocks(p + 1, v)
                            if has(p + 3):
                                norm(p + 3, v)
                            if has(p - 1):
                                residual(p - 1)
                        for p in range(4):
                            stat_(p, p % 2)
                            if p == 1:
                                norm(0, 0)
                            if p == 2:
                                norm(1, 1)
                        k_blocks(0)
                        v_blocks(0, 0)
                        norm(2, 0)
                        steps(dve, step)
                loaded.base += 96
                cold.base += 2
                sel_ok.base += 1
                for c in ctx_in:
                    c.base += 8 * PAIRS
                close(PAIRS, aggr_ok, stat_ok, eps_ok, rstd_ok, xn_ok, xt_pe, xt_ok, q2_pe, q2_ok, k2_pe, k2_ok, v2_pe,
                      v_half, v_ok, s_pe, max_ok, sub_ok, exp_ok, sum_ok, inv_ok, prob_ok, pt_pe, pt_ok, pv_pe, o_ok,
                      d_pe, res_ok)


        def group_steps(eng, step):
            step(0)
            with eng.Fori(1, GROUPS - 1) as g:
                step(g)
            step(GROUPS - 1)

        def has_group(g):
            return not isinstance(g, int) or g < GROUPS

        def x_rows(g, k):
            return x_res[:, bass.ds(g * (G * D) + k * D, D)]

        def vm_rows(g):
            return vm[:, bass.ds(g * G, G), :]

        def gated_feed_forward(n, store=False):
            L = f"L{n}_xattn_"
            with ExitStack() as own:
                def ob(name, shape, dt=F32):
                    return sb(f"f{n}_{name}", shape, dt, own)

                w_in = ob("w_in", [P, 2 * CH, 2, I])
                w_down = ob("w_down", [P, IC, 2, D])
                w_ln = ob("w_ln", [P, CH])
                junk = ob("junk", [P, D])
                mixw = ob("mixw", [P, G, 2])
                sel = ob("sel", [P, G, 2])
                xn = ob("xn", [P, G, 2, D])
                xt = ob("xt", [P, 2 * CH, GT])
                act_g = ob("act_g", [P, 2, GT])
                h = ob("h", [P, IC, GT])
                part = ob("part", [P, 2, D])
                rows_of = [min(P, I - P * m) for m in range(IC)]
                in_banks = [(ps_a[:], ps_b[:]), (ps_s[:, 0:512], ps_s[:, 512:1024])]
                full = I // P * P

                with nc.Block() as block:
                    @block.sync
                    def _(sp):
                        for e, x in enumerate("vl"):
                            for r, y in enumerate(("_gate", "_up")):
                                sp.dma_start(w_in[:, e * CH:e * CH + CH, r],
                                             t[L + x + y].rearrange("(c p) n -> p c n", p=P)).then_inc(loaded.handle, 16)
                            sp.dma_start(w_down[:, 0:IC - 1, e],
                                         t[L + x + "_down"][0:full, :].rearrange("(c p) n -> p c n", p=P)) \
                                .then_inc(loaded.handle, 16)
                            sp.dma_start(w_down[0:I - full, IC - 1, e], t[L + x + "_down"][full:I, :]) \
                                .then_inc(loaded.handle, 16)
                        sp.dma_start(w_ln[:], t[L + "ln_post_attn_w"]).then_inc(loaded.handle, 16)

                        def step(g):
                            sp.wait_ge(res_ok.handle, res_ok.at(g * G + G))
                            sp.dma_start(out_rows(g), x_res[:, bass.ds(g * (G * D), G * D)]
                                         .rearrange("p (n d) -> p n d", d=D)).then_inc(stored.handle, 16)
                        if store:
                            group_steps(sp, step)
                            sp.wait_ge(stored.handle, stored.at(GROUPS))

                    @block.tensor
                    def _(pe):
                        pe.wait_ge(loaded.handle, loaded.at(0, 144))

                        def gate_up(g):
                            pe.wait_ge(xt_ok.handle, xt_ok.at(g * 4 + 4))
                            for m in range(IC):
                                if h_ok.due(g * IC + (m - 1)):
                                    pe.wait_ge(h_ok.handle, h_ok.at(g * IC + (m - 1)))
                                for r in range(2):
                                    for k in range(2 * CH):
                                        ins = nc.tensor.matmul(in_banks[m % 2][r][0:rows_of[m]],
                                                               w_in[:, k, r, m * P:m * P + rows_of[m]], xt[:, k],
                                                               start=(k == 0), stop=(k == 2 * CH - 1))
                                ins.then_inc(g_pe.handle, 1)

                        def xt_(g):
                            pe.wait_ge(xn_ok.handle, xn_ok.at(g * G + G))
                            for k in range(2 * CH):
                                e, c = divmod(k, CH)
                                bank = (ps_t, ps_p)[k % 2]
                                if xt_ok.due(g * 4 + (k - 1)):
                                    pe.wait_ge(xt_ok.handle, xt_ok.at(g * 4 + (k - 1)))
                                for i in range(G):
                                    ins = nc.tensor.transpose(bank[:, i * P:i * P + P], xn[:, i, e, c * P:c * P + P], ident)
                                ins.then_inc(xt_pe.handle, 1)

                        def down(g):
                            pe.wait_ge(h_ok.handle, h_ok.at(g * IC + IC))
                            for i in range(G):
                                if res_ok.due(g * G + (i - 1)):
                                    pe.wait_ge(res_ok.handle, res_ok.at(g * G + (i - 1)))
                                for m in range(IC):
                                    ins = nc.tensor.matmul((ps_o, ps_d)[i % 2][:], h[0:rows_of[m], m, i * P:i * P + P],
                                                           w_down[0:rows_of[m], m].rearrange("p e n -> p (e n)"),
                                                           start=(m == 0), stop=(m == IC - 1))
                                ins.then_inc(d_pe.handle, 1)

                        def step(g):
                            gate_up(g)
                            if has_group(g + 1):
                                xt_(g + 1)
                            down(g)
                        xt_(0)
                        group_steps(pe, step)

                    @block.scalar
                    def _(act):
                        act.wait_ge(loaded.handle, loaded.at(0, 144))

                        def stats(g):
                            if eps_ok.due(g):
                                act.wait_ge(eps_ok.handle, eps_ok.at(g))
                            for k in range(G):
                                if stat_ok.due(g * G + k):
                                    act.wait_ge(stat_ok.handle, stat_ok.at(g * G + k))
                                nc.scalar.activation(junk[:], x_rows(g, k), ACT.Square, scale=D ** -0.5,
                                                     accum_out=stat[:, 0, k:k + 1]).then_inc(stat_ok.handle, 1)

                        def xt_copy(g):
                            if g_pe.due(g * IC):
                                act.wait_ge(g_pe.handle, g_pe.at(g * IC))
                            for k in range(2 * CH):
                                act.wait_ge(xt_pe.handle, xt_pe.at(g * 4 + (k + 1)))
                                nc.scalar.activation(xt[:, k], (ps_t, ps_p)[k % 2][:], ACT.Copy,
                                                     scale=w_ln[:, k % CH:k % CH + 1]).then_inc(xt_ok.handle, 1)

                        def step(g):
                            for m in range(IC):
                                act.wait_ge(g_pe.handle, g_pe.at(g * IC + (m + 1)))
                                if h_ok.due(g * IC + (m - 1)):
                                    act.wait_ge(h_ok.handle, h_ok.at(g * IC + (m - 1)))
                                nc.scalar.activation(act_g[0:rows_of[m], m % 2], in_banks[m % 2][0][0:rows_of[m]],
                                                     ACT.Silu).then_inc(a_ok.handle, 1)
                                if m == 1 and has_group(g + 1):
                                    stats(g + 1)
                            if has_group(g + 1):
                                xt_copy(g + 1)
                        stats(0)
                        xt_copy(0)
                        group_steps(act, step)

                    @block.gpsimd
                    def _(pool):
                        def rstd_(g):
                            pool.wait_ge(stat_ok.handle, stat_ok.at(g * G + G))
                            nc.gpsimd.tensor_tensor(stat[:, 1], stat[:, 0], eps6[:], ALU.add).then_inc(eps_ok.handle, 1)
                            pool.wait_ge(eps_ok.handle, eps_ok.at(g + 1))
                            if mixw_ok.due(g):
                                pool.wait_ge(mixw_ok.handle, mixw_ok.at(g))
                            nc.gpsimd.tensor_tensor(rstd[:, 0], stat[:, 1], half_neg[:], ALU.pow).then_inc(rstd_ok.handle, 1)

                        def step(g):
                            if has_group(g + 1):
                                rstd_(g + 1)
                        rstd_(0)
                        group_steps(pool, step)

                    @block.vector
                    def _(dve):
                        def norm(g):
                            dve.wait_ge(rstd_ok.handle, rstd_ok.at(g + 1))
                            nc.vector.tensor_tensor(mixw[:], vm_rows(g), rstd[:, 0].unsqueeze(2).broadcast_to([P, G, 2]),
                                                    ALU.mult).then_inc(mixw_ok.handle, 1)
                            dve.wait_ge(mixw_ok.handle, mixw_ok.at(g + 1))
                            if xt_pe.due(g * 4):
                                dve.wait_ge(xt_pe.handle, xt_pe.at(g * 4))
                            for k in range(G):
                                for e in range(2):
                                    ins = nc.vector.tensor_scalar(xn[:, k, e], x_rows(g, k), mixw[:, k, e:e + 1], None,
                                                                  ALU.mult)
                                ins.then_inc(xn_ok.handle, 1)

                        def step(g):
                            for m in range(IC):
                                dve.wait_ge(a_ok.handle, a_ok.at(g * IC + (m + 1)))
                                if d_pe.due(g * G):
                                    dve.wait_ge(d_pe.handle, d_pe.at(g * G))
                                nc.vector.tensor_tensor(h[0:rows_of[m], m], in_banks[m % 2][1][0:rows_of[m]],
                                                        act_g[0:rows_of[m], m % 2], ALU.mult).then_inc(h_ok.handle, 1)
                                if m == 3 and has_group(g + 1):
                                    norm(g + 1)
                            if res_ok.due(g * G):
                                dve.wait_ge(res_ok.handle, res_ok.at(g * G))
                            nc.vector.tensor_copy(sel[:], vm_rows(g)).then_inc(sel_ok.handle, 1)
                            dve.wait_ge(sel_ok.handle, sel_ok.at(g + 1))
                            for k in range(G):
                                bank = (ps_o, ps_d)[k % 2]
                                dve.wait_ge(d_pe.handle, d_pe.at(g * G + (k + 1)))
                                nc.vector.scalar_tensor_tensor(part[:, k % 2], bank[:, 0:D], sel[:, k, 0:1], x_rows(g, k),
                                                               ALU.mult, ALU.add).then_inc(mix_ok.handle, 1)
                                dve.wait_ge(mix_ok.handle, mix_ok.at(g * G + (k + 1)))
                                nc.vector.scalar_tensor_tensor(x_rows(g, k), bank[:, D:2 * D], sel[:, k, 1:2],
                                                               part[:, k % 2], ALU.mult, ALU.add).then_inc(res_ok.handle, 1)
                        norm(0)
                        group_steps(dve, step)
                loaded.base += 144
                close(GROUPS, eps_ok, rstd_ok, mixw_ok, sel_ok)
                close(GROUPS * G, stat_ok, xn_ok, d_pe, mix_ok, res_ok)
                close(GROUPS * 2 * CH, xt_pe, xt_ok)
                close(GROUPS * IC, g_pe, a_ok, h_ok)
                if store:
                    close(GROUPS, stored)

        def gelu_feed_forward():
            L = "L2_xattn_"
            M = FF // P
            with ExitStack() as own:
                def ob(name, shape, dt=F32):
                    return sb(f"f2_{name}", shape, dt, own)

                w_in = ob("w_in", [P, CH, FF])
                w_out = ob("w_out", [P, M, D])
                ln = ob("ln", [P, 2, CH])
                gate = ob("gate", [P, 2])
                bn = ob("bn", [P, G, 6])
                mv = ob("mv", [P, G, 2])
                xn = ob("xn", [P, G, D])
                xt = ob("xt", [P, CH, GT])
                h = ob("h", [P, M, GT])
                in_banks = [ps_a[:], ps_b[:], ps_s[:, 0:512], ps_s[:, 512:1024]]

                with nc.Block() as block:
                    @block.sync
                    def _(sp):
                        sp.dma_start(w_in[:], t[L + "W1"].rearrange("(c p) n -> p c n", p=P)).then_inc(loaded.handle, 16)
                        sp.dma_start(w_out[:], t[L + "W2"].rearrange("(c p) n -> p c n", p=P)).then_inc(loaded.handle, 16)
                        sp.dma_start(ln[:, 0], t[L + "ln_ff_g"]).then_inc(loaded.handle, 16)
                        sp.dma_start(ln[:, 1], t[L + "ln_ff_b"]).then_inc(loaded.handle, 16)
                        sp.dma_start(gate[:, 0:1], t[L + "ff_gate"].rearrange("(a n) -> a n", a=1).broadcast_to([P, 1])) \
                            .then_inc(loaded.handle, 16)

                    @block.tensor
                    def _(pe):
                        pe.wait_ge(loaded.handle, loaded.at(0, 80))

                        def up(g):
                            pe.wait_ge(xt_ok.handle, xt_ok.at(g * CH + CH))
                            for m in range(M):
                                if h_ok.due(g * M + (m - 3)):
                                    pe.wait_ge(h_ok.handle, h_ok.at(g * M + (m - 3)))
                                for c in range(CH):
                                    ins = nc.tensor.matmul(in_banks[m % 4], w_in[:, c, m * P:m * P + P], xt[:, c],
                                                           start=(c == 0), stop=(c == CH - 1))
                                ins.then_inc(g_pe.handle, 1)

                        def xt_(g):
                            pe.wait_ge(xn_ok.handle, xn_ok.at(g * G + G))
                            for c in range(CH):
                                bank = (ps_t, ps_p)[c % 2]
                                if xt_ok.due(g * CH + (c - 1)):
                                    pe.wait_ge(xt_ok.handle, xt_ok.at(g * CH + (c - 1)))
                                for i in range(G):
                                    ins = nc.tensor.transpose(bank[:, i * P:i * P + P], xn[:, i, c * P:c * P + P], ident)
                                ins.then_inc(xt_pe.handle, 1)

                        def down(g):
                            pe.wait_ge(h_ok.handle, h_ok.at(g * M + M))
                            for i in range(G):
                                if res_ok.due(g * G + (i - 1)):
                                    pe.wait_ge(res_ok.handle, res_ok.at(g * G + (i - 1)))
                                for m in range(M):
                                    ins = nc.tensor.matmul((ps_o, ps_d)[i % 2][:, 0:D], h[:, m, i * P:i * P + P],
                                                           w_out[:, m], start=(m == 0), stop=(m == M - 1))
                                ins.then_inc(d_pe.handle, 1)

                        def step(g):
                            up(g)
                            if has_group(g + 1):
                                xt_(g + 1)
                            down(g)
                        xt_(0)
                        group_steps(pe, step)

                    @block.scalar
                    def _(act):
                        act.wait_ge(loaded.handle, loaded.at(0, 80))
                        nc.scalar.activation(gate[:, 1:2], gate[:, 0:1], ACT.Tanh).then_inc(sel_ok.handle, 1)

                        def xt_copy(g):
                            if g_pe.due(g * M):
                                act.wait_ge(g_pe.handle, g_pe.at(g * M))
                            for c in range(CH):
                                act.wait_ge(xt_pe.handle, xt_pe.at(g * CH + (c + 1)))
                                nc.scalar.activation(xt[:, c], (ps_t, ps_p)[c % 2][:], ACT.Identity,
                                                     scale=ln[:, 0, c:c + 1], bias=ln[:, 1, c:c + 1]) \
                                    .then_inc(xt_ok.handle, 1)

                        def step(g):
                            for m in range(M):
                                act.wait_ge(g_pe.handle, g_pe.at(g * M + (m + 1)))
                                if d_pe.due(g * G):
                                    act.wait_ge(d_pe.handle, d_pe.at(g * G))
                                nc.scalar.activation(h[:, m], in_banks[m % 4], ACT.Gelu).then_inc(h_ok.handle, 1)
                            if has_group(g + 1):
                                xt_copy(g + 1)
                        xt_copy(0)
                        group_steps(act, step)

                    @block.gpsimd
                    def _(pool):
                        def rstd_(g):
                            pool.wait_ge(stat_ok.handle, stat_ok.at(g * G + G))
                            nc.gpsimd.tensor_tensor(stat[:, 1], mv[:, :, 1], eps5[:], ALU.add).then_inc(eps_ok.handle, 1)
                            pool.wait_ge(eps_ok.handle, eps_ok.at(g + 1))
                            if xn_ok.due(g * G):
                                pool.wait_ge(xn_ok.handle, xn_ok.at(g * G))
                            nc.gpsimd.tensor_tensor(rstd[:, 0], stat[:, 1], half_neg[:], ALU.pow).then_inc(rstd_ok.handle, 1)

                        def step(g):
                            if has_group(g + 1):
                                rstd_(g + 1)
                        rstd_(0)
                        group_steps(pool, step)

                    @block.vector
                    def _(dve):
                        dve.wait_ge(sel_ok.handle, sel_ok.at(1))

                        def stats(g):
                            if xn_ok.due(g * G):
                                dve.wait_ge(xn_ok.handle, xn_ok.at(g * G))
                            for k in range(G):
                                nc.vector.bn_stats(bn[:, k], x_rows(g, k)).then_inc(aggr_ok.handle, 1)
                            dve.wait_ge(aggr_ok.handle, aggr_ok.at(g * G + G))
                            nc.vector.tensor_copy(gate[:, 0:1], gate[:, 1:2])
                            for k in range(G):
                                nc.vector.bn_aggr(mv[:, k], bn[:, k]).then_inc(stat_ok.handle, 1)

                        def norm(g):
                            dve.wait_ge(rstd_ok.handle, rstd_ok.at(g + 1))
                            if xt_pe.due(g * CH):
                                dve.wait_ge(xt_pe.handle, xt_pe.at(g * CH))
                            for k in range(G):
                                nc.vector.tensor_scalar(xn[:, k], x_rows(g, k), mv[:, k, 0:1], rstd[:, 0, k:k + 1],
                                                        ALU.subtract, ALU.mult).then_inc(xn_ok.handle, 1)

                        def step(g):
                            if has_group(g + 1):
                                stats(g + 1)
                                norm(g + 1)
                            for k in range(G):
                                dve.wait_ge(d_pe.handle, d_pe.at(g * G + (k + 1)))
                                nc.vector.scalar_tensor_tensor(x_rows(g, k), (ps_o, ps_d)[k % 2][:, 0:D], gate[:, 1:2],
                                                               x_rows(g, k), ALU.mult, ALU.add).then_inc(res_ok.handle, 1)
                        stats(0)
                        norm(0)
                        group_steps(dve, step)
                loaded.base += 80
                close(GROUPS, eps_ok, rstd_ok)
                close(1, sel_ok)
                close(GROUPS * G, stat_ok, aggr_ok, xn_ok, d_pe, res_ok)
                close(GROUPS * CH, xt_pe, xt_ok)
                close(GROUPS * M, g_pe, h_ok)

        def out_rows(g):
            return t["out"].rearrange("(n two) s d -> (two s) n d", two=2)[:, bass.ds(g * G, G), :]

        phases = [layer0, lambda: self_attention(1), lambda: cross_attention(1), lambda: gated_feed_forward(1),
                  latent_attention, gelu_feed_forward,
                  lambda: self_attention(3), lambda: cross_attention(3), lambda: gated_feed_forward(3, store=True)]
        for phase in phases:
            phase()


_WEIGHTS = {
    0: ["b_gate", "norm_w"],
    1: ["ln_in_w", "ln_post_attn_w", "ln_post_cross_w", "v_qkv", "l_qkv", "v_dense", "l_dense", "cq_w", "ckv_w",
        "cdense_w", "v_gate", "v_up", "v_down", "l_gate", "l_up", "l_down"],
    2: ["ln_q_g", "ln_q_b", "Wq", "Wkv", "Wo", "attn_gate", "ln_ff_g", "ln_ff_b", "W1", "W2", "ff_gate"],
}
_WEIGHTS[3] = _WEIGHTS[1]


def kernel(**inputs):
    import concourse.bacc as bacc
    from concourse.bass_utils import run_bass_kernel_spmd

    host = {n: np.asarray(inputs[n]) for n in ("x", "ctx_1024", "pos_1xS", "mask_BxS_ik0")}
    host["mask_BxS2_bk0"] = np.asarray(inputs["mask_BxS2_bk0"])
    host["W_mem_T"] = np.asarray(inputs["L0_xattn_W_mem"]).T
    host["W_gate_T"] = np.asarray(inputs["L0_xattn_W_gate"]).T
    for n, names in _WEIGHTS.items():
        for w in names:
            a = np.asarray(inputs[f"L{n}_xattn_{w}"])
            host[f"L{n}_xattn_{w}"] = a.reshape(CH, P).T if w.startswith("ln_") else a
    host["consts"] = constants()

    nc = bacc.Bacc("TRN2", target_bir_lowering=False, num_devices=1)
    arrays, t = {}, {}
    for name, a in host.items():
        arrays[f"in_{name}"] = np.ascontiguousarray(a)
        t[name] = nc.dram_tensor(f"in_{name}", a.shape, mybir.dt.from_np(a.dtype), kind="ExternalInput").ap()
    t["out"] = nc.dram_tensor("out", (B, S, D), F32, kind="ExternalOutput").ap()
    build(nc, t)
    r = run_bass_kernel_spmd(nc, [arrays], core_ids=[0])
    return r.results[0]["out"]
```

```python
import numpy as np
import concourse.bass as bass
from concourse import mybir
from contextlib import ExitStack

F32 = mybir.dt.float32
F32R = mybir.dt.float32r
BF16 = mybir.dt.bfloat16
I32 = mybir.dt.int32
U8 = mybir.dt.uint8
ALU = mybir.AluOpType
ACT = mybir.ActivationFunctionType
AX = mybir.AxisListType

P = 128
B, S, D = 64, 64, 256
DC = 128
PAIRS = B // 2
CH = D // P
NH = 16
HD = D // NH
CHD = DC // NH
HD2 = 64
INNER = NH * HD2
J = NH // 2
I = 688
IC = -(-I // P)
FF = 4 * D
G = 4
GROUPS = PAIRS // G
GT = G * P
MASKED = -1.0e38
FIRST, LAST = 3, 26

C_IDENT, C_H16, C_H8, C_CAUSAL, C_BLOCK, C_ROPE, C_IOTA = 0, 128, 136, 152, 216, 344, 376
C_ALL = 377


def constants():
    c = np.zeros((P, C_ALL), np.float32)
    r = np.arange(P)
    c[:, C_IDENT:C_IDENT + P] = np.eye(P)
    c[:, C_H16:C_H16 + 8] = (r[:, None] // HD) == np.arange(8)
    c[:, C_H8:C_H8 + 16] = (r[:, None] // CHD) == np.arange(16)
    c[:, C_CAUSAL:C_CAUSAL + S] = np.where(np.arange(S) > (r % S)[:, None], np.float32(MASKED), 0)
    c[:, C_BLOCK:C_BLOCK + P] = np.where(r[:, None] // S != r[None] // S, np.float32(MASKED), 0)
    inv = np.float32(1) / np.float32(10000) ** (np.arange(0, HD, 2, dtype=np.float32) / np.float32(HD))
    f = np.outer(np.arange(S, dtype=np.float32), inv).astype(np.float32)
    c[:S, C_ROPE:C_ROPE + HD] = np.concatenate([np.cos(f), np.cos(f)], 1)
    c[:S, C_ROPE + HD:C_ROPE + 2 * HD] = np.concatenate([-np.sin(f), np.sin(f)], 1)
    c[:, C_IOTA] = r
    return c


class Count:

    def __init__(self, handle, per=1):
        self.handle, self.per, self.base = handle, per, 0

    def at(self, units, extra=0):
        return units * self.per + (self.base + extra)

    def due(self, units, extra=0):
        return not isinstance(units, int) or units * self.per + extra > 0

    def close(self, units):
        self.base += self.per * units


def build(nc, t):
    with ExitStack() as ctx:
        def sb(name, shape, dt=F32, where=None):
            return (where or ctx).enter_context(nc.sbuf_tensor(name, shape, dt))

        def ps(name, cols=512):
            return ctx.enter_context(nc.psum_tensor(name, [P, cols], F32))

        def count(name, per=1):
            return Count(ctx.enter_context(nc.semaphore(name)), per)

        x_res = sb("x_res", [P, PAIRS * D])
        const = sb("const", [P, C_ALL])
        ident_b = sb("ident_b", [P, P], BF16)
        causal_b = sb("causal_b", [P, S], BF16)
        block_b = sb("block_b", [P, P], BF16)
        keymask = sb("keymask", [P, PAIRS, S], BF16)
        rope = sb("rope", [P, 2 * HD])
        vm = sb("vm", [P, PAIRS, 2])
        half_neg = sb("half_neg", [P, G])
        eps6 = sb("eps6", [P, G])
        eps5 = sb("eps5", [P, G])
        stat = sb("stat", [P, 2, G])
        rstd = sb("rstd", [P, 2, G])
        km_raw = sb("km_raw", [P, PAIRS, S], U8)
        ident = const[:, C_IDENT:C_IDENT + P]

        pool_w = sb("pool_w", [P, 10 * 1024])

        def view(buf, at, *shape):
            v = buf[:, at:at + int(np.prod(shape))]
            names = "abc"[:len(shape)]
            return v if len(shape) == 1 else v.rearrange(f"p ({' '.join(names)}) -> p {' '.join(names)}",
                                                         **dict(zip(names[1:], shape[1:])))
        w_l0 = (view(pool_w, 0, D), view(pool_w, D, 2 * CH, D), view(pool_w, D + 2 * CH * D, D), view(pool_w, 2 * D + 2 * CH * D, D))
        self_w = sb("self_w", [P, 2 * CH * 3 * D + CH * 2 * D])
        w_self = (view(self_w, 0, 2 * CH, 3 * D), view(self_w, 2 * CH * 3 * D, CH, 2, D), sb("s_w_ln", [P, CH]))
        w_cross = (sb("c_w_q", [P, CH, DC]), sb("c_w_kv", [P, 2 * DC]), sb("c_w_out", [P, D]), sb("c_w_ln", [P, CH]))
        w_gated = (view(pool_w, 0, 2 * CH, 2, I), view(pool_w, 3 * CH * INNER, IC, 2, D), sb("f_w_ln", [P, CH]))
        w_latent = (view(pool_w, 0, CH, INNER), view(pool_w, CH * INNER, 2 * INNER), view(pool_w, 2 * CH * INNER, J, D),
                    sb("a2_ln", [P, 2, CH]), sb("a2_gate", [P, 2]))
        w_gelu = (view(pool_w, 3 * CH * INNER, CH, FF), view(pool_w, 3 * CH * INNER + CH * FF, FF // P, D), sb("f2_ln", [P, 2, CH]),
                  sb("f2_gate", [P, 2]))

        ps_t = ps("ps_t")
        ps_a = ps("ps_a")
        ps_b = ps("ps_b")
        ps_s = ps("ps_s", 1024)
        ps_p = ps("ps_p")
        ps_o = ps("ps_o")
        ps_d = ps("ps_d")

        shapes_in = count("shapes_in", 16)
        keymask_in = count("keymask_in", 16)
        weights_in = [count(f"weights_in{u}", 16) for u in range(2)]
        ctx_in = [count(f"ctx_in{u}", 16) for u in range(2)]
        stored = count("stored", 16)
        cold = count("cold")
        stat_ok = count("stat_ok")
        aggr_ok = count("aggr_ok")
        eps_ok = count("eps_ok")
        rstd_ok = count("rstd_ok")
        mixw_ok = count("mixw_ok")
        xn_ok = count("xn_ok")
        xt_pe = count("xt_pe")
        xt_ok = count("xt_ok")
        qk_pe = count("qk_pe")
        rope1 = count("rope1")
        rope_ok = count("rope_ok")
        qkt_pe = count("qkt_pe")
        qkt_ok = count("qkt_ok")
        kx_ok = count("kx_ok")
        v_pe = count("v_pe")
        v_ok = count("v_ok")
        s_pe = count("s_pe", 2)
        max_ok = count("max_ok", 2)
        sub_ok = count("sub_ok", 2)
        exp_ok = count("exp_ok", 2)
        sum_ok = count("sum_ok", 2)
        inv_ok = count("inv_ok")
        prob_ok = count("prob_ok")
        pt_pe = count("pt_pe", 2)
        pt_ok = count("pt_ok", 2)
        pv_pe = count("pv_pe", 2)
        o_ok = count("o_ok", 2)
        d_pe = count("d_pe")
        sel_ok = count("sel_ok")
        q2_pe, q2_ok, k2_pe, k2_ok, v2_pe = (
            count(name, 2) for name in ("q2_pe", "q2_ok", "k2_pe", "k2_ok", "v2_pe"))
        v_half = count("v_half")
        g_pe = count("g_pe")
        affine_ok = count("affine_ok")
        xlow_ok = count("xlow_ok")
        whigh_ok = count("whigh_ok")
        xhigh_ok = count("xhigh_ok")
        wlow_ok = count("wlow_ok")
        wpad_ok = count("wpad_ok")
        prod_ok = count("prod_ok")
        hhigh_ok = count("hhigh_ok")
        a_ok = count("a_ok")
        h_ok = count("h_ok")
        mix_ok = count("mix_ok")
        res_ok = count("res_ok")
        def arrival(p, u, dmas):
            return (p + (2 - u)) * (8 * dmas) + ctx_in[u].base

        def close(units, *used):
            for c in used:
                c.close(units)

        def x_tile(p):
            return x_res[:, bass.ds(p * D, D)]

        def steps(eng, step):
            for p in range(FIRST):
                step(p, p % 2)
            with eng.Fori(0, (LAST - FIRST + 1) // 2) as i:
                for u in range(2):
                    step(2 * i + (FIRST + u), (FIRST + u) % 2)
            for p in range(LAST + 1, PAIRS + 1):
                step(p, p % 2)

        def has(p):
            return not isinstance(p, int) or 0 <= p < PAIRS

        def load_l0(eng, sem):
            w_mem, w_gate, bias, w_norm = w_l0
            eng.dma_start(w_mem[:], t["W_mem_T"]).then_inc(sem, 16)
            eng.dma_start(w_gate[:], t["W_gate_T"].rearrange("(c p) n -> p c n", p=P)).then_inc(sem, 16)
            eng.dma_start(bias[:], t["L0_xattn_b_gate"].rearrange("(a n) -> a n", a=1).broadcast_to([P, D])) \
                .then_inc(sem, 16)
            eng.dma_start(w_norm[:], t["L0_xattn_norm_w"].rearrange("(a n) -> a n", a=1).broadcast_to([P, D])) \
                .then_inc(sem, 16)

        def load_self(eng, sem, n):
            w_qkv, w_out, w_ln = w_self
            for e, x in enumerate("vl"):
                eng.dma_start(w_qkv[:, e * CH:e * CH + CH],
                              t[f"L{n}_xattn_{x}_qkv"].rearrange("(c p) n -> p c n", p=P)).then_inc(sem, 16)
                eng.dma_start(w_out[:, :, e], t[f"L{n}_xattn_{x}_dense"].rearrange("(c p) n -> p c n", p=P)) \
                    .then_inc(sem, 16)
            eng.dma_start(w_ln[:], t[f"L{n}_xattn_ln_in_w"]).then_inc(sem, 16)

        def load_cross(eng, sem, n):
            w_q, w_kv, w_out, w_ln = w_cross
            eng.dma_start(w_q[:], t[f"L{n}_xattn_cq_w"].rearrange("(c p) n -> p c n", p=P)).then_inc(sem, 16)
            eng.dma_start(w_kv[:], t[f"L{n}_xattn_ckv_w"]).then_inc(sem, 16)
            eng.dma_start(w_out[:], t[f"L{n}_xattn_cdense_w"]).then_inc(sem, 16)
            eng.dma_start(w_ln[:], t[f"L{n}_xattn_ln_post_cross_w"]).then_inc(sem, 16)

        def load_gated(eng, sem, n):
            w_in, w_down, w_ln = w_gated
            full = I // P * P
            for e, x in enumerate("vl"):
                for r, y in enumerate(("gate", "up")):
                    eng.dma_start(w_in[:, e * CH:e * CH + CH, r],
                                  t[f"L{n}_xattn_{x}_{y}"].rearrange("(c p) n -> p c n", p=P)).then_inc(sem, 16)
                down = t[f"L{n}_xattn_{x}_down"]
                eng.dma_start(w_down[:, 0:IC - 1, e], down[0:full, :].rearrange("(c p) n -> p c n", p=P)) \
                    .then_inc(sem, 16)
                eng.dma_start(w_down[0:I - full, IC - 1, e], down[full:I, :]).then_inc(sem, 16)
            eng.dma_start(w_ln[:], t[f"L{n}_xattn_ln_post_attn_w"]).then_inc(sem, 16)

        def load_latent(eng, sem):
            w_q, w_kv, w_out, ln, gate = w_latent
            eng.dma_start(w_q[:], t["L2_xattn_Wq"].rearrange("(c p) n -> p c n", p=P)).then_inc(sem, 16)
            eng.dma_start(w_kv[:], t["L2_xattn_Wkv"]).then_inc(sem, 16)
            eng.dma_start(w_out[:], t["L2_xattn_Wo"].rearrange("(c p) n -> p c n", p=P)).then_inc(sem, 16)
            eng.dma_start(ln[:, 0], t["L2_xattn_ln_q_g"]).then_inc(sem, 16)
            eng.dma_start(ln[:, 1], t["L2_xattn_ln_q_b"]).then_inc(sem, 16)
            eng.dma_start(gate[:, 0:1], t["L2_xattn_attn_gate"].rearrange("(a n) -> a n", a=1).broadcast_to([P, 1])) \
                .then_inc(sem, 16)

        def load_gelu(eng, sem):
            w_in, w_out, ln, gate = w_gelu
            eng.dma_start(w_in[:], t["L2_xattn_W1"].rearrange("(c p) n -> p c n", p=P)).then_inc(sem, 16)
            eng.dma_start(w_out[:], t["L2_xattn_W2"].rearrange("(c p) n -> p c n", p=P)).then_inc(sem, 16)
            eng.dma_start(ln[:, 0], t["L2_xattn_ln_ff_g"]).then_inc(sem, 16)
            eng.dma_start(ln[:, 1], t["L2_xattn_ln_ff_b"]).then_inc(sem, 16)
            eng.dma_start(gate[:, 0:1], t["L2_xattn_ff_gate"].rearrange("(a n) -> a n", a=1).broadcast_to([P, 1])) \
                .then_inc(sem, 16)

        with ExitStack() as own:
            m_raw = sb("m_raw", [B, S], I32, own)
            m_one = sb("m_one", [B, S], F32, own)
            vm_bs = sb("vm_bs", [B, 2, S], F32, own)
            pos_raw = sb("pos_raw", [S, S], I32, own)
            pos = sb("pos", [S, 2, S], F32, own)
            onehot = sb("onehot", [S, 2, S], F32, own)
            with nc.Block() as block:
                @block.sync
                def _(sp):
                    sp.dma_start(const[:], t["consts"]).then_inc(shapes_in.handle, 16)
                    sp.dma_start(m_raw[:], t["mask_BxS_ik0"]).then_inc(shapes_in.handle, 16)
                    sp.dma_start(pos_raw[:], t["pos_1xS"].broadcast_to([S, S])).then_inc(shapes_in.handle, 16)

                @block.scalar
                def _(act):
                    load_l0(act, weights_in[0].handle)

                @block.gpsimd
                def _(pool):
                    nc.gpsimd.memset(eps6[:], 1e-6)
                    nc.gpsimd.memset(eps5[:], 1e-5)
                    nc.gpsimd.memset(half_neg[:], -0.5).then_inc(cold.handle, 1)

                @block.vector
                def _(dve):
                    dve.wait_ge(shapes_in.handle, 48)
                    nc.vector.tensor_copy(ident_b[:], ident)
                    nc.vector.tensor_copy(causal_b[:], const[:, C_CAUSAL:C_CAUSAL + S])
                    nc.vector.tensor_copy(block_b[:], const[:, C_BLOCK:C_BLOCK + P])
                    nc.vector.tensor_scalar(m_one[:], m_raw[:], 1.0, None, ALU.is_equal).then_inc(aggr_ok.handle, 1)
                    nc.vector.memset(vm_bs[:], 0.0).then_inc(sub_ok.handle, 1)
                    dve.wait_ge(aggr_ok.handle, 1)
                    dve.wait_ge(sub_ok.handle, 1)
                    for r in range(2):
                        nc.vector.tensor_tensor(vm_bs[:, r, 0:S - 1], m_one[:, 0:S - 1], m_one[:, 1:S], ALU.mult) \
                            .then_inc(sel_ok.handle, 1)
                    nc.vector.tensor_copy(pos[:, 0], pos_raw[:]).then_inc(rope1.handle, 1)
                    dve.wait_ge(rope1.handle, 1)
                    nc.vector.tensor_scalar(pos[:, 1], pos[:, 0], 0.0, float(S), ALU.is_lt, ALU.mult) \
                        .then_inc(rope1.handle, 1)
                    dve.wait_ge(rope1.handle, 2)
                    nc.vector.tensor_tensor(pos[:, 0], pos[:, 0], pos[:, 1], ALU.add).then_inc(rope1.handle, 1)
                    dve.wait_ge(rope1.handle, 3)
                    nc.vector.tensor_scalar(pos[:, 1], pos[:, 0], 0.0, float(S - 1), ALU.max, ALU.min) \
                        .then_inc(rope1.handle, 1)
                    dve.wait_ge(rope1.handle, 4)
                    for r in range(2):
                        nc.vector.tensor_scalar(onehot[:, r], pos[:, 1], const[0:S, C_IOTA:C_IOTA + 1], None,
                                                ALU.is_equal).then_inc(sel_ok.handle, 1)
                    nc.vector.memset(stat[:], 1.0).then_inc(cold.handle, 1)
                    dve.wait_ge(xt_pe.handle, 1)
                    nc.vector.tensor_copy(rope[:], ps_a[:, 0:2 * HD]).then_inc(cold.handle, 1)
                    for u in range(2):
                        nc.vector.tensor_copy(
                            vm[S * u:S * u + S, :, 0],
                            ps_t[S * u:S * u + S, 0:B].rearrange("p (n two) -> p n two", two=2)[:, :, u]) \
                            .then_inc(mix_ok.handle, 1)
                    dve.wait_ge(mix_ok.handle, 2)
                    nc.vector.tensor_scalar(vm[:, :, 1], vm[:, :, 0], -1.0, 1.0, ALU.mult, ALU.add) \
                        .then_inc(cold.handle, 1)

                @block.tensor
                def _(pe):
                    pe.wait_ge(shapes_in.handle, 48)
                    pe.wait_ge(sel_ok.handle, 4)
                    nc.tensor.matmul(ps_a[:, 0:2 * HD], onehot[:].rearrange("p r s -> p (r s)"),
                                     const[0:S, C_ROPE:C_ROPE + 2 * HD], start=True, stop=True)
                    nc.tensor.transpose(ps_t[:, 0:B], vm_bs[:].rearrange("p r s -> p (r s)"), ident[0:B, 0:B]) \
                        .then_inc(xt_pe.handle, 1)
            cold.base += 4
            aggr_ok.base += 1
            sub_ok.base += 1
            sel_ok.base += 4
            rope1.base += 4
            mix_ok.base += 2
            xt_pe.base += 1

        def put_rstd(pool, p, u, eps):
            pool.wait_ge(stat_ok.handle, stat_ok.at(p + 1))
            nc.gpsimd.tensor_tensor(stat[:, u, 1:2], stat[:, u, 0:1], eps[:, 0:1], ALU.add).then_inc(eps_ok.handle, 1)
            pool.wait_ge(eps_ok.handle, eps_ok.at(p + 1))
            if xn_ok.due(p - 1):
                pool.wait_ge(xn_ok.handle, xn_ok.at(p - 1))
            nc.gpsimd.tensor_tensor(rstd[:, u, 0:1], stat[:, u, 1:2], half_neg[:, 0:1], ALU.pow) \
                .then_inc(rstd_ok.handle, 1)

        def half(r):
            return slice(J * r, J * r + J)

        def softmax_front(dve, mx, probs, p, u):
            s3 = ps_s[:].rearrange("p (h k) -> p h k", k=S)
            pr = probs[:, u].rearrange("p (h k) -> p h k", k=S)
            for r in range(2):
                dve.wait_ge(s_pe.handle, s_pe.at(p, r + 1))
                nc.vector.tensor_reduce(mx[:, u, half(r)], s3[:, half(r)], op=ALU.max, axis=AX.X) \
                    .then_inc(max_ok.handle, 1)
            for r in range(2):
                dve.wait_ge(max_ok.handle, max_ok.at(p, r + 1))
                if r == 0 and pt_pe.due(p - 1):
                    dve.wait_ge(pt_pe.handle, pt_pe.at(p - 1))
                nc.vector.tensor_tensor(pr[:, half(r)], s3[:, half(r)],
                                        mx[:, u, half(r)].unsqueeze(2).broadcast_to([P, J, S]), ALU.subtract) \
                    .then_inc(sub_ok.handle, 1)

        def softmax_exp(act, probs, p, u, scale):
            for r in range(2):
                act.wait_ge(sub_ok.handle, sub_ok.at(p, r + 1))
                cols = slice(J * S * r, J * S * (r + 1))
                nc.scalar.activation(probs[:, u, cols], probs[:, u, cols], ACT.Exp, scale=scale).then_inc(exp_ok.handle, 1)

        def softmax_sum(dve, sm, probs, p, u):
            for r in range(2):
                dve.wait_ge(exp_ok.handle, exp_ok.at(p, r + 1))
                if r == 0 and prob_ok.due(p - 1):
                    dve.wait_ge(prob_ok.handle, prob_ok.at(p - 1))
                nc.vector.tensor_reduce(sm[:, u, 0, half(r)], probs[:, u].rearrange("p (h k) -> p h k", k=S)[:, half(r)],
                                        op=ALU.add, axis=AX.X).then_inc(sum_ok.handle, 1)
            dve.wait_ge(sum_ok.handle, sum_ok.at(p + 1))
            nc.vector.reciprocal(sm[:, u, 1], sm[:, u, 0]).then_inc(inv_ok.handle, 1)

        def softmax_norm(pool, sm, probs, p, u):
            pool.wait_ge(inv_ok.handle, inv_ok.at(p + 1))
            pr = probs[:, u].rearrange("p (h k) -> p h k", k=S)
            nc.gpsimd.tensor_tensor(pr, pr, sm[:, u, 1].unsqueeze(2).broadcast_to([P, NH, S]), ALU.mult) \
                .then_inc(prob_ok.handle, 1)

        def prob_transposes(pe, probs, p, u):
            pe.wait_ge(prob_ok.handle, prob_ok.at(p + 1))
            for r, bank in enumerate((ps_p, ps_d)):
                if r == 0:
                    if pt_ok.due(p):
                        pe.wait_ge(pt_ok.handle, pt_ok.at(p))
                    if o_ok.due(p):
                        pe.wait_ge(o_ok.handle, o_ok.at(p))
                else:
                    if res_ok.due(p):
                        pe.wait_ge(res_ok.handle, res_ok.at(p))
                for j in range(4):
                    ins = nc.tensor.transpose(bank[:, j * P:j * P + P],
                                              probs[:, u, (4 * r + j) * P:(4 * r + j + 1) * P], ident)
                ins.then_inc(pt_pe.handle, 1)

        def prob_copies(act, pt, p):
            for r, bank in enumerate((ps_p, ps_d)):
                act.wait_ge(pt_pe.handle, pt_pe.at(p, r + 1))
                if r == 0:
                    if pv_pe.due(p):
                        act.wait_ge(pv_pe.handle, pv_pe.at(p))
                nc.scalar.activation(pt[:, 4 * r:4 * r + 4].rearrange("p j q -> p (j q)"), bank[:], ACT.Copy) \
                    .then_inc(pt_ok.handle, 1)

        def layer0(loaded, load_next):
            with ExitStack() as own:
                w_mem, w_gate, bias, w_norm = w_l0
                rows = sb("l0_rows", [P, 2, D + DC], F32, own)
                xt = sb("l0_xt", [P, 2, 3 * P], F32, own)
                mpt = sb("l0_mpt", [P, 2 * P], F32, own)
                mp = sb("l0_mp", [P, 2, D], F32, own)
                gx = sb("l0_gx", [P, PAIRS * D], F32, own)
                mx = sb("l0_mx", [P, 2, 2], F32, own)
                sm = sb("l0_sm", [P, 2, 2], F32, own)
                pr = sb("l0_pr", [P, 2, 2, P], F32, own)
                pt = sb("l0_pt", [P, P], F32, own)
                mc = sb("l0_mc", [P, 2, D], F32, own)
                mct = sb("l0_mct", [P, 2 * P], F32, own)
                z = sb("l0_z", [P, 3, D], F32, own)
                junk = sb("l0_junk", [P, D], F32, own)
                SCALE = D ** -0.5

                with nc.Block() as block:
                    @block.sync
                    def _(sp):
                        def step(p, u):
                            if has(p + 2):
                                if xt_pe.due(p + 1):
                                    sp.wait_ge(xt_pe.handle, xt_pe.at(p + 1))
                                sp.dma_start(rows[:, u, 0:D], x_flat[bass.ds((p + 2) * P, P), :]) \
                                    .then_inc(ctx_in[u].handle, 16)
                                sp.dma_start(rows[:, u, D:D + DC], ctx_rows(p + 2)).then_inc(ctx_in[u].handle, 16)
                                sp.dma_start(x_tile(p + 2), x_flat[bass.ds((p + 2) * P, P), :]) \
                                    .then_inc(ctx_in[u].handle, 16)
                        for p in (-2, -1):
                            step(p, p % 2)
                        km = t["mask_BxS2_bk0"].rearrange("(n two) k -> two n k", two=2)
                        for u in range(2):
                            sp.dma_start(km_raw[S * u:S * u + S], km[u:u + 1].broadcast_to([S, PAIRS, S])) \
                                .then_inc(keymask_in.handle, 16)
                        steps(sp, step)

                    @block.tensor
                    def _(pe):
                        pe.wait_ge(loaded.handle, loaded.at(0, 64))

                        def xt_(p, u):
                            pe.wait_ge(ctx_in[u].handle, arrival(p, u, 3))
                            if xt_ok.due(p):
                                pe.wait_ge(xt_ok.handle, xt_ok.at(p))
                            for c in range(3):
                                ins = nc.tensor.transpose(ps_t[:, c * P:c * P + P], rows[:, u, c * P:c * P + P], ident)
                            ins.then_inc(xt_pe.handle, 1)

                        def memory_t(p, u):
                            pe.wait_ge(xt_ok.handle, xt_ok.at(p + 1))
                            if qkt_ok.due(p):
                                pe.wait_ge(qkt_ok.handle, qkt_ok.at(p))
                            for c in range(CH):
                                ins = nc.tensor.matmul(ps_a[:, c * P:c * P + P], w_mem[:, c * P:c * P + P],
                                                       xt[:, u, 2 * P:3 * P], start=True, stop=True)
                            ins.then_inc(qk_pe.handle, 1)

                        def memory(p, u):
                            if v_ok.due(p):
                                pe.wait_ge(v_ok.handle, v_ok.at(p))
                            nc.tensor.matmul(ps_b[:, 0:D], xt[:, u, 2 * P:3 * P], w_mem[:], start=True, stop=True)
                            for c in range(CH):
                                ins = nc.tensor.matmul(ps_b[:, D:2 * D], xt[:, u, c * P:c * P + P], w_gate[:, c],
                                                       start=(c == 0), stop=(c == CH - 1))
                            ins.then_inc(v_pe.handle, 1)

                        def scores(p, u):
                            pe.wait_ge(qkt_ok.handle, qkt_ok.at(p + 1))
                            if exp_ok.due(p):
                                pe.wait_ge(exp_ok.handle, exp_ok.at(p))
                            nc.tensor.matmul(ps_s[:, 0:P], ident_b[:], block_b[:], start=True, stop=False)
                            for c in range(CH):
                                ins = nc.tensor.matmul(ps_s[:, 0:P], xt[:, u, c * P:c * P + P], mpt[:, c * P:c * P + P],
                                                       start=False, stop=(c == CH - 1))
                            ins.then_inc(s_pe.handle, 2)

                        def probs_t(p, u):
                            pe.wait_ge(prob_ok.handle, prob_ok.at(p + 1))
                            if pt_ok.due(p):
                                pe.wait_ge(pt_ok.handle, pt_ok.at(p))
                            nc.tensor.transpose(ps_p[:, 0:P], pr[:, u, 1], ident).then_inc(pt_pe.handle, 2)

                        def context(p, u):
                            pe.wait_ge(pt_ok.handle, pt_ok.at(p + 1))
                            pe.wait_ge(v_ok.handle, v_ok.at(p + 1))
                            if o_ok.due(p):
                                pe.wait_ge(o_ok.handle, o_ok.at(p))
                            nc.tensor.matmul(ps_o[:, 0:D], pt[:], mp[:, u], start=True, stop=True) \
                                .then_inc(pv_pe.handle, 1)

                        def context_t(p, u):
                            pe.wait_ge(o_ok.handle, o_ok.at(p, 1))
                            for c in range(CH):
                                ins = nc.tensor.transpose(ps_o[:, D + c * P:D + c * P + P], mc[:, u, c * P:c * P + P], ident)
                            ins.then_inc(pv_pe.handle, 1)

                        def gate(p, u):
                            pe.wait_ge(o_ok.handle, o_ok.at(p + 1))
                            if sel_ok.due(p):
                                pe.wait_ge(sel_ok.handle, sel_ok.at(p))
                            for c in range(CH):
                                ins = nc.tensor.matmul(ps_d[:, 0:D], mct[:, c * P:c * P + P], w_gate[:, CH + c],
                                                       start=(c == 0), stop=(c == CH - 1))
                            ins.then_inc(d_pe.handle, 1)

                        def step(p, u):
                            v = 1 - u
                            if has(p):
                                scores(p, u)
                            if has(p - 1):
                                probs_t(p - 1, v)
                            if has(p + 1):
                                memory_t(p + 1, v)
                            if has(p - 1):
                                context(p - 1, v)
                            if has(p + 1):
                                memory(p + 1, v)
                            if has(p - 1):
                                context_t(p - 1, v)
                            if has(p + 2):
                                xt_(p + 2, u)
                            if has(p - 1):
                                gate(p - 1, v)
                        xt_(0, 0)
                        memory_t(0, 0)
                        memory(0, 0)
                        xt_(1, 1)
                        steps(pe, step)

                    @block.scalar
                    def _(act):
                        load_next(act)

                        def xt_copy(p, u):
                            act.wait_ge(xt_pe.handle, xt_pe.at(p + 1))
                            if has(p - 1):
                                if s_pe.due(p - 1):
                                    act.wait_ge(s_pe.handle, s_pe.at(p - 1))
                                if v_pe.due(p - 1):
                                    act.wait_ge(v_pe.handle, v_pe.at(p - 1))
                            nc.scalar.activation(xt[:, u], ps_t[:, 0:3 * P], ACT.Copy).then_inc(xt_ok.handle, 1)

                        def mpt_copy(p):
                            act.wait_ge(qk_pe.handle, qk_pe.at(p + 1))
                            if s_pe.due(p):
                                act.wait_ge(s_pe.handle, s_pe.at(p))
                            nc.scalar.activation(mpt[:], ps_a[:, 0:2 * P], ACT.Copy).then_inc(qkt_ok.handle, 1)

                        def step(p, u):
                            v = 1 - u
                            if has(p - 2):
                                act.wait_ge(sel_ok.handle, sel_ok.at(p - 1))
                                nc.scalar.activation(z[:, 1], z[:, 0], ACT.Tanh, scale=0.5).then_inc(rope1.handle, 1)
                            if has(p - 1):
                                act.wait_ge(pt_pe.handle, pt_pe.at(p))
                                if pv_pe.due(p - 1):
                                    act.wait_ge(pv_pe.handle, pv_pe.at(p - 1))
                                nc.scalar.activation(pt[:], ps_p[:, 0:P], ACT.Copy).then_inc(pt_ok.handle, 2)
                            if has(p):
                                act.wait_ge(sub_ok.handle, sub_ok.at(p + 1))
                                if prob_ok.due(p - 1):
                                    act.wait_ge(prob_ok.handle, prob_ok.at(p - 1))
                                nc.scalar.activation(pr[:, u, 0], ps_s[:, 0:P], ACT.Exp, bias=mx[:, u, 1:2],
                                                     scale=SCALE, accum_out=sm[:, u, 0:1]).then_inc(exp_ok.handle, 2)
                            if has(p - 2):
                                act.wait_ge(mix_ok.handle, mix_ok.at(p - 1))
                                if eps_ok.due(p - 3):
                                    act.wait_ge(eps_ok.handle, eps_ok.at(p - 3))
                                if stat_ok.due(p - 2):
                                    act.wait_ge(stat_ok.handle, stat_ok.at(p - 2))
                                nc.scalar.activation(junk[:], x_tile(p - 2), ACT.Square, scale=D ** -0.5,
                                                     accum_out=stat[:, u, 0:1]).then_inc(stat_ok.handle, 1)
                            if has(p + 1):
                                mpt_copy(p + 1)
                            if has(p - 1):
                                act.wait_ge(pv_pe.handle, pv_pe.at(p - 1, 1))
                                if mix_ok.due(p - 2):
                                    act.wait_ge(mix_ok.handle, mix_ok.at(p - 2))
                                nc.scalar.activation(mc[:, v], ps_o[:, 0:D], ACT.Copy).then_inc(o_ok.handle, 1)
                            if has(p - 1):
                                act.wait_ge(pv_pe.handle, pv_pe.at(p))
                                if d_pe.due(p - 1):
                                    act.wait_ge(d_pe.handle, d_pe.at(p - 1))
                                nc.scalar.activation(mct[:], ps_o[:, D:D + 2 * P], ACT.Copy).then_inc(o_ok.handle, 1)
                            if has(p + 2):
                                xt_copy(p + 2, u)
                        xt_copy(0, 0)
                        mpt_copy(0)
                        xt_copy(1, 1)
                        steps(act, step)
                        step(PAIRS + 1, 1)

                    @block.vector
                    def _(dve):
                        dve.wait_ge(loaded.handle, loaded.at(0, 64))

                        def v_copy(p, u):
                            dve.wait_ge(v_pe.handle, v_pe.at(p + 1))
                            if pv_pe.due(p - 2, 1):
                                dve.wait_ge(pv_pe.handle, pv_pe.at(p - 2, 1))
                            nc.vector.tensor_tensor(gx[:, bass.ds(p * D, D)], ps_b[:, D:2 * D], bias[:], ALU.add) \
                                .then_inc(kx_ok.handle, 1)
                            nc.vector.tensor_copy(mp[:, u], ps_b[:, 0:D]).then_inc(v_ok.handle, 1)

                        def step(p, u):
                            v = 1 - u
                            if has(p - 2):
                                dve.wait_ge(d_pe.handle, d_pe.at(p - 1))
                                if rope1.due(p - 2):
                                    dve.wait_ge(rope1.handle, rope1.at(p - 2))
                                dve.wait_ge(kx_ok.handle, kx_ok.at(p - 1))
                                nc.vector.tensor_tensor(z[:, 0], ps_d[:, 0:D], gx[:, bass.ds((p - 2) * D, D)], ALU.add) \
                                    .then_inc(sel_ok.handle, 1)
                            if has(p):
                                dve.wait_ge(s_pe.handle, s_pe.at(p + 1))
                                nc.vector.tensor_reduce(mx[:, u, 0:1], ps_s[:, 0:P], op=ALU.max, axis=AX.X) \
                                    .then_inc(max_ok.handle, 2)
                                dve.wait_ge(max_ok.handle, max_ok.at(p + 1))
                                nc.vector.tensor_scalar(mx[:, u, 1:2], mx[:, u, 0:1], -SCALE, None, ALU.mult) \
                                    .then_inc(sub_ok.handle, 2)
                            if has(p - 2):
                                dve.wait_ge(rope1.handle, rope1.at(p - 1))
                                nc.vector.scalar_tensor_tensor(z[:, 2], z[:, 1], 1.0, mc[:, u], ALU.add, ALU.mult) \
                                    .then_inc(aggr_ok.handle, 1)
                                dve.wait_ge(aggr_ok.handle, aggr_ok.at(p - 1))
                                nc.vector.scalar_tensor_tensor(x_tile(p - 2), z[:, 2], 0.5, x_tile(p - 2),
                                                               ALU.mult, ALU.add).then_inc(mix_ok.handle, 1)
                            if has(p):
                                dve.wait_ge(exp_ok.handle, exp_ok.at(p + 1))
                                nc.vector.reciprocal(sm[:, u, 1:2], sm[:, u, 0:1]).then_inc(inv_ok.handle, 1)
                                dve.wait_ge(inv_ok.handle, inv_ok.at(p + 1))
                                if pt_pe.due(p - 1):
                                    dve.wait_ge(pt_pe.handle, pt_pe.at(p - 1))
                                nc.vector.tensor_scalar(pr[:, u, 1], pr[:, u, 0], sm[:, u, 1:2], None, ALU.mult) \
                                    .then_inc(prob_ok.handle, 1)
                            if has(p + 1):
                                v_copy(p + 1, v)
                            if has(p - 2):
                                dve.wait_ge(rstd_ok.handle, rstd_ok.at(p - 1))
                                dve.wait_ge(stat_ok.handle, stat_ok.at(p - 1))
                                nc.vector.scalar_tensor_tensor(x_tile(p - 2), x_tile(p - 2), rstd[:, u, 0:1],
                                                               w_norm[:], ALU.mult, ALU.mult).then_inc(res_ok.handle, 1)
                        v_copy(0, 0)
                        steps(dve, step)
                        step(PAIRS + 1, 1)

                    @block.gpsimd
                    def _(pool):
                        def step(p, u):
                            if has(p - 2):
                                pool.wait_ge(stat_ok.handle, stat_ok.at(p - 1))
                                nc.gpsimd.tensor_tensor(stat[:, u, 1:2], stat[:, u, 0:1], eps6[:, 0:1], ALU.add) \
                                    .then_inc(eps_ok.handle, 1)
                                pool.wait_ge(eps_ok.handle, eps_ok.at(p - 1))
                                if res_ok.due(p - 3):
                                    pool.wait_ge(res_ok.handle, res_ok.at(p - 3))
                                nc.gpsimd.tensor_tensor(rstd[:, u, 0:1], stat[:, u, 1:2], half_neg[:, 0:1], ALU.pow) \
                                    .then_inc(rstd_ok.handle, 1)
                        steps(pool, step)
                        step(PAIRS + 1, 1)
                loaded.base += 64
                for c in ctx_in:
                    c.base += 24 * PAIRS
                close(PAIRS, stat_ok, aggr_ok, eps_ok, rstd_ok, xt_pe, xt_ok, qk_pe, rope1, qkt_ok, kx_ok,
                      v_pe, v_ok, s_pe, max_ok, sub_ok, exp_ok, inv_ok, prob_ok, pt_pe, pt_ok, pv_pe, o_ok, d_pe,
                      sel_ok, mix_ok, res_ok)

        x_flat = t["x"].rearrange("b s d -> (b s) d")
        ctx_flat = t["ctx_1024"].rearrange("b s d -> (b s) d")

        def ctx_rows(p):
            return ctx_flat[bass.ds(p * P, P), :]

        def self_attention(n, loaded, load_next):
            with ExitStack() as own:
                def ob(name, shape, dt=F32):
                    return sb(f"s{n}_{name}", shape, dt, own)

                w_qkv, w_out, w_ln = w_self
                junk = ob("junk", [P, D])
                mixw = ob("mixw", [P, 2])
                xn = ob("xn", [P, 2, D])
                xt = ob("xt", [P, 2, CH, 2, P])
                xh = ob("xh", [P, CH, 2, P], F32R)
                xl = ob("xl", [P, CH, 2, P], F32R)
                wh = ob("wh", [P, 2 * CH, 2 * D], F32R)
                wl = ob("wl", [P, 2 * CH, 2 * D], F32R)
                oh = ob("oh", [P, CH, 2 * D], F32R)
                ol = ob("ol", [P, CH, 2 * D], F32R)
                roped = ob("roped", [P, 2, 2 * D])
                qkt = ob("qkt", [P, 4, P])
                kx = ob("kx", [P, CH, 2, 8, S])
                vb = ob("vb", [P, 2, 2, J, 2, HD])
                mx = ob("mx", [P, 2, NH])
                sm = ob("sm", [P, 2, 2, NH])
                probs = ob("probs", [P, 2, NH * S])
                pt = ob("pt", [P, J, P])
                oth = ob("oth", [P, CH, P], F32R)
                otl = ob("otl", [P, CH, P], F32R)
                sel = ob("sel", [P, 2])
                part = ob("part", [P, D])

                with nc.Block() as block:
                    @block.tensor
                    def _(pe):
                        pe.wait_ge(loaded.handle, loaded.at(0, 80))
                        pe.wait_ge(cold.handle, cold.at(0, 1))

                        def xt_(p, u):
                            pe.wait_ge(xn_ok.handle, xn_ok.at(p + 1))
                            if qkt_ok.due(p):
                                pe.wait_ge(qkt_ok.handle, qkt_ok.at(p))
                            for c in range(CH):
                                for e in range(2):
                                    ins = nc.tensor.transpose(ps_t[:, (2 * c + e) * P:(2 * c + e + 1) * P],
                                                              xn[:, e, c * P:c * P + P], ident)
                            ins.then_inc(xt_pe.handle, 1)

                        def proj_qk(p, u):
                            pe.wait_ge(xlow_ok.handle, xlow_ok.at(p + 1))
                            if rope1.due(p):
                                pe.wait_ge(rope1.handle, rope1.at(p))
                            for k in range(2 * CH):
                                e, c = divmod(k, CH)
                                nc.tensor.matmul(ps_a[:], xh[:, c, e], wh[:, k], start=(k == 0), stop=False)
                                nc.tensor.matmul(ps_a[:], xh[:, c, e], wl[:, k], start=False, stop=False)
                                ins = nc.tensor.matmul(ps_a[:], xl[:, c, e], wh[:, k], start=False,
                                                       stop=(k == 2 * CH - 1))
                            ins.then_inc(qk_pe.handle, 1)

                        def proj_v(p, u):
                            if v_ok.due(p):
                                pe.wait_ge(v_ok.handle, v_ok.at(p))
                            for b in range(2):
                                for h in range(2):
                                    for k in range(2 * CH):
                                        e, c = divmod(k, CH)
                                        w = w_qkv[:, k, 2 * D:3 * D].rearrange("p (j h d) -> p j h d", h=2, d=HD)
                                        ins = nc.tensor.matmul(ps_b[S * h:S * h + S, b * P:b * P + P],
                                                               xt[:, u, c, e, b * S:b * S + S], w[:, :, h],
                                                               start=(k == 0), stop=(k == 2 * CH - 1))
                            ins.then_inc(v_pe.handle, 1)

                        def qk_t(p):
                            pe.wait_ge(rope_ok.handle, rope_ok.at(p + 1))
                            pe.wait_ge(xt_ok.handle, xt_ok.at(p + 1))
                            for c in range(4):
                                ins = nc.tensor.transpose(ps_t[:, c * P:c * P + P], roped[:, 0, c * P:c * P + P], ident)
                            ins.then_inc(qkt_pe.handle, 1)

                        def scores(p):
                            if sub_ok.due(p):
                                pe.wait_ge(sub_ok.handle, sub_ok.at(p))
                            pe.wait_ge(kx_ok.handle, kx_ok.at(p + 1))
                            for h in range(CH):
                                out = ps_s[:, 512 * h:512 * h + 512]
                                nc.tensor.matmul(out, ident_b[:], causal_b[:].unsqueeze(1).broadcast_to([P, 8, S]),
                                                 start=True, stop=False, skip_group_check=True)
                                for b in range(2):
                                    ins = nc.tensor.matmul(out[b * S:b * S + S], qkt[:, h, b * S:b * S + S],
                                                           kx[:, h, b].rearrange("p h k -> p (h k)"),
                                                           start=False, stop=True, skip_group_check=True)
                                ins.then_inc(s_pe.handle, 1)

                        def pv(p, u):
                            pe.wait_ge(pt_ok.handle, pt_ok.at(p + 1))
                            pe.wait_ge(v_ok.handle, v_ok.at(p + 1))
                            if o_ok.due(p):
                                pe.wait_ge(o_ok.handle, o_ok.at(p))
                            for b in range(2):
                                for j in range(J):
                                    r, h = j % 4, j // 4
                                    ins = nc.tensor.matmul(
                                        ps_o[32 * r:32 * r + 32, h * P + b * S:h * P + b * S + S],
                                        vb[:, u, b, j].rearrange("p h d -> p (h d)"), pt[:, j, b * S:b * S + S],
                                        start=True, stop=True, skip_group_check=True)
                            ins.then_inc(pv_pe.handle, 2)

                        def dense(p):
                            pe.wait_ge(o_ok.handle, o_ok.at(p + 1))
                            for c in range(CH):
                                nc.tensor.matmul(ps_d[:], oth[:, c], oh[:, c], start=(c == 0), stop=False)
                                nc.tensor.matmul(ps_d[:], oth[:, c], ol[:, c], start=False, stop=False)
                                ins = nc.tensor.matmul(ps_d[:], otl[:, c], oh[:, c], start=False, stop=(c == CH - 1))
                            ins.then_inc(d_pe.handle, 1)

                        def step(p, u):
                            v = 1 - u
                            if has(p + 1):
                                proj_qk(p + 1, v)
                            if has(p):
                                scores(p)
                            if has(p + 1):
                                qk_t(p + 1)
                            if has(p - 1):
                                prob_transposes(pe, probs, p - 1, v)
                            if has(p + 2):
                                xt_(p + 2, u)
                            if has(p - 1):
                                pv(p - 1, v)
                            if has(p + 1):
                                proj_v(p + 1, v)
                            if has(p - 1):
                                dense(p - 1)
                        xt_(0, 0)
                        pe.wait_ge(wlow_ok.handle, wlow_ok.at(2 * CH))
                        proj_qk(0, 0)
                        qk_t(0)
                        xt_(1, 1)
                        proj_v(0, 0)
                        pe.wait_ge(wlow_ok.handle, wlow_ok.at(3 * CH))
                        steps(pe, step)

                    @block.scalar
                    def _(act):
                        load_next(act)
                        act.wait_ge(loaded.handle, loaded.at(0, 80))

                        def stat_(p, u):
                            if eps_ok.due(p - 1):
                                act.wait_ge(eps_ok.handle, eps_ok.at(p - 1))
                            if stat_ok.due(p):
                                act.wait_ge(stat_ok.handle, stat_ok.at(p))
                            nc.scalar.activation(junk[:], x_tile(p), ACT.Square, scale=D ** -0.5,
                                                 accum_out=stat[:, u, 0:1]).then_inc(stat_ok.handle, 1)

                        def xt_copy(p, u):
                            act.wait_ge(xt_pe.handle, xt_pe.at(p + 1))
                            if v_pe.due(p - 1):
                                act.wait_ge(v_pe.handle, v_pe.at(p - 1))
                            for c in range(CH):
                                ins = nc.scalar.activation(xt[:, u, c].rearrange("p e n -> p (e n)"),
                                                           ps_t[:, 2 * c * P:2 * (c + 1) * P], ACT.Copy,
                                                           scale=w_ln[:, c:c + 1])
                            ins.then_inc(xt_ok.handle, 1)

                        def x_high(p, u):
                            act.wait_ge(xt_ok.handle, xt_ok.at(p + 1))
                            if qk_pe.due(p):
                                act.wait_ge(qk_pe.handle, qk_pe.at(p))
                            nc.scalar.activation(xh[:].rearrange("p c e n -> p (c e n)"),
                                                 xt[:, u].rearrange("p c e n -> p (c e n)"), ACT.Copy) \
                                .then_inc(xhigh_ok.handle, 1)

                        def qkt_copy(p):
                            act.wait_ge(qkt_pe.handle, qkt_pe.at(p + 1))
                            if s_pe.due(p):
                                act.wait_ge(s_pe.handle, s_pe.at(p))
                            nc.scalar.activation(qkt[:].rearrange("p c n -> p (c n)"), ps_t[:], ACT.Copy) \
                                .then_inc(qkt_ok.handle, 1)

                        def step(p, u):
                            v = 1 - u
                            if has(p + 1):
                                qkt_copy(p + 1)
                            if has(p - 1):
                                prob_copies(act, pt, p - 1)
                            if has(p):
                                softmax_exp(act, probs, p, u, HD ** -0.5)
                            if has(p - 1):
                                act.wait_ge(pv_pe.handle, pv_pe.at(p))
                                if d_pe.due(p - 1):
                                    act.wait_ge(d_pe.handle, d_pe.at(p - 1))
                                nc.scalar.activation(oth[:].rearrange("p c n -> p (c n)"), ps_o[:, 0:2 * P], ACT.Copy) \
                                    .then_inc(hhigh_ok.handle, 1)
                            if has(p + 2):
                                xt_copy(p + 2, u)
                                x_high(p + 2, u)
                            if has(p + 4):
                                stat_(p + 4, u)
                        for k in range(2 * CH):
                            nc.scalar.activation(wh[:, k], w_qkv[:, k, 0:2 * D], ACT.Copy).then_inc(whigh_ok.handle, 1)
                        for c in range(CH):
                            nc.scalar.activation(oh[:, c], w_out[:, c].rearrange("p e n -> p (e n)"), ACT.Copy) \
                                .then_inc(whigh_ok.handle, 1)
                        for p in range(4):
                            stat_(p, p % 2)
                            if p == 1:
                                xt_copy(0, 0)
                                x_high(0, 0)
                        qkt_copy(0)
                        xt_copy(1, 1)
                        x_high(1, 1)
                        steps(act, step)

                    @block.gpsimd
                    def _(pool):
                        nc.gpsimd.memset(vb[:].rearrange("p a b j h d -> p (a b j h d)"), 0.0).then_inc(cold.handle, 1)

                        def spread(p):
                            pool.wait_ge(qkt_ok.handle, qkt_ok.at(p + 1))
                            if s_pe.due(p):
                                pool.wait_ge(s_pe.handle, s_pe.at(p))
                            for h in range(CH):
                                for b in range(2):
                                    ins = nc.gpsimd.tensor_tensor(
                                        kx[:, h, b], qkt[:, 2 + h, b * S:b * S + S].unsqueeze(1).broadcast_to([P, 8, S]),
                                        const[:, C_H16:C_H16 + 8].unsqueeze(2).broadcast_to([P, 8, S]), ALU.mult)
                            ins.then_inc(kx_ok.handle, 1)

                        def step(p, u):
                            if has(p + 1):
                                spread(p + 1)
                            if has(p):
                                softmax_norm(pool, sm, probs, p, u)
                            if has(p + 4):
                                put_rstd(pool, p + 4, u, eps6)
                        for p in range(4):
                            put_rstd(pool, p, p % 2, eps6)
                        spread(0)
                        steps(pool, step)

                    @block.vector
                    def _(dve):
                        dve.wait_ge(cold.handle, cold.at(0, 1))

                        def norm(p, u):
                            dve.wait_ge(rstd_ok.handle, rstd_ok.at(p + 1))
                            if xt_pe.due(p):
                                dve.wait_ge(xt_pe.handle, xt_pe.at(p))
                            nc.vector.tensor_scalar(mixw[:], vm[:, bass.ds(p, 1), :].rearrange("p a e -> p (a e)"),
                                                    rstd[:, u, 0:1], None, ALU.mult).then_inc(mixw_ok.handle, 1)
                            dve.wait_ge(mixw_ok.handle, mixw_ok.at(p + 1))
                            for e in range(2):
                                ins = nc.vector.tensor_scalar(xn[:, e], x_tile(p), mixw[:, e:e + 1], None, ALU.mult)
                            ins.then_inc(xn_ok.handle, 1)

                        def x_low(p, u):
                            dve.wait_ge(xhigh_ok.handle, xhigh_ok.at(p + 1))
                            nc.vector.tensor_tensor(xl[:].rearrange("p c e n -> p (c e n)"),
                                                    xt[:, u].rearrange("p c e n -> p (c e n)"),
                                                    xh[:].rearrange("p c e n -> p (c e n)").bitcast(F32), ALU.subtract) \
                                .then_inc(xlow_ok.handle, 1)

                        def out_low(p):
                            dve.wait_ge(hhigh_ok.handle, hhigh_ok.at(p + 1))
                            nc.vector.tensor_tensor(otl[:].rearrange("p c n -> p (c n)"), ps_o[:, 0:2 * P],
                                                    oth[:].rearrange("p c n -> p (c n)").bitcast(F32), ALU.subtract) \
                                .then_inc(o_ok.handle, 2)

                        def rope_(p):
                            dve.wait_ge(qk_pe.handle, qk_pe.at(p + 1))
                            if qkt_pe.due(p):
                                dve.wait_ge(qkt_pe.handle, qkt_pe.at(p))
                            a = ps_a[:].rearrange("p (h d) -> p h d", d=HD)
                            o = [roped[:, r].rearrange("p (h d) -> p h d", d=HD) for r in range(2)]
                            H2 = HD // 2

                            def table(c0, w):
                                return rope[:, c0:c0 + w].unsqueeze(1).broadcast_to([P, 2 * NH, w])
                            nc.vector.tensor_tensor(o[0], a, table(0, HD), ALU.mult)
                            nc.vector.tensor_tensor(o[1][:, :, 0:H2], a[:, :, H2:HD], table(HD, H2), ALU.mult)
                            nc.vector.tensor_tensor(o[1][:, :, H2:HD], a[:, :, 0:H2], table(HD + H2, H2), ALU.mult) \
                                .then_inc(rope1.handle, 1)
                            dve.wait_ge(rope1.handle, rope1.at(p + 1))
                            nc.vector.tensor_tensor(roped[:, 0], roped[:, 0], roped[:, 1], ALU.add) \
                                .then_inc(rope_ok.handle, 1)

                        def v_blocks(p, u):
                            dve.wait_ge(v_pe.handle, v_pe.at(p + 1))
                            if pv_pe.due(p - 1):
                                dve.wait_ge(pv_pe.handle, pv_pe.at(p - 1))
                            for h in range(2):
                                rows = slice(S * h, S * h + S)
                                ins = nc.vector.tensor_copy(
                                    vb[rows, u, :, :, h].rearrange("p b j d -> p (b j) d"),
                                    ps_b[rows, 0:D].rearrange("p (bj d) -> p bj d", d=HD))
                            ins.then_inc(v_ok.handle, 1)

                        def residual(p):
                            dve.wait_ge(d_pe.handle, d_pe.at(p + 1))
                            nc.vector.tensor_copy(sel[:], vm[:, bass.ds(p, 1), :].rearrange("p a e -> p (a e)")) \
                                .then_inc(sel_ok.handle, 1)
                            dve.wait_ge(sel_ok.handle, sel_ok.at(p + 1))
                            nc.vector.scalar_tensor_tensor(part[:], ps_d[:, 0:D], sel[:, 0:1], x_tile(p),
                                                           ALU.mult, ALU.add).then_inc(mix_ok.handle, 1)
                            dve.wait_ge(mix_ok.handle, mix_ok.at(p + 1))
                            nc.vector.scalar_tensor_tensor(x_tile(p), ps_d[:, D:2 * D], sel[:, 1:2], part[:],
                                                           ALU.mult, ALU.add).then_inc(res_ok.handle, 1)

                        def step(p, u):
                            v = 1 - u
                            if has(p + 1):
                                rope_(p + 1)
                            if has(p):
                                softmax_front(dve, mx, probs, p, u)
                            if has(p - 1):
                                out_low(p - 1)
                            if has(p):
                                softmax_sum(dve, sm, probs, p, u)
                            if has(p + 2):
                                x_low(p + 2, u)
                            if has(p + 3):
                                norm(p + 3, v)
                            if has(p + 1):
                                v_blocks(p + 1, v)
                            if has(p - 1):
                                residual(p - 1)
                        norm(0, 0)
                        for k in range(2 * CH):
                            dve.wait_ge(whigh_ok.handle, whigh_ok.at(k + 1))
                            nc.vector.tensor_tensor(wl[:, k], w_qkv[:, k, 0:2 * D], wh[:, k].bitcast(F32), ALU.subtract) \
                                .then_inc(wlow_ok.handle, 1)
                        x_low(0, 0)
                        for c in range(CH):
                            dve.wait_ge(whigh_ok.handle, whigh_ok.at(2 * CH + c + 1))
                            nc.vector.tensor_tensor(ol[:, c], w_out[:, c].rearrange("p e n -> p (e n)"),
                                                    oh[:, c].bitcast(F32), ALU.subtract).then_inc(wlow_ok.handle, 1)
                        norm(1, 1)
                        rope_(0)
                        x_low(1, 1)
                        norm(2, 0)
                        v_blocks(0, 0)
                        steps(dve, step)
                loaded.base += 80
                cold.base += 1
                close(3 * CH, whigh_ok, wlow_ok)
                close(PAIRS, xlow_ok, xhigh_ok, hhigh_ok)
                close(PAIRS, stat_ok, eps_ok, rstd_ok, mixw_ok, xn_ok, xt_pe, xt_ok, qk_pe, rope1, rope_ok, qkt_pe,
                      qkt_ok, kx_ok, v_pe, v_ok, s_pe, max_ok, sub_ok, exp_ok, sum_ok, inv_ok, prob_ok, pt_pe, pt_ok,
                      pv_pe, o_ok, d_pe, sel_ok, mix_ok, res_ok)

        def cross_attention(n, loaded, load_next):
            with ExitStack() as own:
                def ob(name, shape, dt=F32):
                    return sb(f"c{n}_{name}", shape, dt, own)

                w_q, w_kv, w_out, w_ln = w_cross
                ctx_t = ob("ctx_t", [P, 2, DC])
                junk = ob("junk", [P, D])
                xn = ob("xn", [P, D])
                xt = ob("xt", [P, 2, 3, P])
                qkt = ob("qkt", [P, 2, 2, P])
                kx = ob("kx", [P, 2, 2, NH, S])
                vb = ob("vb", [P, 2, 2, J, 2 * HD])
                mx = ob("mx", [P, 2, NH])
                sm = ob("sm", [P, 2, 2, NH])
                probs = ob("probs", [P, 2, NH * S])
                pt = ob("pt", [P, J, P])
                ot = ob("ot", [P, P])

                with nc.Block() as block:
                    @block.sync
                    def _(sp):
                        def step(p, u):
                            if has(p + 2):
                                if xt_pe.due(p + 1):
                                    sp.wait_ge(xt_pe.handle, xt_pe.at(p + 1))
                                sp.dma_start(ctx_t[:, u], ctx_rows(p + 2)).then_inc(ctx_in[u].handle, 16)
                        for p in (-2, -1):
                            step(p, p % 2)
                        steps(sp, step)

                    @block.tensor
                    def _(pe):
                        pe.wait_ge(loaded.handle, loaded.at(0, 64))
                        pe.wait_ge(cold.handle, cold.at(0, 1))

                        def xt_(p, u):
                            pe.wait_ge(xn_ok.handle, xn_ok.at(p + 1))
                            pe.wait_ge(ctx_in[u].handle, arrival(p, u, 1))
                            if xt_ok.due(p):
                                pe.wait_ge(xt_ok.handle, xt_ok.at(p))
                            for c in range(CH):
                                nc.tensor.transpose(ps_t[:, c * P:c * P + P], xn[:, c * P:c * P + P], ident)
                            nc.tensor.transpose(ps_t[:, CH * P:CH * P + P], ctx_t[:, u], ident).then_inc(xt_pe.handle, 1)

                        def proj_qk(p, u):
                            pe.wait_ge(xt_ok.handle, xt_ok.at(p + 1))
                            if qkt_ok.due(p):
                                pe.wait_ge(qkt_ok.handle, qkt_ok.at(p))
                            for c in range(CH):
                                nc.tensor.matmul(ps_a[:, 0:P], w_q[:, c], xt[:, u, c], start=(c == 0), stop=(c == CH - 1))
                            nc.tensor.matmul(ps_a[:, P:2 * P], w_kv[:, 0:DC], xt[:, u, CH], start=True, stop=True) \
                                .then_inc(qk_pe.handle, 1)

                        def proj_v(p, u):
                            if v_ok.due(p):
                                pe.wait_ge(v_ok.handle, v_ok.at(p))
                            w = w_kv[:, DC:2 * DC].rearrange("p (j h d) -> p j h d", h=2, d=CHD)
                            for b in range(2):
                                for h in range(2):
                                    ins = nc.tensor.matmul(ps_b[S * h:S * h + S, b * S:b * S + S],
                                                           xt[:, u, CH, b * S:b * S + S], w[:, :, h],
                                                           start=True, stop=True)
                            ins.then_inc(v_pe.handle, 1)

                        def scores(p, u):
                            if sub_ok.due(p):
                                pe.wait_ge(sub_ok.handle, sub_ok.at(p))
                            pe.wait_ge(kx_ok.handle, kx_ok.at(p + 1))
                            for h in range(2):
                                for b in range(2):
                                    ins = nc.tensor.matmul(ps_s[b * S:b * S + S, 512 * h:512 * h + 512],
                                                           qkt[:, u, 0, b * S:b * S + S],
                                                           kx[:, u, b, 8 * h:8 * h + 8].rearrange("p h k -> p (h k)"),
                                                           start=True, stop=True)
                                ins.then_inc(s_pe.handle, 1)

                        def pv(p, u):
                            pe.wait_ge(pt_ok.handle, pt_ok.at(p + 1))
                            pe.wait_ge(v_ok.handle, v_ok.at(p + 1))
                            if o_ok.due(p):
                                pe.wait_ge(o_ok.handle, o_ok.at(p))
                            for b in range(2):
                                for j in range(J):
                                    r = j // 2
                                    ins = nc.tensor.matmul(
                                        ps_o[32 * r:32 * r + 32, b * S:b * S + S], vb[:, u, b, j],
                                        pt[:, j, b * S:b * S + S], start=(j % 2 == 0), stop=(j % 2 == 1))
                            ins.then_inc(pv_pe.handle, 2)

                        def dense(p):
                            pe.wait_ge(o_ok.handle, o_ok.at(p + 1))
                            nc.tensor.matmul(ps_d[:, 0:D], ot[:], w_out[:], start=True, stop=True).then_inc(d_pe.handle, 1)

                        def step(p, u):
                            v = 1 - u
                            if has(p + 1):
                                proj_qk(p + 1, v)
                            if has(p):
                                scores(p, u)
                            if has(p - 1):
                                prob_transposes(pe, probs, p - 1, v)
                            if has(p + 2):
                                xt_(p + 2, u)
                            if has(p - 1):
                                pv(p - 1, v)
                            if has(p + 1):
                                proj_v(p + 1, v)
                            if has(p - 1):
                                dense(p - 1)
                        xt_(0, 0)
                        proj_qk(0, 0)
                        xt_(1, 1)
                        proj_v(0, 0)
                        steps(pe, step)

                    @block.scalar
                    def _(act):
                        load_next(act)
                        act.wait_ge(loaded.handle, loaded.at(0, 64))

                        def stat_(p, u):
                            if eps_ok.due(p - 1):
                                act.wait_ge(eps_ok.handle, eps_ok.at(p - 1))
                            if stat_ok.due(p):
                                act.wait_ge(stat_ok.handle, stat_ok.at(p))
                            nc.scalar.activation(junk[:], x_tile(p), ACT.Square, scale=D ** -0.5,
                                                 accum_out=stat[:, u, 0:1]).then_inc(stat_ok.handle, 1)

                        def xt_copy(p, u):
                            act.wait_ge(xt_pe.handle, xt_pe.at(p + 1))
                            if v_pe.due(p - 1):
                                act.wait_ge(v_pe.handle, v_pe.at(p - 1))
                            for c in range(CH):
                                nc.scalar.activation(xt[:, u, c], ps_t[:, c * P:c * P + P], ACT.Copy, scale=w_ln[:, c:c + 1])
                            nc.scalar.activation(xt[:, u, CH], ps_t[:, CH * P:CH * P + P], ACT.Copy) \
                                .then_inc(xt_ok.handle, 1)

                        def qkt_copy(p, u):
                            act.wait_ge(qk_pe.handle, qk_pe.at(p + 1))
                            if s_pe.due(p - 1):
                                act.wait_ge(s_pe.handle, s_pe.at(p - 1))
                            nc.scalar.activation(qkt[:, u].rearrange("p c n -> p (c n)"), ps_a[:, 0:2 * P], ACT.Copy) \
                                .then_inc(qkt_ok.handle, 1)

                        def step(p, u):
                            v = 1 - u
                            if has(p + 1):
                                qkt_copy(p + 1, v)
                            if has(p - 1):
                                prob_copies(act, pt, p - 1)
                            if has(p):
                                softmax_exp(act, probs, p, u, CHD ** -0.5)
                            if has(p - 1):
                                act.wait_ge(pv_pe.handle, pv_pe.at(p))
                                if d_pe.due(p - 1):
                                    act.wait_ge(d_pe.handle, d_pe.at(p - 1))
                                nc.scalar.activation(ot[:], ps_o[:, 0:P], ACT.Copy).then_inc(o_ok.handle, 2)
                            if has(p + 2):
                                xt_copy(p + 2, u)
                            if has(p + 4):
                                stat_(p + 4, u)
                        for p in range(4):
                            stat_(p, p % 2)
                            if p == 1:
                                xt_copy(0, 0)
                            if p == 2:
                                qkt_copy(0, 0)
                                xt_copy(1, 1)
                        steps(act, step)

                    @block.gpsimd
                    def _(pool):
                        nc.gpsimd.memset(vb[:].rearrange("p a b j c -> p (a b j c)"), 0.0).then_inc(cold.handle, 1)

                        def spread(p, u):
                            pool.wait_ge(qkt_ok.handle, qkt_ok.at(p + 1))
                            if s_pe.due(p - 1):
                                pool.wait_ge(s_pe.handle, s_pe.at(p - 1))
                            for b in range(2):
                                ins = nc.gpsimd.tensor_tensor(
                                    kx[:, u, b], qkt[:, u, 1, b * S:b * S + S].unsqueeze(1).broadcast_to([P, NH, S]),
                                    const[:, C_H8:C_H8 + NH].unsqueeze(2).broadcast_to([P, NH, S]), ALU.mult)
                            ins.then_inc(kx_ok.handle, 1)

                        def step(p, u):
                            if has(p + 1):
                                spread(p + 1, 1 - u)
                            if has(p):
                                softmax_norm(pool, sm, probs, p, u)
                            if has(p + 4):
                                put_rstd(pool, p + 4, u, eps6)
                        for p in range(4):
                            put_rstd(pool, p, p % 2, eps6)
                        spread(0, 0)
                        steps(pool, step)

                    @block.vector
                    def _(dve):
                        dve.wait_ge(cold.handle, cold.at(0, 1))

                        def norm(p, u):
                            dve.wait_ge(rstd_ok.handle, rstd_ok.at(p + 1))
                            if xt_pe.due(p):
                                dve.wait_ge(xt_pe.handle, xt_pe.at(p))
                            nc.vector.tensor_scalar(xn[:], x_tile(p), rstd[:, u, 0:1], None, ALU.mult) \
                                .then_inc(xn_ok.handle, 1)

                        def v_blocks(p, u):
                            dve.wait_ge(v_pe.handle, v_pe.at(p + 1))
                            if pv_pe.due(p - 1):
                                dve.wait_ge(pv_pe.handle, pv_pe.at(p - 1))
                            for h in range(2):
                                rows = slice(S * h, S * h + S)
                                v4 = ps_b[rows, 0:2 * S].rearrange("p (r two d) -> p r two d", two=2, d=CHD)
                                to = vb[rows, u].rearrange("p b (r two) c -> p (b r) two c", two=2)
                                for j in range(2):
                                    at = 2 * CHD * j + CHD * h
                                    ins = nc.vector.tensor_copy(to[:, :, j, at:at + CHD], v4[:, :, j])
                            ins.then_inc(v_ok.handle, 1)

                        def residual(p):
                            dve.wait_ge(d_pe.handle, d_pe.at(p + 1))
                            nc.vector.tensor_tensor(x_tile(p), ps_d[:, 0:D], x_tile(p), ALU.add).then_inc(res_ok.handle, 1)

                        def step(p, u):
                            v = 1 - u
                            if has(p):
                                softmax_front(dve, mx, probs, p, u)
                                softmax_sum(dve, sm, probs, p, u)
                            if has(p + 3):
                                norm(p + 3, v)
                            if has(p + 1):
                                v_blocks(p + 1, v)
                            if has(p - 1):
                                residual(p - 1)
                        norm(0, 0)
                        norm(1, 1)
                        norm(2, 0)
                        v_blocks(0, 0)
                        steps(dve, step)
                loaded.base += 64
                cold.base += 1
                for c in ctx_in:
                    c.base += 8 * PAIRS
                close(PAIRS, stat_ok, eps_ok, rstd_ok, xn_ok, xt_pe, xt_ok, qk_pe, qkt_ok, kx_ok, v_pe, v_ok,
                      s_pe, max_ok, sub_ok, exp_ok, sum_ok, inv_ok, prob_ok, pt_pe, pt_ok, pv_pe, o_ok, d_pe, res_ok)

        def latent_attention(loaded, load_next):
            with ExitStack() as own:
                def ob(name, shape, dt=F32):
                    return sb(f"a2_{name}", shape, dt, own)

                w_q, w_kv, w_out, ln, gate = w_latent
                ctx_t = ob("ctx_t", [P, 2, DC])
                bn = ob("bn", [P, 2, 6])
                mv = ob("mv", [P, 2, 2])
                xn = ob("xn", [P, D])
                xt = ob("xt", [P, 2, 3, P])
                qt = ob("qt", [P, J, P])
                kx = ob("kx", [P, J, 2, 2, S])
                vb = ob("vb", [P, 2, 2, J, 2, HD2])
                mx = ob("mx", [P, 2, NH])
                sm = ob("sm", [P, 2, 2, NH])
                probs = ob("probs", [P, 2, NH * S])
                pt = ob("pt", [P, J, P])
                oth = ob("oth", [P, J, P], F32R)
                otl = ob("otl", [P, J, P], F32R)
                oh = ob("oh", [P, J * D], F32R)
                ol = ob("ol", [P, J * D], F32R)
                w_out_flat = w_out.rearrange("p c n -> p (c n)")
                SPLIT = 2 * D
                splits = [slice(SPLIT * k, SPLIT * k + SPLIT) for k in range(J * D // SPLIT)]

                with nc.Block() as block:
                    @block.sync
                    def _(sp):
                        def step(p, u):
                            if has(p + 2):
                                if xt_pe.due(p + 1):
                                    sp.wait_ge(xt_pe.handle, xt_pe.at(p + 1))
                                sp.dma_start(ctx_t[:, u], ctx_rows(p + 2)).then_inc(ctx_in[u].handle, 16)
                        for p in (-2, -1):
                            step(p, p % 2)
                        steps(sp, step)

                    @block.tensor
                    def _(pe):
                        pe.wait_ge(loaded.handle, loaded.at(0, 96))
                        pe.wait_ge(cold.handle, cold.at(0, 2))

                        def xt_(p, u):
                            pe.wait_ge(xn_ok.handle, xn_ok.at(p + 1))
                            pe.wait_ge(ctx_in[u].handle, arrival(p, u, 1))
                            if xt_ok.due(p):
                                pe.wait_ge(xt_ok.handle, xt_ok.at(p))
                            for c in range(CH):
                                nc.tensor.transpose(ps_t[:, c * P:c * P + P], xn[:, c * P:c * P + P], ident)
                            nc.tensor.transpose(ps_t[:, CH * P:CH * P + P], ctx_t[:, u], ident).then_inc(xt_pe.handle, 1)

                        def proj_q(p, u):
                            pe.wait_ge(xt_ok.handle, xt_ok.at(p + 1))
                            if v_ok.due(p):
                                pe.wait_ge(v_ok.handle, v_ok.at(p))
                            for r, bank in enumerate((ps_a, ps_b)):
                                for j in range(4):
                                    at = (4 * r + j) * P
                                    for c in range(CH):
                                        ins = nc.tensor.matmul(bank[:, j * P:j * P + P], w_q[:, c, at:at + P], xt[:, u, c],
                                                               start=(c == 0), stop=(c == CH - 1))
                                ins.then_inc(q2_pe.handle, 1)

                        def proj_k(p, u):
                            for r, bank in enumerate((ps_a, ps_b)):
                                pe.wait_ge(q2_ok.handle, q2_ok.at(p, r + 1))
                                for j in range(4):
                                    at = (4 * r + j) * P
                                    ins = nc.tensor.matmul(bank[:, j * P:j * P + P], w_kv[:, at:at + P], xt[:, u, CH],
                                                           start=True, stop=True)
                                ins.then_inc(k2_pe.handle, 1)

                        def proj_v(p, u):
                            w = w_kv[:, INNER:2 * INNER].rearrange("p (j h d) -> p j h d", h=2, d=HD2)
                            for b, bank in enumerate((ps_a, ps_b)):
                                pe.wait_ge(k2_ok.handle, k2_ok.at(p, b + 1))
                                for h in range(2):
                                    ins = nc.tensor.matmul(bank[S * h:S * h + S], xt[:, u, CH, b * S:b * S + S], w[:, :, h],
                                                           start=True, stop=True)
                                ins.then_inc(v2_pe.handle, 1)

                        def scores(p):
                            if sub_ok.due(p):
                                pe.wait_ge(sub_ok.handle, sub_ok.at(p))
                            pe.wait_ge(k2_ok.handle, k2_ok.at(p + 1))
                            for h in range(2):
                                bank = ps_s[:, 512 * h:512 * h + 512]
                                nc.tensor.matmul(bank, ident_b[:],
                                                 keymask[:, bass.ds(p, 1), :].broadcast_to([P, 8, S]),
                                                 start=True, stop=False, skip_group_check=True)
                                for b in range(2):
                                    for j in range(4):
                                        ins = nc.tensor.matmul(
                                            ps_s[b * S:b * S + S, 512 * h + P * j:512 * h + P * j + P],
                                            qt[:, 4 * h + j, b * S:b * S + S],
                                            kx[:, 4 * h + j, b].rearrange("p h k -> p (h k)"),
                                            start=False, stop=True, skip_group_check=True)
                                ins.then_inc(s_pe.handle, 1)

                        def pv(p, u):
                            pe.wait_ge(pt_ok.handle, pt_ok.at(p + 1))
                            pe.wait_ge(v_ok.handle, v_ok.at(p + 1))
                            if o_ok.due(p):
                                pe.wait_ge(o_ok.handle, o_ok.at(p))
                            for r, bank in enumerate((ps_o, ps_p)):
                                for b in range(2):
                                    for j in range(4):
                                        ins = nc.tensor.matmul(
                                            bank[:, j * P + b * S:j * P + b * S + S],
                                            vb[:, u, b, 4 * r + j].rearrange("p h d -> p (h d)"),
                                            pt[:, 4 * r + j, b * S:b * S + S], start=True, stop=True)
                                ins.then_inc(pv_pe.handle, 1)

                        def dense(p):
                            pe.wait_ge(o_ok.handle, o_ok.at(p + 1))
                            for c in range(J):
                                high, low = oh[:, c * D:c * D + D], ol[:, c * D:c * D + D]
                                nc.tensor.matmul(ps_d[:, 0:D], oth[:, c], high, start=(c == 0), stop=False)
                                nc.tensor.matmul(ps_d[:, 0:D], oth[:, c], low, start=False, stop=False)
                                ins = nc.tensor.matmul(ps_d[:, 0:D], otl[:, c], high, start=False, stop=(c == J - 1))
                            ins.then_inc(d_pe.handle, 1)

                        def step(p, u):
                            v = 1 - u
                            if has(p):
                                scores(p)
                            if has(p + 1):
                                proj_q(p + 1, v)
                            if has(p - 1):
                                prob_transposes(pe, probs, p - 1, v)
                            if has(p + 1):
                                proj_k(p + 1, v)
                            if has(p - 1):
                                pv(p - 1, v)
                            if has(p + 1):
                                proj_v(p + 1, v)
                            if has(p + 2):
                                xt_(p + 2, u)
                            if has(p - 1):
                                dense(p - 1)
                        xt_(0, 0)
                        proj_q(0, 0)
                        proj_k(0, 0)
                        proj_v(0, 0)
                        xt_(1, 1)
                        pe.wait_ge(wlow_ok.handle, wlow_ok.at(len(splits)))
                        steps(pe, step)

                    @block.scalar
                    def _(act):
                        load_next(act)
                        act.wait_ge(loaded.handle, loaded.at(0, 96))
                        nc.scalar.activation(gate[:, 1:2], gate[:, 0:1], ACT.Tanh).then_inc(sel_ok.handle, 1)

                        def xt_copy(p, u):
                            act.wait_ge(xt_pe.handle, xt_pe.at(p + 1))
                            if v2_pe.due(p - 1):
                                act.wait_ge(v2_pe.handle, v2_pe.at(p - 1))
                            for c in range(CH):
                                nc.scalar.activation(xt[:, u, c], ps_t[:, c * P:c * P + P], ACT.Identity,
                                                     scale=ln[:, 0, c:c + 1], bias=ln[:, 1, c:c + 1])
                            nc.scalar.activation(xt[:, u, CH], ps_t[:, CH * P:CH * P + P], ACT.Copy) \
                                .then_inc(xt_ok.handle, 1)

                        def q_copy(p):
                            for r, bank in enumerate((ps_a, ps_b)):
                                act.wait_ge(q2_pe.handle, q2_pe.at(p, r + 1))
                                if r == 0:
                                    if s_pe.due(p):
                                        act.wait_ge(s_pe.handle, s_pe.at(p))
                                nc.scalar.activation(qt[:, 4 * r:4 * r + 4].rearrange("p j n -> p (j n)"), bank[:],
                                                     ACT.Copy).then_inc(q2_ok.handle, 1)

                        def v_blocks(p, u, b):
                            bank = (ps_a, ps_b)[b]
                            act.wait_ge(v2_pe.handle, v2_pe.at(p, b + 1))
                            if pv_pe.due(p - 1):
                                act.wait_ge(pv_pe.handle, pv_pe.at(p - 1))
                            for h in range(2):
                                rows = slice(S * h, S * h + S)
                                ins = nc.scalar.activation(vb[rows, u, b, :, h],
                                                           bank[rows].rearrange("p (j d) -> p j d", d=HD2), ACT.Copy)
                            return ins

                        def step(p, u):
                            v = 1 - u
                            if has(p + 1):
                                q_copy(p + 1)
                            if has(p - 1):
                                prob_copies(act, pt, p - 1)
                            if has(p):
                                softmax_exp(act, probs, p, u, HD2 ** -0.5)
                            if has(p - 1):
                                for r, bank in enumerate((ps_o, ps_p)):
                                    act.wait_ge(pv_pe.handle, pv_pe.at(p - 1, r + 1))
                                    if r == 0:
                                        if d_pe.due(p - 1):
                                            act.wait_ge(d_pe.handle, d_pe.at(p - 1))
                                    nc.scalar.activation(oth[:, 4 * r:4 * r + 4].rearrange("p j n -> p (j n)"), bank[:],
                                                         ACT.Copy).then_inc(hhigh_ok.handle, 1)
                            if has(p + 1):
                                v_blocks(p + 1, v, 0).then_inc(v_half.handle, 1)
                            if has(p + 2):
                                xt_copy(p + 2, u)
                        xt_copy(0, 0)
                        q_copy(0)
                        v_blocks(0, 0, 0).then_inc(v_half.handle, 1)
                        xt_copy(1, 1)
                        for cols in splits:
                            nc.scalar.activation(oh[:, cols], w_out_flat[:, cols], ACT.Copy).then_inc(whigh_ok.handle, 1)
                        steps(act, step)

                    @block.gpsimd
                    def _(pool):
                        nc.gpsimd.memset(vb[:].rearrange("p a b j h d -> p (a b j h d)"), 0.0).then_inc(cold.handle, 1)

                        def step(p, u):
                            if has(p):
                                softmax_norm(pool, sm, probs, p, u)
                            if has(p + 4):
                                put_rstd_var(pool, p + 4, u)

                        def put_rstd_var(pool, p, u):
                            pool.wait_ge(stat_ok.handle, stat_ok.at(p + 1))
                            nc.gpsimd.tensor_tensor(stat[:, u, 1:2], mv[:, u, 1:2], eps5[:, 0:1], ALU.add) \
                                .then_inc(eps_ok.handle, 1)
                            pool.wait_ge(eps_ok.handle, eps_ok.at(p + 1))
                            if xn_ok.due(p - 1):
                                pool.wait_ge(xn_ok.handle, xn_ok.at(p - 1))
                            nc.gpsimd.tensor_tensor(rstd[:, u, 0:1], stat[:, u, 1:2], half_neg[:, 0:1], ALU.pow) \
                                .then_inc(rstd_ok.handle, 1)
                        for p in range(4):
                            put_rstd_var(pool, p, p % 2)
                        steps(pool, step)

                    @block.vector
                    def _(dve):
                        dve.wait_ge(keymask_in.handle, 32)
                        nc.vector.tensor_scalar(keymask[:], km_raw[:], 1.0, -MASKED, ALU.subtract, ALU.mult)
                        nc.vector.memset(kx[:].rearrange("p j b h k -> p (j b h k)"), 0.0).then_inc(cold.handle, 1)
                        dve.wait_ge(cold.handle, cold.at(0, 2))
                        dve.wait_ge(sel_ok.handle, sel_ok.at(1))

                        def stat_(p, u):
                            if xn_ok.due(p - 1):
                                dve.wait_ge(xn_ok.handle, xn_ok.at(p - 1))
                            nc.vector.bn_stats(bn[:, u], x_tile(p)).then_inc(aggr_ok.handle, 1)
                            dve.wait_ge(aggr_ok.handle, aggr_ok.at(p + 1))
                            nc.vector.tensor_copy(gate[:, 0:1], gate[:, 1:2])
                            nc.vector.bn_aggr(mv[:, u], bn[:, u]).then_inc(stat_ok.handle, 1)

                        def norm(p, u):
                            dve.wait_ge(rstd_ok.handle, rstd_ok.at(p + 1))
                            if xt_pe.due(p):
                                dve.wait_ge(xt_pe.handle, xt_pe.at(p))
                            nc.vector.tensor_scalar(xn[:], x_tile(p), mv[:, u, 0:1], rstd[:, u, 0:1],
                                                    ALU.subtract, ALU.mult).then_inc(xn_ok.handle, 1)

                        def k_blocks(p):
                            for r, bank in enumerate((ps_a, ps_b)):
                                dve.wait_ge(k2_pe.handle, k2_pe.at(p, r + 1))
                                if r == 0:
                                    if s_pe.due(p):
                                        dve.wait_ge(s_pe.handle, s_pe.at(p))
                                for h in range(2):
                                    rows = slice(S * h, S * h + S)
                                    ins = nc.vector.tensor_copy(
                                        kx[rows, 4 * r:4 * r + 4, :, h].rearrange("p j b k -> p (j b) k"),
                                        bank[rows].rearrange("p (jb k) -> p jb k", k=S))
                                ins.then_inc(k2_ok.handle, 1)

                        def v_blocks(p, u):
                            dve.wait_ge(v2_pe.handle, v2_pe.at(p + 1))
                            if pv_pe.due(p - 1):
                                dve.wait_ge(pv_pe.handle, pv_pe.at(p - 1))
                            dve.wait_ge(v_half.handle, v_half.at(p + 1))
                            for h in range(2):
                                rows = slice(S * h, S * h + S)
                                ins = nc.vector.tensor_copy(vb[rows, u, 1, :, h],
                                                            ps_b[rows].rearrange("p (j d) -> p j d", d=HD2))
                            ins.then_inc(v_ok.handle, 1)

                        def out_low(p):
                            for r, bank in enumerate((ps_o, ps_p)):
                                dve.wait_ge(hhigh_ok.handle, hhigh_ok.at(2 * p + (r + 1)))
                                high = oth[:, 4 * r:4 * r + 4].rearrange("p j n -> p (j n)").bitcast(F32)
                                nc.vector.tensor_tensor(otl[:, 4 * r:4 * r + 4].rearrange("p j n -> p (j n)"), bank[:],
                                                        high, ALU.subtract).then_inc(o_ok.handle, 1)

                        def residual(p):
                            dve.wait_ge(d_pe.handle, d_pe.at(p + 1))
                            nc.vector.scalar_tensor_tensor(x_tile(p), ps_d[:, 0:D], gate[:, 1:2], x_tile(p),
                                                           ALU.mult, ALU.add).then_inc(res_ok.handle, 1)

                        def step(p, u):
                            v = 1 - u
                            if has(p):
                                softmax_front(dve, mx, probs, p, u)
                                softmax_sum(dve, sm, probs, p, u)
                            if has(p + 1):
                                k_blocks(p + 1)
                            if has(p - 1):
                                out_low(p - 1)
                            if has(p + 4):
                                stat_(p + 4, u)
                            if has(p + 1):
                                v_blocks(p + 1, v)
                            if has(p + 3):
                                norm(p + 3, v)
                            if has(p - 1):
                                residual(p - 1)
                        for p in range(4):
                            stat_(p, p % 2)
                            if p == 1:
                                norm(0, 0)
                            if p == 2:
                                norm(1, 1)
                        k_blocks(0)
                        v_blocks(0, 0)
                        norm(2, 0)
                        for k, cols in enumerate(splits):
                            dve.wait_ge(whigh_ok.handle, whigh_ok.at(k + 1))
                            nc.vector.tensor_tensor(ol[:, cols], w_out_flat[:, cols], oh[:, cols].bitcast(F32),
                                                    ALU.subtract).then_inc(wlow_ok.handle, 1)
                        steps(dve, step)
                loaded.base += 96
                cold.base += 2
                sel_ok.base += 1
                close(len(splits), whigh_ok, wlow_ok)
                close(2 * PAIRS, hhigh_ok)
                for c in ctx_in:
                    c.base += 8 * PAIRS
                close(PAIRS, aggr_ok, stat_ok, eps_ok, rstd_ok, xn_ok, xt_pe, xt_ok, q2_pe, q2_ok, k2_pe, k2_ok, v2_pe,
                      v_half, v_ok, s_pe, max_ok, sub_ok, exp_ok, sum_ok, inv_ok, prob_ok, pt_pe, pt_ok, pv_pe, o_ok,
                      d_pe, res_ok)

        def group_steps(eng, step):
            step(0)
            with eng.Fori(1, GROUPS - 1) as g:
                step(g)
            step(GROUPS - 1)

        def has_group(g):
            return not isinstance(g, int) or g < GROUPS

        def x_rows(g, k):
            return x_res[:, bass.ds(g * (G * D) + k * D, D)]

        def vm_rows(g):
            return vm[:, bass.ds(g * G, G), :]

        def gated_feed_forward(n, loaded, load_next, store=False):
            with ExitStack() as own:
                def ob(name, shape, dt=F32):
                    return sb(f"f{n}_{name}", shape, dt, own)

                w_in, w_down, w_ln = w_gated
                mixw = ob("mixw", [P, G, 2])
                sel = ob("sel", [P, G, 2])
                xh = ob("xh", [P, 2 * CH, GT], F32R)
                xl = ob("xl", [P, 2 * CH, GT], F32R)
                wh = ob("wh", [P, 2 * CH * 2 * I + IC * P - I], F32R)
                wl = ob("wl", [P, 2 * CH * 2 * I + IC * P - I], F32R)
                dh = ob("dh", [P, IC, 2 * D], F32R)
                dl = ob("dl", [P, IC, 2 * D], F32R)
                hh = ob("hh", [P, IC, GT], F32R)
                hl = ob("hl", [P, IC, GT], F32R)
                xn = view(self_w, 0, G, 2, D)
                act_g = view(self_w, G * 2 * D, 2, GT)
                part = view(self_w, G * 2 * D + 2 * GT, 2, D)
                junk = view(self_w, G * 2 * D + 2 * GT + 2 * D, D)
                xt_banks = (ps_t, ps_p, ps_o, ps_t)
                xt_order = (2, 0, 1, 3)
                rows_of = [min(P, I - P * m) for m in range(IC)]
                in_banks = [(ps_a[:], ps_b[:]), (ps_s[:, 0:512], ps_s[:, 512:1024])]

                with nc.Block() as block:
                    @block.sync
                    def _(sp):
                        def step(g):
                            sp.wait_ge(res_ok.handle, res_ok.at(g * G + G))
                            sp.dma_start(out_rows(g), x_res[:, bass.ds(g * (G * D), G * D)]
                                         .rearrange("p (n d) -> p n d", d=D)).then_inc(stored.handle, 16)
                        if store:
                            group_steps(sp, step)
                            sp.wait_ge(stored.handle, stored.at(GROUPS))

                    @block.tensor
                    def _(pe):
                        pe.wait_ge(loaded.handle, loaded.at(0, 144))

                        def gate_up(g):
                            pe.wait_ge(xlow_ok.handle, xlow_ok.at(g * 4 + 4))
                            for m in range(IC):
                                if m == IC - 1 and has_group(g + 1):
                                    xt_(g + 1)
                                if h_ok.due(g * IC + (m - 1)):
                                    pe.wait_ge(h_ok.handle, h_ok.at(g * IC + (m - 1)))
                                for r in range(2):
                                    bank = in_banks[m % 2][r]
                                    for k in range(2 * CH):
                                        at = (2 * k + r) * I + m * P
                                        high, low = wh[:, at:at + P], wl[:, at:at + P]
                                        nc.tensor.matmul(bank, high, xh[:, k], start=(k == 0), stop=False)
                                        nc.tensor.matmul(bank, high, xl[:, k], start=False, stop=False)
                                        ins = nc.tensor.matmul(bank, low, xh[:, k], start=False,
                                                               stop=(k == 2 * CH - 1))
                                ins.then_inc(g_pe.handle, 1)

                        def xt_chunk(k):
                            e, c = divmod(k, CH)
                            for i in range(G):
                                ins = nc.tensor.transpose(xt_banks[k][:, i * P:i * P + P], xn[:, i, e, c * P:c * P + P],
                                                          ident)
                            ins.then_inc(xt_pe.handle, 1)

                        def xt_(g):
                            pe.wait_ge(xn_ok.handle, xn_ok.at(g * G + G))
                            if xlow_ok.due(g * 4):
                                pe.wait_ge(xlow_ok.handle, xlow_ok.at(g * 4))
                            xt_chunk(0)
                            xt_chunk(1)
                            if res_ok.due(g * G - G):
                                pe.wait_ge(res_ok.handle, res_ok.at(g * G - G))
                            xt_chunk(2)

                        def xt_last(g):
                            pe.wait_ge(xlow_ok.handle, xlow_ok.at(g * 4 + 2))
                            xt_chunk(3)

                        def down(g):
                            if isinstance(g, int) and g == 0:
                                pe.wait_ge(wlow_ok.handle, wlow_ok.at(4 * CH + IC))
                            for i in range(G):
                                if res_ok.due(g * G + (i - 1)):
                                    pe.wait_ge(res_ok.handle, res_ok.at(g * G + (i - 1)))
                                if i == 1 and has_group(g + 1):
                                    xt_last(g + 1)
                                bank = (ps_d, ps_o)[i % 2][:]
                                for m in range(IC):
                                    if i == 0:
                                        pe.wait_ge(h_ok.handle, h_ok.at(g * IC + (m + 1)))
                                    n = rows_of[m]
                                    high, low = hh[0:n, m, i * P:i * P + P], hl[0:n, m, i * P:i * P + P]
                                    nc.tensor.matmul(bank, high, dh[0:n, m], start=(m == 0), stop=False)
                                    nc.tensor.matmul(bank, high, dl[0:n, m], start=False, stop=False)
                                    ins = nc.tensor.matmul(bank, low, dh[0:n, m], start=False, stop=(m == IC - 1))
                                ins.then_inc(d_pe.handle, 1)

                        def step(g):
                            gate_up(g)
                            down(g)
                        xt_(0)
                        xt_last(0)
                        pe.wait_ge(wlow_ok.handle, wlow_ok.at(4 * CH))
                        pe.wait_ge(wpad_ok.handle, wpad_ok.at(1))
                        group_steps(pe, step)

                    @block.scalar
                    def _(act):
                        act.wait_ge(loaded.handle, loaded.at(0, 144))

                        def stats(g):
                            if eps_ok.due(g):
                                act.wait_ge(eps_ok.handle, eps_ok.at(g))
                            for k in range(G):
                                if stat_ok.due(g * G + k):
                                    act.wait_ge(stat_ok.handle, stat_ok.at(g * G + k))
                                nc.scalar.activation(junk, x_rows(g, k), ACT.Square, scale=D ** -0.5,
                                                     accum_out=stat[:, 0, k:k + 1]).then_inc(stat_ok.handle, 1)

                        def xt_copy(g):
                            if g_pe.due(g * IC):
                                act.wait_ge(g_pe.handle, g_pe.at(g * IC))
                            for k in xt_order:
                                act.wait_ge(xt_pe.handle, xt_pe.at(g * 4 + (k + 1)))
                                nc.scalar.activation(xh[:, k], xt_banks[k][:], ACT.Copy,
                                                     scale=w_ln[:, k % CH:k % CH + 1]).then_inc(xt_ok.handle, 1)

                        def step(g):
                            for m in range(IC):
                                act.wait_ge(g_pe.handle, g_pe.at(g * IC + (m + 1)))
                                if h_ok.due(g * IC + (m - 1)):
                                    act.wait_ge(h_ok.handle, h_ok.at(g * IC + (m - 1)))
                                nc.scalar.activation(act_g[0:rows_of[m], m % 2], in_banks[m % 2][0][0:rows_of[m]],
                                                     ACT.Silu).then_inc(a_ok.handle, 1)
                                act.wait_ge(prod_ok.handle, prod_ok.at(g * IC + (m + 1)))
                                if d_pe.due(g * G):
                                    act.wait_ge(d_pe.handle, d_pe.at(g * G))
                                nc.scalar.activation(hh[0:rows_of[m], m], act_g[0:rows_of[m], m % 2],
                                                     ACT.Copy).then_inc(hhigh_ok.handle, 1)
                                if m == 1 and has_group(g + 1):
                                    stats(g + 1)
                            if has_group(g + 1):
                                xt_copy(g + 1)
                        stats(0)
                        for k in range(2 * CH):
                            for r in range(2):
                                at = (2 * k + r) * I
                                nc.scalar.activation(wh[:, at:at + I], w_in[:, k, r], ACT.Copy).then_inc(whigh_ok.handle, 1)
                        xt_copy(0)
                        for m in range(IC):
                            n = rows_of[m]
                            nc.scalar.activation(dh[0:n, m], w_down[0:n, m].rearrange("p e n -> p (e n)"), ACT.Copy) \
                                .then_inc(whigh_ok.handle, 1)
                        act.wait_ge(wlow_ok.handle, wlow_ok.at(4 * CH + IC))
                        load_next(act)
                        group_steps(act, step)

                    @block.gpsimd
                    def _(pool):
                        nc.gpsimd.memset(wh[:, 4 * CH * I:].bitcast(F32), 0.0)
                        nc.gpsimd.memset(wl[:, 4 * CH * I:].bitcast(F32), 0.0).then_inc(wpad_ok.handle, 1)

                        def rstd_(g):
                            pool.wait_ge(stat_ok.handle, stat_ok.at(g * G + G))
                            nc.gpsimd.tensor_tensor(stat[:, 1], stat[:, 0], eps6[:], ALU.add).then_inc(eps_ok.handle, 1)
                            pool.wait_ge(eps_ok.handle, eps_ok.at(g + 1))
                            if mixw_ok.due(g):
                                pool.wait_ge(mixw_ok.handle, mixw_ok.at(g))
                            nc.gpsimd.tensor_tensor(rstd[:, 0], stat[:, 1], half_neg[:], ALU.pow).then_inc(rstd_ok.handle, 1)

                        def step(g):
                            if has_group(g + 1):
                                rstd_(g + 1)
                        rstd_(0)
                        group_steps(pool, step)

                    @block.vector
                    def _(dve):
                        def norm(g):
                            dve.wait_ge(rstd_ok.handle, rstd_ok.at(g + 1))
                            nc.vector.tensor_tensor(mixw[:], vm_rows(g), rstd[:, 0].unsqueeze(2).broadcast_to([P, G, 2]),
                                                    ALU.mult).then_inc(mixw_ok.handle, 1)
                            dve.wait_ge(mixw_ok.handle, mixw_ok.at(g + 1))
                            if xt_pe.due(g * 4):
                                dve.wait_ge(xt_pe.handle, xt_pe.at(g * 4))
                            for k in range(G):
                                for e in range(2):
                                    ins = nc.vector.tensor_scalar(xn[:, k, e], x_rows(g, k), mixw[:, k, e:e + 1], None,
                                                                  ALU.mult)
                                ins.then_inc(xn_ok.handle, 1)

                        def low_parts(g):
                            for n, k in enumerate(xt_order):
                                dve.wait_ge(xt_ok.handle, xt_ok.at(g * 4 + (n + 1)))
                                nc.vector.scalar_tensor_tensor(xl[:, k], xt_banks[k][:], w_ln[:, k % CH:k % CH + 1],
                                                               xh[:, k].bitcast(F32), ALU.mult, ALU.subtract) \
                                    .then_inc(xlow_ok.handle, 1)

                        def step(g):
                            for m in range(IC):
                                dve.wait_ge(a_ok.handle, a_ok.at(g * IC + (m + 1)))
                                now = act_g[0:rows_of[m], m % 2]
                                nc.vector.tensor_tensor(now, in_banks[m % 2][1][0:rows_of[m]], now, ALU.mult) \
                                    .then_inc(prod_ok.handle, 1)
                                dve.wait_ge(hhigh_ok.handle, hhigh_ok.at(g * IC + (m + 1)))
                                nc.vector.tensor_tensor(hl[0:rows_of[m], m], now, hh[0:rows_of[m], m].bitcast(F32),
                                                        ALU.subtract).then_inc(h_ok.handle, 1)
                                if m == 2 and has_group(g + 1):
                                    norm(g + 1)
                            if has_group(g + 1):
                                low_parts(g + 1)
                            if res_ok.due(g * G):
                                dve.wait_ge(res_ok.handle, res_ok.at(g * G))
                            nc.vector.tensor_copy(sel[:], vm_rows(g)).then_inc(sel_ok.handle, 1)
                            dve.wait_ge(sel_ok.handle, sel_ok.at(g + 1))
                            for k in range(G):
                                bank = (ps_d, ps_o)[k % 2]
                                dve.wait_ge(d_pe.handle, d_pe.at(g * G + (k + 1)))
                                nc.vector.scalar_tensor_tensor(part[:, k % 2], bank[:, 0:D], sel[:, k, 0:1], x_rows(g, k),
                                                               ALU.mult, ALU.add).then_inc(mix_ok.handle, 1)
                                dve.wait_ge(mix_ok.handle, mix_ok.at(g * G + (k + 1)))
                                nc.vector.scalar_tensor_tensor(x_rows(g, k), bank[:, D:2 * D], sel[:, k, 1:2],
                                                               part[:, k % 2], ALU.mult, ALU.add).then_inc(res_ok.handle, 1)
                        norm(0)
                        for k in range(2 * CH):
                            for r in range(2):
                                at = (2 * k + r) * I
                                dve.wait_ge(whigh_ok.handle, whigh_ok.at(2 * k + r + 1))
                                nc.vector.tensor_tensor(wl[:, at:at + I], w_in[:, k, r], wh[:, at:at + I].bitcast(F32),
                                                        ALU.subtract).then_inc(wlow_ok.handle, 1)
                        low_parts(0)
                        for m in range(IC):
                            n = rows_of[m]
                            dve.wait_ge(whigh_ok.handle, whigh_ok.at(4 * CH + m + 1))
                            nc.vector.tensor_tensor(dl[0:n, m], w_down[0:n, m].rearrange("p e n -> p (e n)"),
                                                    dh[0:n, m].bitcast(F32), ALU.subtract).then_inc(wlow_ok.handle, 1)
                        group_steps(dve, step)
                loaded.base += 144
                close(GROUPS, eps_ok, rstd_ok, mixw_ok, sel_ok)
                close(GROUPS * G, stat_ok, xn_ok, d_pe, mix_ok, res_ok)
                close(GROUPS * 2 * CH, xt_pe, xt_ok, xlow_ok)
                close(4 * CH + IC, whigh_ok, wlow_ok)
                close(1, wpad_ok)
                close(GROUPS * IC, g_pe, a_ok, prod_ok, hhigh_ok, h_ok)
                if store:
                    close(GROUPS, stored)

        def gelu_feed_forward(loaded, load_next):
            M = FF // P
            with ExitStack() as own:
                def ob(name, shape, dt=F32):
                    return sb(f"f2_{name}", shape, dt, own)

                w_in, w_out, ln, gate = w_gelu
                bn = ob("bn", [P, G, 6])
                mv = ob("mv", [P, G, 2])
                xn = ob("xn", [P, G, D])
                affine = ob("affine", [P, GT])
                xh = ob("xh", [P, CH, GT], F32R)
                xl = ob("xl", [P, CH, GT], F32R)
                wh = ob("wh", [P, CH * FF], F32R)
                wl = ob("wl", [P, CH * FF], F32R)
                oh = ob("oh", [P, M * D], F32R)
                ol = ob("ol", [P, M * D], F32R)
                h = ob("h", [P, 2, GT])
                hh = ob("hh", [P, M, GT], F32R)
                hl = ob("hl", [P, M, GT], F32R)
                HALF = FF // 2
                w_in_flat, w_out_flat = (w.rearrange("p c n -> p (c n)") for w in (w_in, w_out))
                splits = [(wh, wl, w_in_flat, HALF * k) for k in range(2 * CH)] + \
                         [(oh, ol, w_out_flat, HALF * k) for k in range(M * D // HALF)]
                in_banks = [ps_a[:], ps_b[:], ps_s[:, 0:512], ps_s[:, 512:1024]]

                with nc.Block() as block:
                    @block.tensor
                    def _(pe):
                        pe.wait_ge(loaded.handle, loaded.at(0, 80))

                        def up(g):
                            pe.wait_ge(xlow_ok.handle, xlow_ok.at(g * CH + CH))
                            for m in range(M):
                                if m == M - 1 and has_group(g + 1):
                                    xt_(g + 1)
                                if a_ok.due(g * M + (m - 3)):
                                    pe.wait_ge(a_ok.handle, a_ok.at(g * M + (m - 3)))
                                for c in range(CH):
                                    at = c * FF + m * P
                                    high, low = wh[:, at:at + P], wl[:, at:at + P]
                                    nc.tensor.matmul(in_banks[m % 4], high, xh[:, c], start=(c == 0), stop=False)
                                    nc.tensor.matmul(in_banks[m % 4], high, xl[:, c], start=False, stop=False)
                                    ins = nc.tensor.matmul(in_banks[m % 4], low, xh[:, c], start=False,
                                                           stop=(c == CH - 1))
                                ins.then_inc(g_pe.handle, 1)

                        def xt_(g):
                            pe.wait_ge(xn_ok.handle, xn_ok.at(g * G + G))
                            if xlow_ok.due(g * CH):
                                pe.wait_ge(xlow_ok.handle, xlow_ok.at(g * CH))
                            for c in range(CH):
                                bank = (ps_t, ps_p)[c]
                                for i in range(G):
                                    ins = nc.tensor.transpose(bank[:, i * P:i * P + P], xn[:, i, c * P:c * P + P], ident)
                                ins.then_inc(xt_pe.handle, 1)

                        def down(g):
                            if isinstance(g, int) and g == 0:
                                pe.wait_ge(wlow_ok.handle, wlow_ok.at(len(splits)))
                            for i in range(G):
                                if res_ok.due(g * G + (i - 1)):
                                    pe.wait_ge(res_ok.handle, res_ok.at(g * G + (i - 1)))
                                bank = (ps_o, ps_d)[i % 2][:, 0:D]
                                for m in range(M):
                                    if i == 0:
                                        pe.wait_ge(h_ok.handle, h_ok.at(g * M + (m + 1)))
                                    high, low = hh[:, m, i * P:i * P + P], hl[:, m, i * P:i * P + P]
                                    nc.tensor.matmul(bank, high, oh[:, m * D:m * D + D], start=(m == 0), stop=False)
                                    nc.tensor.matmul(bank, high, ol[:, m * D:m * D + D], start=False, stop=False)
                                    ins = nc.tensor.matmul(bank, low, oh[:, m * D:m * D + D], start=False,
                                                           stop=(m == M - 1))
                                ins.then_inc(d_pe.handle, 1)

                        def step(g):
                            up(g)
                            down(g)
                        xt_(0)
                        pe.wait_ge(wlow_ok.handle, wlow_ok.at(2 * CH))
                        group_steps(pe, step)

                    @block.scalar
                    def _(act):
                        load_next(act)
                        act.wait_ge(loaded.handle, loaded.at(0, 80))
                        nc.scalar.activation(gate[:, 1:2], gate[:, 0:1], ACT.Tanh).then_inc(sel_ok.handle, 1)

                        def xt_copy(g):
                            if g_pe.due(g * M):
                                act.wait_ge(g_pe.handle, g_pe.at(g * M))
                            for c in range(CH):
                                act.wait_ge(xt_pe.handle, xt_pe.at(g * CH + (c + 1)))
                                nc.scalar.activation(xh[:, c], (ps_t, ps_p)[c % 2][:], ACT.Identity,
                                                     scale=ln[:, 0, c:c + 1], bias=ln[:, 1, c:c + 1]) \
                                    .then_inc(xt_ok.handle, 1)

                        def step(g):
                            for m in range(M):
                                act.wait_ge(g_pe.handle, g_pe.at(g * M + (m + 1)))
                                if h_ok.due(g * M + (m - 1)):
                                    act.wait_ge(h_ok.handle, h_ok.at(g * M + (m - 1)))
                                nc.scalar.activation(h[:, m % 2], in_banks[m % 4], ACT.Gelu).then_inc(a_ok.handle, 1)
                                act.wait_ge(a_ok.handle, a_ok.at(g * M + (m + 1)))
                                if d_pe.due(g * G):
                                    act.wait_ge(d_pe.handle, d_pe.at(g * G))
                                nc.scalar.activation(hh[:, m], h[:, m % 2], ACT.Copy).then_inc(hhigh_ok.handle, 1)
                            if has_group(g + 1):
                                xt_copy(g + 1)
                        for high, _, w, at in splits[:2 * CH]:
                            nc.scalar.activation(high[:, at:at + HALF], w[:, at:at + HALF], ACT.Copy) \
                                .then_inc(whigh_ok.handle, 1)
                        xt_copy(0)
                        for high, _, w, at in splits[2 * CH:]:
                            nc.scalar.activation(high[:, at:at + HALF], w[:, at:at + HALF], ACT.Copy) \
                                .then_inc(whigh_ok.handle, 1)
                        group_steps(act, step)

                    @block.gpsimd
                    def _(pool):
                        def rstd_(g):
                            pool.wait_ge(stat_ok.handle, stat_ok.at(g * G + G))
                            nc.gpsimd.tensor_tensor(stat[:, 1], mv[:, :, 1], eps5[:], ALU.add).then_inc(eps_ok.handle, 1)
                            pool.wait_ge(eps_ok.handle, eps_ok.at(g + 1))
                            if xn_ok.due(g * G):
                                pool.wait_ge(xn_ok.handle, xn_ok.at(g * G))
                            nc.gpsimd.tensor_tensor(rstd[:, 0], stat[:, 1], half_neg[:], ALU.pow).then_inc(rstd_ok.handle, 1)

                        def step(g):
                            if has_group(g + 1):
                                rstd_(g + 1)
                        rstd_(0)
                        group_steps(pool, step)

                    @block.vector
                    def _(dve):
                        dve.wait_ge(sel_ok.handle, sel_ok.at(1))

                        def stats(g):
                            if xn_ok.due(g * G):
                                dve.wait_ge(xn_ok.handle, xn_ok.at(g * G))
                            for k in range(G):
                                nc.vector.bn_stats(bn[:, k], x_rows(g, k)).then_inc(aggr_ok.handle, 1)
                            dve.wait_ge(aggr_ok.handle, aggr_ok.at(g * G + G))
                            nc.vector.tensor_copy(gate[:, 0:1], gate[:, 1:2])
                            for k in range(G):
                                nc.vector.bn_aggr(mv[:, k], bn[:, k]).then_inc(stat_ok.handle, 1)

                        def norm(g):
                            dve.wait_ge(rstd_ok.handle, rstd_ok.at(g + 1))
                            if xt_pe.due(g * CH):
                                dve.wait_ge(xt_pe.handle, xt_pe.at(g * CH))
                            for k in range(G):
                                nc.vector.tensor_scalar(xn[:, k], x_rows(g, k), mv[:, k, 0:1], rstd[:, 0, k:k + 1],
                                                        ALU.subtract, ALU.mult).then_inc(xn_ok.handle, 1)

                        def low_part(g, c):
                            dve.wait_ge(xt_ok.handle, xt_ok.at(g * CH + (c + 1)))
                            if xlow_ok.due(g * CH + c):
                                dve.wait_ge(xlow_ok.handle, xlow_ok.at(g * CH + c))
                            nc.vector.tensor_scalar(affine[:], (ps_t, ps_p)[c][:], ln[:, 0, c:c + 1], ln[:, 1, c:c + 1],
                                                    ALU.mult, ALU.add).then_inc(affine_ok.handle, 1)
                            dve.wait_ge(affine_ok.handle, affine_ok.at(g * CH + (c + 1)))
                            nc.vector.tensor_tensor(xl[:, c], affine[:], xh[:, c].bitcast(F32), ALU.subtract) \
                                .then_inc(xlow_ok.handle, 1)

                        def step(g):
                            for m in range(M):
                                dve.wait_ge(hhigh_ok.handle, hhigh_ok.at(g * M + (m + 1)))
                                nc.vector.tensor_tensor(hl[:, m], h[:, m % 2], hh[:, m].bitcast(F32), ALU.subtract) \
                                    .then_inc(h_ok.handle, 1)
                                if m == 0 and has_group(g + 1):
                                    stats(g + 1)
                                if m == 3 and has_group(g + 1):
                                    norm(g + 1)
                            for k in range(G):
                                if k < CH and has_group(g + 1):
                                    low_part(g + 1, k)
                                dve.wait_ge(d_pe.handle, d_pe.at(g * G + (k + 1)))
                                nc.vector.scalar_tensor_tensor(x_rows(g, k), (ps_o, ps_d)[k % 2][:, 0:D], gate[:, 1:2],
                                                               x_rows(g, k), ALU.mult, ALU.add).then_inc(res_ok.handle, 1)
                        stats(0)
                        norm(0)
                        for k, (high, low, w, at) in enumerate(splits):
                            if k == 2 * CH:
                                low_part(0, 0)
                                low_part(0, 1)
                            dve.wait_ge(whigh_ok.handle, whigh_ok.at(k + 1))
                            nc.vector.tensor_tensor(low[:, at:at + HALF], w[:, at:at + HALF],
                                                    high[:, at:at + HALF].bitcast(F32), ALU.subtract) \
                                .then_inc(wlow_ok.handle, 1)
                        group_steps(dve, step)
                loaded.base += 80
                close(GROUPS, eps_ok, rstd_ok)
                close(1, sel_ok)
                close(GROUPS * G, stat_ok, aggr_ok, xn_ok, d_pe, res_ok)
                close(len(splits), whigh_ok, wlow_ok)
                close(GROUPS * CH, xt_pe, xt_ok, affine_ok, xlow_ok)
                close(GROUPS * M, g_pe, a_ok, hhigh_ok, h_ok)

        def out_rows(g):
            return t["out"].rearrange("(n two) s d -> (two s) n d", two=2)[:, bass.ds(g * G, G), :]

        phases = [(layer0, None),
                  (lambda *w: self_attention(1, *w), lambda eng, sem: load_self(eng, sem, 1)),
                  (lambda *w: cross_attention(1, *w), lambda eng, sem: load_cross(eng, sem, 1)),
                  (lambda *w: gated_feed_forward(1, *w), lambda eng, sem: load_gated(eng, sem, 1)),
                  (latent_attention, load_latent),
                  (gelu_feed_forward, load_gelu),
                  (lambda *w: self_attention(3, *w), lambda eng, sem: load_self(eng, sem, 3)),
                  (lambda *w: cross_attention(3, *w), lambda eng, sem: load_cross(eng, sem, 3)),
                  (lambda *w: gated_feed_forward(3, *w, store=True), lambda eng, sem: load_gated(eng, sem, 3))]
        for k, (phase, _) in enumerate(phases):
            def load_next(eng):
                if k + 1 < len(phases):
                    phases[k + 1][1](eng, weights_in[(k + 1) % 2].handle)
            phase(weights_in[k % 2], load_next)


_WEIGHTS = {
    0: ["b_gate", "norm_w"],
    1: ["ln_in_w", "ln_post_attn_w", "ln_post_cross_w", "v_qkv", "l_qkv", "v_dense", "l_dense", "cq_w", "ckv_w",
        "cdense_w", "v_gate", "v_up", "v_down", "l_gate", "l_up", "l_down"],
    2: ["ln_q_g", "ln_q_b", "Wq", "Wkv", "Wo", "attn_gate", "ln_ff_g", "ln_ff_b", "W1", "W2", "ff_gate"],
}
_WEIGHTS[3] = _WEIGHTS[1]


def kernel(**inputs):
    import concourse.bacc as bacc
    from concourse.bass_utils import run_bass_kernel_spmd

    host = {n: np.asarray(inputs[n]) for n in ("x", "ctx_1024", "pos_1xS", "mask_BxS_ik0")}
    host["mask_BxS2_bk0"] = np.asarray(inputs["mask_BxS2_bk0"])
    host["W_mem_T"] = np.asarray(inputs["L0_xattn_W_mem"]).T
    host["W_gate_T"] = np.asarray(inputs["L0_xattn_W_gate"]).T
    for n, names in _WEIGHTS.items():
        for w in names:
            a = np.asarray(inputs[f"L{n}_xattn_{w}"])
            host[f"L{n}_xattn_{w}"] = a.reshape(CH, P).T if w.startswith("ln_") else a
    host["consts"] = constants()

    nc = bacc.Bacc("TRN2", target_bir_lowering=False, num_devices=1)
    arrays, t = {}, {}
    for name, a in host.items():
        arrays[f"in_{name}"] = np.ascontiguousarray(a)
        t[name] = nc.dram_tensor(f"in_{name}", a.shape, mybir.dt.from_np(a.dtype), kind="ExternalInput").ap()
    t["out"] = nc.dram_tensor("out", (B, S, D), F32, kind="ExternalOutput").ap()
    build(nc, t)
    r = run_bass_kernel_spmd(nc, [arrays], core_ids=[0])
    return r.results[0]["out"]
```
